# Optimizing a Trainium2 kernel written in Bass

```python
import numpy as np
import jax
import jax.numpy as jnp

def _softmax(x, axis=-1):
    return jax.nn.softmax(x, axis=axis)

def _gelu(x):
    return jax.nn.gelu(x, approximate=True)

def _silu(x):
    return jax.nn.silu(x)

def _sigmoid(x):
    return jax.nn.sigmoid(x)

def _layernorm(x, axis=-1, eps=1e-05):
    m = jnp.mean(x, axis=axis, keepdims=True)
    v = jnp.var(x, axis=axis, keepdims=True)
    return (x - m) / jnp.sqrt(v + eps)

def _scatter_add(tgt, idx, src, axis=0):
    return tgt.at[idx].add(src)

def _segment_sum(src, seg, n):
    return jax.ops.segment_sum(src, seg, n)
kernel_name = 'mk_gnn_ffn_d2_gnn_r16_0528b3'

def setup_inputs(seed: int=0):
    np.random.seed(seed)
    _w = jnp.asarray

    def _rec_inputs():
        import jax
        import jax.numpy as jnp
        _gk = jax.random.key(seed)
        x = -8.776e-05 + 1 * jax.random.normal(jax.random.fold_in(_gk, 1), (3125, 256), jnp.float32)
        src = jax.random.randint(jax.random.fold_in(_gk, 2), (50000,), 0, 3125, jnp.int32)
        dst = jax.random.randint(jax.random.fold_in(_gk, 3), (50000,), 0, 3125, jnp.int32)
        _o = jnp.argsort(dst, stable=True)
        src = src[_o]
        dst = dst[_o]
        edge_type_16 = jax.random.randint(jax.random.fold_in(_gk, 13), (50000,), 0, 16, jnp.int32)
        edge_weight1 = jax.random.uniform(jax.random.fold_in(_gk, 14), (50000, 1), jnp.float32, 0.0, 0.999998)
        return (x, src, dst, edge_type_16, edge_weight1)
    x, src, dst, edge_type_16, edge_weight1 = _rec_inputs()

    def _L0_gnn_setup():
        import jax, jax.numpy as jnp
        import numpy as np
        N_NODES = 1250
        N_EDGES = 20000
        NUM_RELS = 16
        IN_FEAT = 256
        OUT_FEAT = 256
        key = jax.random.key(seed)
        k_h, k_w, k_n, k_s, k_d, k_r = jax.random.split(key, 6)
        h = jax.random.normal(k_h, (N_NODES, IN_FEAT), dtype=jnp.float32)
        weight = jax.random.normal(k_w, (NUM_RELS, IN_FEAT, OUT_FEAT), dtype=jnp.float32)
        norm = jax.random.uniform(k_n, (N_EDGES, 1), dtype=jnp.float32)
        src = jax.random.randint(k_s, (N_EDGES,), 0, N_NODES, dtype=jnp.int32)
        dst = jax.random.randint(k_d, (N_EDGES,), 0, N_NODES, dtype=jnp.int32)
        rel_type = jax.random.randint(k_r, (N_EDGES,), 0, NUM_RELS, dtype=jnp.int32)
        return {'h': h, 'weight': weight, 'norm': norm, 'src': src, 'dst': dst, 'rel_type': rel_type}
    _L0_gnn_all = _L0_gnn_setup()
    _L0_gnn_in = {k: v for k, v in _L0_gnn_all.items() if k in ('weight',)}
    del _L0_gnn_all

    def _L0_ffn_setup():
        import jax, jax.numpy as jnp
        import numpy as np
        D_MODEL = 256
        N_EXPERTS = 16
        HIDDEN = 512
        SCALE = 0.02
        key = jax.random.key(seed)
        ks = jax.random.split(key, 5)
        x = jax.random.normal(ks[0], (4, 512, D_MODEL), dtype=jnp.float32)
        gate_w = jax.random.normal(ks[1], (D_MODEL, N_EXPERTS), dtype=jnp.float32) * SCALE
        gate_b = jnp.zeros((N_EXPERTS,), dtype=jnp.float32)
        w1 = jax.random.normal(ks[2], (N_EXPERTS, D_MODEL, HIDDEN), dtype=jnp.float32) * SCALE
        w2 = jax.random.normal(ks[3], (N_EXPERTS, D_MODEL, HIDDEN), dtype=jnp.float32) * SCALE
        w3 = jax.random.normal(ks[4], (N_EXPERTS, HIDDEN, D_MODEL), dtype=jnp.float32) * SCALE
        return {'x': x, 'gate_w': gate_w, 'gate_b': gate_b, 'w1': w1, 'w2': w2, 'w3': w3}
    _L0_ffn_all = _L0_ffn_setup()
    _L0_ffn_in = {k: v for k, v in _L0_ffn_all.items() if k in ('gate_w', 'gate_b', 'w1', 'w2', 'w3')}
    del _L0_ffn_all

    def _L1_gnn_setup():
        import jax, jax.numpy as jnp
        import numpy as np
        N_NODES = 625
        N_EDGES = 20000
        HIDDEN = 256
        HEADS = 8
        HEAD_DIM = HIDDEN // HEADS
        NEG_SLOPE = 0.2

        def gat_conv(x, src, dst, W, a_src, a_dst, b):
            N = x.shape[0]
            h = (x @ W).reshape(N, HEADS, HEAD_DIM)
            alpha_s = jnp.einsum('nhc,hc->nh', h, a_src)
            alpha_d = jnp.einsum('nhc,hc->nh', h, a_dst)
            e = alpha_s[src] + alpha_d[dst]
            e = jnp.where(e > 0, e, NEG_SLOPE * e)
            m = jax.ops.segment_max(e, dst, num_segments=N)
            ex = jnp.exp(e - m[dst])
            denom = jax.ops.segment_sum(ex, dst, num_segments=N)
            alpha = ex / (denom[dst] + 1e-16)
            msg = h[src] * alpha[:, :, None]
            out = jax.ops.segment_sum(msg, dst, num_segments=N)
            return out.reshape(N, HEADS * HEAD_DIM) + b
        key = jax.random.key(seed)
        ks = jax.random.split(key, 12)
        x = jax.random.normal(ks[0], (N_NODES, HIDDEN), dtype=jnp.float32)
        edges_idx = jax.random.randint(ks[1], (2, N_EDGES), 0, N_NODES, dtype=jnp.int64)
        s = 1.0 / np.sqrt(HIDDEN)
        W1 = jax.random.normal(ks[2], (HIDDEN, HEADS * HEAD_DIM), dtype=jnp.float32) * s
        a_src1 = jax.random.normal(ks[3], (HEADS, HEAD_DIM), dtype=jnp.float32) * s
        a_dst1 = jax.random.normal(ks[4], (HEADS, HEAD_DIM), dtype=jnp.float32) * s
        b1 = jnp.zeros((HEADS * HEAD_DIM,), dtype=jnp.float32)
        W2 = jax.random.normal(ks[5], (HIDDEN, HEADS * HEAD_DIM), dtype=jnp.float32) * s
        a_src2 = jax.random.normal(ks[6], (HEADS, HEAD_DIM), dtype=jnp.float32) * s
        a_dst2 = jax.random.normal(ks[7], (HEADS, HEAD_DIM), dtype=jnp.float32) * s
        b2 = jnp.zeros((HEADS * HEAD_DIM,), dtype=jnp.float32)
        return {'x': x, 'edges_idx': edges_idx, 'W1': W1, 'a_src1': a_src1, 'a_dst1': a_dst1, 'b1': b1, 'W2': W2, 'a_src2': a_src2, 'a_dst2': a_dst2, 'b2': b2}
    _L1_gnn_all = _L1_gnn_setup()
    _L1_gnn_in = {k: v for k, v in _L1_gnn_all.items() if k in ('W1', 'a_src1', 'a_dst1', 'b1', 'W2', 'a_src2', 'a_dst2', 'b2')}
    del _L1_gnn_all

    def _L1_ffn_setup():
        import jax, jax.numpy as jnp
        import numpy as np
        B, A = (256, 8)
        IN, OUT = (256, 256)
        SH1, SH2 = (256, 128)
        EH1, EH2 = (128, 64)
        E, TOPK = (4, 2)

        def _shared_mlp(x, W1, b1, W2, b2, W3, b3):
            h = jax.nn.relu(x @ W1 + b1)
            h = jax.nn.relu(h @ W2 + b2)
            return h @ W3 + b3

        def _experts_mlp(x, eW1, eb1, eW2, eb2, eW3, eb3):
            h = jax.nn.relu(jnp.einsum('baf,efh->ebah', x, eW1) + eb1[:, None, None, :])
            h = jax.nn.relu(jnp.einsum('ebah,ehg->ebag', h, eW2) + eb2[:, None, None, :])
            o = jnp.einsum('ebag,ego->ebao', h, eW3) + eb3[:, None, None, :]
            return jnp.moveaxis(o, 0, -1)
        key = jax.random.key(seed)
        ks = jax.random.split(key, 16)
        s = 0.05
        return {'x': jax.random.normal(ks[0], (B, A, IN), jnp.float32), 'sW1': jax.random.normal(ks[1], (IN, SH1), jnp.float32) * s, 'sb1': jnp.zeros((SH1,), jnp.float32), 'sW2': jax.random.normal(ks[2], (SH1, SH2), jnp.float32) * s, 'sb2': jnp.zeros((SH2,), jnp.float32), 'sW3': jax.random.normal(ks[3], (SH2, OUT), jnp.float32) * s, 'sb3': jnp.zeros((OUT,), jnp.float32), 'eW1': jax.random.normal(ks[4], (E, IN, EH1), jnp.float32) * s, 'eb1': jnp.zeros((E, EH1), jnp.float32), 'eW2': jax.random.normal(ks[5], (E, EH1, EH2), jnp.float32) * s, 'eb2': jnp.zeros((E, EH2), jnp.float32), 'eW3': jax.random.normal(ks[6], (E, EH2, OUT), jnp.float32) * s, 'eb3': jnp.zeros((E, OUT), jnp.float32), 'gW': jax.random.normal(ks[7], (IN, E), jnp.float32) * s, 'gb': jnp.zeros((E,), jnp.float32)}
    _L1_ffn_all = _L1_ffn_setup()
    _L1_ffn_in = {k: v for k, v in _L1_ffn_all.items() if k in ('sW1', 'sb1', 'sW2', 'sb2', 'sW3', 'sb3', 'eW1', 'eb1', 'eW2', 'eb2', 'eW3', 'eb3', 'gW', 'gb')}
    del _L1_ffn_all
    return {'x': x, 'src': src, 'dst': dst, 'edge_type_16': edge_type_16, 'edge_weight1': edge_weight1, 'L0_gnn_weight': _L0_gnn_in['weight'], 'L0_ffn_gate_w': _L0_ffn_in['gate_w'], 'L0_ffn_gate_b': _L0_ffn_in['gate_b'], 'L0_ffn_w1': _L0_ffn_in['w1'], 'L0_ffn_w2': _L0_ffn_in['w2'], 'L0_ffn_w3': _L0_ffn_in['w3'], 'L1_gnn_W1': _L1_gnn_in['W1'], 'L1_gnn_a_src1': _L1_gnn_in['a_src1'], 'L1_gnn_a_dst1': _L1_gnn_in['a_dst1'], 'L1_gnn_b1': _L1_gnn_in['b1'], 'L1_gnn_W2': _L1_gnn_in['W2'], 'L1_gnn_a_src2': _L1_gnn_in['a_src2'], 'L1_gnn_a_dst2': _L1_gnn_in['a_dst2'], 'L1_gnn_b2': _L1_gnn_in['b2'], 'L1_ffn_sW1': _L1_ffn_in['sW1'], 'L1_ffn_sb1': _L1_ffn_in['sb1'], 'L1_ffn_sW2': _L1_ffn_in['sW2'], 'L1_ffn_sb2': _L1_ffn_in['sb2'], 'L1_ffn_sW3': _L1_ffn_in['sW3'], 'L1_ffn_sb3': _L1_ffn_in['sb3'], 'L1_ffn_eW1': _L1_ffn_in['eW1'], 'L1_ffn_eb1': _L1_ffn_in['eb1'], 'L1_ffn_eW2': _L1_ffn_in['eW2'], 'L1_ffn_eb2': _L1_ffn_in['eb2'], 'L1_ffn_eW3': _L1_ffn_in['eW3'], 'L1_ffn_eb3': _L1_ffn_in['eb3'], 'L1_ffn_gW': _L1_ffn_in['gW'], 'L1_ffn_gb': _L1_ffn_in['gb']}

def reference(x, src, dst, edge_type_16, edge_weight1, L0_gnn_weight, L0_ffn_gate_w, L0_ffn_gate_b, L0_ffn_w1, L0_ffn_w2, L0_ffn_w3, L1_gnn_W1, L1_gnn_a_src1, L1_gnn_a_dst1, L1_gnn_b1, L1_gnn_W2, L1_gnn_a_src2, L1_gnn_a_dst2, L1_gnn_b2, L1_ffn_sW1, L1_ffn_sb1, L1_ffn_sW2, L1_ffn_sb2, L1_ffn_sW3, L1_ffn_sb3, L1_ffn_eW1, L1_ffn_eb1, L1_ffn_eW2, L1_ffn_eb2, L1_ffn_eW3, L1_ffn_eb3, L1_ffn_gW, L1_ffn_gb):
    import jax
    import jax.numpy as jnp

    def _L0_gnn_ref(h, weight, norm, src, dst, rel_type):
        import jax, jax.numpy as jnp
        import numpy as np
        N_NODES = 1250
        N_EDGES = 20000
        NUM_RELS = 16
        IN_FEAT = 256
        OUT_FEAT = 256
        transformed = jnp.einsum('ni,rio->rno', h, weight)
        msg = transformed[rel_type, src] * norm
        out = jax.ops.segment_sum(msg, dst, num_segments=h.shape[0])
        return out

    def _L0_ffn_ref(x, gate_w, gate_b, w1, w2, w3):
        import jax, jax.numpy as jnp
        import numpy as np
        D_MODEL = 256
        N_EXPERTS = 16
        HIDDEN = 512
        SCALE = 0.02
        n_experts = w1.shape[0]
        logits = jnp.einsum('bsd,de->bse', x, gate_w) + gate_b
        probs = jax.nn.softmax(logits, axis=-1)
        top_probs, top_idx = jax.lax.top_k(probs, 2)
        top_probs = top_probs / jnp.sum(top_probs, axis=-1, keepdims=True)
        dispatch = jnp.sum(jax.nn.one_hot(top_idx, n_experts, dtype=x.dtype) * top_probs[..., None], axis=-2)
        h1 = jnp.einsum('bsd,edh->bseh', x, w1)
        h2 = jnp.einsum('bsd,edh->bseh', x, w2)
        hidden = jax.nn.silu(h1) * h2
        expert_out = jnp.einsum('bseh,eho->bseo', hidden, w3)
        return jnp.einsum('bseo,bse->bso', expert_out, dispatch)

    def _L1_gnn_ref(x, edges_idx, W1, a_src1, a_dst1, b1, W2, a_src2, a_dst2, b2):
        import jax, jax.numpy as jnp
        import numpy as np
        N_NODES = 625
        N_EDGES = 20000
        HIDDEN = 256
        HEADS = 8
        HEAD_DIM = HIDDEN // HEADS
        NEG_SLOPE = 0.2

        def gat_conv(x, src, dst, W, a_src, a_dst, b):
            N = x.shape[0]
            h = (x @ W).reshape(N, HEADS, HEAD_DIM)
            alpha_s = jnp.einsum('nhc,hc->nh', h, a_src)
            alpha_d = jnp.einsum('nhc,hc->nh', h, a_dst)
            e = alpha_s[src] + alpha_d[dst]
            e = jnp.where(e > 0, e, NEG_SLOPE * e)
            m = jax.ops.segment_max(e, dst, num_segments=N)
            ex = jnp.exp(e - m[dst])
            denom = jax.ops.segment_sum(ex, dst, num_segments=N)
            alpha = ex / (denom[dst] + 1e-16)
            msg = h[src] * alpha[:, :, None]
            out = jax.ops.segment_sum(msg, dst, num_segments=N)
            return out.reshape(N, HEADS * HEAD_DIM) + b
        src = edges_idx[0]
        dst = edges_idx[1]
        h = gat_conv(x, src, dst, W1, a_src1, a_dst1, b1)
        h = jax.nn.elu(h)
        out = gat_conv(h, src, dst, W2, a_src2, a_dst2, b2)
        return out

    def _L1_ffn_ref(x, sW1, sb1, sW2, sb2, sW3, sb3, eW1, eb1, eW2, eb2, eW3, eb3, gW, gb):
        import jax, jax.numpy as jnp
        import numpy as np
        B, A = (256, 8)
        IN, OUT = (256, 256)
        SH1, SH2 = (256, 128)
        EH1, EH2 = (128, 64)
        E, TOPK = (4, 2)

        def _shared_mlp(x, W1, b1, W2, b2, W3, b3):
            h = jax.nn.relu(x @ W1 + b1)
            h = jax.nn.relu(h @ W2 + b2)
            return h @ W3 + b3

        def _experts_mlp(x, eW1, eb1, eW2, eb2, eW3, eb3):
            h = jax.nn.relu(jnp.einsum('baf,efh->ebah', x, eW1) + eb1[:, None, None, :])
            h = jax.nn.relu(jnp.einsum('ebah,ehg->ebag', h, eW2) + eb2[:, None, None, :])
            o = jnp.einsum('ebag,ego->ebao', h, eW3) + eb3[:, None, None, :]
            return jnp.moveaxis(o, 0, -1)
        all_out = _experts_mlp(x, eW1, eb1, eW2, eb2, eW3, eb3)
        shared = _shared_mlp(x, sW1, sb1, sW2, sb2, sW3, sb3)
        gates = jax.nn.softmax(x @ gW + gb, axis=-1)
        topv, topi = jax.lax.top_k(gates, TOPK)
        topw = jax.nn.softmax(topv, axis=-1)
        sel = jnp.take_along_axis(all_out, topi[:, :, None, :], axis=-1)
        gated = jnp.sum(sel * topw[:, :, None, :], axis=-1)
        return shared + gated
    edge_index = jnp.stack([src, dst])
    x = x + _L0_gnn_ref(_layernorm(x, axis=-1), L0_gnn_weight, edge_weight1, src, dst, edge_type_16)
    x = x + _L0_ffn_ref(_layernorm(x, axis=-1)[None], L0_ffn_gate_w, L0_ffn_gate_b, L0_ffn_w1, L0_ffn_w2, L0_ffn_w3)[0]
    x = x + _L1_gnn_ref(_layernorm(x, axis=-1), edge_index, L1_gnn_W1, L1_gnn_a_src1, L1_gnn_a_dst1, L1_gnn_b1, L1_gnn_W2, L1_gnn_a_src2, L1_gnn_a_dst2, L1_gnn_b2)
    x = x + _L1_ffn_ref(_layernorm(x, axis=-1)[None], L1_ffn_sW1, L1_ffn_sb1, L1_ffn_sW2, L1_ffn_sb2, L1_ffn_sW3, L1_ffn_sb3, L1_ffn_eW1, L1_ffn_eb1, L1_ffn_eW2, L1_ffn_eb2, L1_ffn_eW3, L1_ffn_eb3, L1_ffn_gW, L1_ffn_gb)[0]
    return x

_drawn_inputs = setup_inputs


def setup_inputs(seed=0):
    import zlib

    import numpy as np

    out = dict(_drawn_inputs(seed))
    spreads = {'L0_ffn_gate_b': (0.0, 0.8),
     'L1_gnn_b1': (0.0, 0.8),
     'L1_gnn_b2': (0.0, 2.0),
     'L1_ffn_sb1': (0.0, 0.8),
     'L1_ffn_sb2': (0.0, 2.0),
     'L1_ffn_sb3': (0.0, 2.0),
     'L1_ffn_eb1': (0.0, 0.8),
     'L1_ffn_eb2': (0.0, 2.0),
     'L1_ffn_eb3': (0.0, 2.0),
     'L1_ffn_gb': (0.0, 0.8)}
    factors = {'L0_ffn_gate_w': 8.0,
     'L0_ffn_w1': 8.0,
     'L0_ffn_w2': 8.0,
     'L0_ffn_w3': 8.0,
     'L1_gnn_W1': 8.0,
     'L1_gnn_a_src1': 8.0,
     'L1_gnn_a_dst1': 8.0,
     'L1_gnn_W2': 8.0,
     'L1_gnn_a_src2': 8.0,
     'L1_gnn_a_dst2': 8.0,
     'L1_ffn_sW1': 8.0,
     'L1_ffn_sW2': 8.0,
     'L1_ffn_sW3': 8.0,
     'L1_ffn_eW1': 8.0,
     'L1_ffn_eW2': 8.0,
     'L1_ffn_eW3': 8.0,
     'L1_ffn_gW': 8.0}
    for name, (base, spread) in spreads.items():
        noise = np.random.default_rng([zlib.crc32(name.encode()), seed]).standard_normal(out[name].shape)
        drawn = base * np.exp(spread * noise) if base else spread * noise
        out[name] = jnp.asarray(drawn.astype(out[name].dtype))
    for name, factor in factors.items():
        out[name] = (out[name] * factor).astype(out[name].dtype)
    return out
```

```python
from contextlib import ExitStack

import concourse.bass as bass
from concourse import mybir

F32 = mybir.dt.float32
BF16 = mybir.dt.bfloat16
I32 = mybir.dt.int32
U32 = mybir.dt.uint32
ALU = mybir.AluOpType
ACT = mybir.ActivationFunctionType
AX = mybir.AxisListType.X

P = 128
N = 3125
NT = 25
NP = NT * P
E = 50000
ET = 391
S = 416
NS = NT + 1
D = 256
R = 16
BIG = 1.0e30
CH = 32
NCH = S // CH
HW = 33
MSG = 8 * HW
ROW = MSG + 8
HID = 512


class Engine:

    def __init__(self, sem):
        self.sem = sem
        self.n = 0
        self.ops = []

    def put(self, fn, *args, after=(), sig=True, **kw):
        if sig:
            self.n += 1
        self.ops.append((fn, args, kw, tuple(after), (self.sem, 1) if sig else None))
        return (self.sem, self.n)

    def dma(self, fn, stream, *args, after=(), **kw):
        stream.n += 16
        self.ops.append((fn, args, kw, tuple(after), (stream.sem, 16)))
        return (stream.sem, stream.n)

    def last(self):
        return (self.sem, self.n)

    def play(self, eng):
        seen = {}
        for fn, args, kw, after, inc in self.ops:
            for sem, v in after:
                if v > seen.get(id(sem), 0):
                    eng.wait_ge(sem, v)
                    seen[id(sem)] = v
            ins = fn(*args, **kw)
            if inc is not None:
                ins.then_inc(*inc)


class Stream:

    def __init__(self, sem):
        self.sem = sem
        self.n = 0

    def done(self):
        return (self.sem, self.n)


def build(nc, a, out):
    with ExitStack() as ctx:
        def sb(name, shape, dt=F32):
            return ctx.enter_context(nc.sbuf_tensor(name, shape, dt))

        def stream(name):
            return Stream(ctx.enter_context(nc.semaphore(name)))

        PE, DVE, AC, PL, SP = (Engine(ctx.enter_context(nc.semaphore("s_" + n)))
                               for n in ("pe", "dve", "act", "pool", "sp"))
        vec, act, ten, pool, sync = nc.vector, nc.scalar, nc.tensor, nc.gpsimd, nc.sync
        B = [ctx.enter_context(nc.psum_tensor(f"bank{i}", [P, 512], F32)) for i in range(8)]

        TR = nc.dram_tensor("tr", [NP * R, D], F32, kind="Internal").ap()
        HT = [nc.dram_tensor(f"ht{i}", [NP, ROW], F32, kind="Internal").ap() for i in range(2)]
        SE = {k: nc.dram_tensor("se_" + k, [ET, P], F32 if k == "nrm" else I32, kind="Internal").ap()
              for k in ("src", "dst", "rel", "nrm")}
        RD = nc.dram_tensor("rd", [S, P], F32, kind="Internal").ap()
        DLD = nc.dram_tensor("dld", [S, P], BF16, kind="Internal").ap()

        X = sb("X", [P, NS, D])
        XT = sb("XT", [P, 2, NP])
        ident = sb("ident", [P, P])
        iorow = sb("iorow", [P, P])
        iocol = sb("iocol", [P, 1])
        epsc = sb("epsc", [P, 1])
        ioi = sb("ioi", [P, P], I32)
        idx1T = sb("idx1T", [P, 512], I32)
        srcT = sb("srcT", [P, 512], I32)
        nrmT = sb("nrmT", [P, 512])
        dlT = sb("dlT", [P, 512])
        laT = sb("laT", [P, 512])
        doff = {m: sb(f"doff{m}", [1, S], I32) for m in (8, 48, D, MSG)}
        bns = sb("bns", [P, 4, 6])
        mv = sb("mv", [P, NT, 2])
        rstd = sb("rstd", [P, NT])
        xn = sb("xn", [P, 4, D])
        ARENA = 33500
        arena = sb("arena", [P, ARENA])
        top = [0]

        def take(n, shape=None, dt=F32):
            v = arena[:, top[0]:top[0] + n]
            top[0] += n
            assert top[0] <= ARENA, top[0]
            return v if dt == F32 else v.bitcast(dt)

        s_x = stream("d_x")
        s_x2 = stream("d_x2")
        s_out = stream("d_out")

        def everyone():
            return [q.last() for q in (PE, DVE, AC, PL, SP)]

        c0 = PL.put(pool.memset, ident[:, :], 0.0)
        c1 = PL.put(pool.affine_select, out=ident[:, :], in_=ident[:, :], compare_op=ALU.not_equal, fill=1.0,
                    base=0, pattern=[[-1, P]], channel_multiplier=1, after=[c0])
        c2 = PL.put(pool.iota, ioi[:, :], [[1, P]], base=0, channel_multiplier=0)
        k1 = DVE.put(vec.tensor_copy, iorow[:, :], ioi[:, :], after=[c2])
        c3 = PL.put(pool.iota, ioi[:, 0:1], [[0, 1]], base=0, channel_multiplier=1, after=[k1])
        k2 = DVE.put(vec.tensor_copy, iocol[:, :], ioi[:, 0:1], after=[c3])
        c4 = PL.put(pool.iota, ioi[:, 0:4], [[P, 4]], base=0, channel_multiplier=1, after=[k2])
        k3 = DVE.put(vec.memset, epsc[:, :], 1e-5)
        xz = DVE.put(vec.memset, X[:, NT - 1:NS, :], 0.0)
        const = [c1, k1, k2, k3]

        x_main = SP.dma(sync.dma_start, s_x, X[:, 0:NT - 1, :],
                        a["x"][0:(NT - 1) * P, :].rearrange("(t p) d -> p t d", p=P))
        x_tail = SP.dma(sync.dma_start, s_x2, X[0:N - (NT - 1) * P, NT - 1, :], a["x"][(NT - 1) * P:N, :], after=[xz])

        free = [None] * 8

        def fr(b):
            return [free[b]] if free[b] else []

        def transpose_into_xt(i, src, ready, reuse):
            b = 6 + i % 2
            PE.put(ten.transpose, B[b][:, 0:P], src[:, 0:P], ident[:, :], after=[ready] + fr(b) + const, sig=False)
            t = PE.put(ten.transpose, B[b][:, P:2 * P], src[:, P:2 * P], ident[:, :])
            free[b] = AC.put(act.copy, XT[:, :, i * P:(i + 1) * P], B[b][:, 0:2 * P].rearrange("p (k c) -> p k c", k=2),
                             after=[t] + reuse)
            return t, free[b]

        xn_free = [None] * 4

        def layernorm(after):
            reuse = [PE.last()]
            ag = None
            bs = [None] * 4
            for i in range(NT):
                st = DVE.put(vec.bn_stats, bns[:, i % 4, :], X[:, i, :], after=after + [t for t in [bs[i % 4]] if t])
                ag = bs[i % 4] = DVE.put(vec.bn_aggr, mv[:, i, :], bns[:, i % 4, :], after=[st])
            sq = AC.put(act.activation, rstd[:, :], mv[:, :, 1], ACT.Sqrt, bias=epsc[:, 0:1], after=[ag] + const)
            rc = DVE.put(vec.reciprocal, rstd[:, :], rstd[:, :], after=[sq])
            done = None
            for i in range(NT):
                w = [t for t in [xn_free[i % 4]] if t]
                n = DVE.put(vec.tensor_scalar, xn[:, i % 4, :], X[:, i, :], mv[:, i, 0:1], rstd[:, i:i + 1],
                            ALU.subtract, ALU.mult, after=[rc] + w)
                xn_free[i % 4], done = transpose_into_xt(i, xn[:, i % 4, :], n, reuse)
            return done

        xt = layernorm([x_main, x_tail])

        base0 = top[0]
        wrel = take(2 * R * D).rearrange("p (k r d) -> p k r d", k=2, r=R)
        stage = take(2 * R * D).rearrange("p (b n) -> p b n", b=2)
        s_w = stream("d_w")
        s_tr = [stream(f"d_tr{i}") for i in range(2)]
        for k in range(2):
            w_in = SP.dma(sync.dma_start, s_w, wrel[:, k, :, :],
                          a["L0_gnn_weight"][:, k * P:(k + 1) * P, :].rearrange("r p d -> p r d"))
        st_free = [None] * 2
        tr_rows = TR.rearrange("(n r) d -> n (r d)", r=R)
        for i in range(NT):
            cps = []
            for j in range(8):
                b = j % 6
                for k in range(2):
                    mm = PE.put(ten.matmul, B[b][:, :], XT[:, k, i * P:(i + 1) * P],
                                wrel[:, k, 2 * j:2 * j + 2, :].rearrange("p r d -> p (r d)"),
                                start=(k == 0), stop=(k == 1), after=[xt, w_in] + fr(b), sig=(k == 1))
                w = [t for t in [st_free[i % 2]] if t]
                free[b] = AC.put(act.copy, stage[:, i % 2, j * 512:(j + 1) * 512], B[b][:, :], after=[mm] + w)
            st_free[i % 2] = SP.dma(sync.dma_start, s_tr[i % 2], tr_rows[i * P:(i + 1) * P, :], stage[:, i % 2, :],
                                    after=[free[b]])
        tr_done = list(st_free)

        names = ("src", "dst", "rel", "nrm")
        inputs = {"src": a["src"], "dst": a["dst"], "rel": a["edge_type_16"],
                  "nrm": a["edge_weight1"].rearrange("e o -> (e o)")}
        full = (ET - 1) * P
        rest = E - full
        padi = take(P, dt=I32)
        padf = take(P)
        s_cp = stream("d_cp")
        pz = [DVE.put(vec.memset, padi[0:1, 0:64], 0), DVE.put(vec.memset, padi[0:1, 64:P], 1000000),
              DVE.put(vec.memset, padf[0:1, :], 0.0)]
        for k in names:
            PL.dma(pool.dma_start, s_cp, SE[k][0:ET - 1, :], inputs[k][0:full].rearrange("(t c) -> t c", c=P))
            PL.dma(pool.dma_start, s_cp, SE[k][ET - 1:ET, 0:rest], inputs[k][full:E].rearrange("(t c) -> t c", t=1))
            pad = {"src": padi[0:1, 0:P - rest], "rel": padi[0:1, 0:P - rest],
                   "dst": padi[0:1, 64:64 + P - rest], "nrm": padf[0:1, 0:P - rest]}[k]
            PL.dma(pool.dma_start, s_cp, SE[k][ET - 1:ET, rest:P], pad, after=pz)
        edges = s_cp.done()

        fi = take(4, dt=I32)
        ff = take(4)
        sio = take(4)
        thr = take(4)
        cnt = take(4)
        tf = take(4)
        ti = take(4, dt=I32)
        df = take(4)
        d128 = take(4)
        drow = take(512)
        diag = take(512).rearrange("p (g c) -> p g c", g=4)
        ones = take(P)
        junk = take(512)
        s_f = stream("d_f")
        z = DVE.put(vec.memset, fi, 1000000)
        PL.dma(pool.dma_start, s_f, fi[:, 0:3], SE["dst"][0:3 * P, 0:1].rearrange("(g p) o -> p (g o)", p=P),
               after=[edges, z], allow_slow_non_contiguous=True)
        f_in = PL.dma(pool.dma_start, s_f, fi[0:ET - 3 * P, 3:4], SE["dst"][3 * P:ET, 0:1], allow_slow_non_contiguous=True)
        o1 = DVE.put(vec.memset, ones, 1.0)
        v = DVE.put(vec.tensor_copy, sio, ioi[:, 0:4], after=[c4])
        t1 = DVE.put(vec.tensor_scalar, thr, sio, float(P), float(P), ALU.mult, ALU.add, after=[v])
        f1 = DVE.put(vec.tensor_copy, ff, fi, after=[f_in])
        f2 = DVE.put(vec.scalar_tensor_tensor, ff, sio, float(P), ff, ALU.mult, ALU.add, after=[f1])
        mm = None
        for g in range(4):
            q = DVE.put(vec.tensor_scalar, diag[:, g, :], ident[:, :], ff[:, g:g + 1], None, ALU.mult, after=[f2] + const)
            mm = PE.put(ten.matmul, B[0][:, g * P:(g + 1) * P], ones, diag[:, g, :], start=True, stop=True,
                        after=[q, o1] + fr(0))
        ct = None
        for g in range(4):
            w = [ct] if ct else []
            ct = DVE.put(vec.tensor_scalar, junk[:, 0:ET], B[0][:, 0:ET], thr[:, g:g + 1], None, ALU.is_lt, ALU.add,
                         accum_out=cnt[:, g:g + 1], after=[mm, t1] + w)
        free[0] = ct
        u = DVE.put(vec.tensor_scalar, tf, cnt, -1.0, 0.0, ALU.add, ALU.max, after=[ct])
        ti_ok = DVE.put(vec.tensor_copy, ti, tf, after=[u])
        u = DVE.put(vec.tensor_tensor, df, sio, tf, ALU.subtract, after=[u])
        d_ok = DVE.put(vec.tensor_scalar, d128, df, float(P), None, ALU.mult, after=[u])
        for g in range(4):
            mm = PE.put(ten.matmul, B[1][0:1, g * P:(g + 1) * P], df[:, g:g + 1], ident[:, :], start=True, stop=True,
                        after=[d_ok] + fr(1))
        u = DVE.put(vec.tensor_copy, drow[0:1, :], B[1][0:1, :], after=[mm])
        free[1] = u
        offs = None
        for m in doff:
            offs = DVE.put(vec.tensor_scalar, doff[m][:, :], drow[0:1, 0:S], float(m), None, ALU.mult, after=[u])

        rows = {k: take(512, dt=(F32 if k == "nrm" else I32)).rearrange("p (g c) -> p g c", g=4) for k in names}
        s_rw = stream("d_rw")
        zr = None
        for k in names:
            zr = DVE.put(vec.memset, rows[k][:, 3, :], 0.0 if k == "nrm" else 0)
        for k in names:
            for g in range(4):
                m = P if g < 3 else S - 3 * P
                PL.dma(pool.indirect_dma_start, s_rw, rows[k][0:m, g, :], None, SE[k],
                       bass.IndirectOffsetOnAxis(ap=ti[0:m, g:g + 1], axis=0), after=[ti_ok, edges, zr])
        got = s_rw.done()
        i1 = take(512).rearrange("p (g c) -> p g c", g=4)
        sf = take(512).rearrange("p (g c) -> p g c", g=4)
        dl = take(512).rearrange("p (g c) -> p g c", g=4)
        dlb = take(256, dt=BF16).rearrange("p (g c) -> p g c", g=4)
        ne = take(4 * (P + 1)).rearrange("p (g c) -> p g c", g=4)
        rr = take(512).rearrange("p (g c) -> p g c", g=4)
        q1 = DVE.put(vec.scalar_tensor_tensor, i1, rows["src"], float(R), rows["rel"], ALU.mult, ALU.add, after=[got])
        q2 = DVE.put(vec.tensor_copy, sf, rows["src"])
        for g in range(4):
            q3 = DVE.put(vec.tensor_scalar, dl[:, g, :], rows["dst"][:, g, :], d128[:, g:g + 1], None, ALU.subtract,
                         after=[d_ok])
        q4 = DVE.put(vec.tensor_copy, dlb, dl, after=[q3])
        DVE.put(vec.memset, ne[:, :, 0:1], 1.0)
        DVE.put(vec.memset, ne[:, :, P:P + 1], 1.0)
        q5 = DVE.put(vec.tensor_tensor, ne[:, :, 1:P], dl[:, :, 1:P], dl[:, :, 0:P - 1], ALU.not_equal)
        q6 = DVE.put(vec.tensor_scalar, rr, ne[:, :, 0:P], -BIG, None, ALU.mult, after=[q5])
        tabs = [(i1, idx1T, q1), (sf, srcT, q2), (rows["nrm"], nrmT, got), (dl, dlT, q3), (ne[:, :, 1:P + 1], laT, q5)]
        tab = {}
        for n, (src, dst, ok) in enumerate(tabs):
            b = 2 + n % 4
            for g in range(4):
                mm = PE.put(ten.transpose, B[b][:, g * P:(g + 1) * P], src[:, g, :], ident[:, :],
                            after=[ok] + fr(b) + const)
            tab[n] = free[b] = DVE.put(vec.tensor_copy, dst[:, :], B[b][:, :], after=[mm])
        s_dl = stream("d_dl")
        for src, dst, ok in ((rr, RD, q6), (dlb, DLD, q4)):
            SP.dma(sync.dma_start, s_dl, dst[0:3 * P, :].rearrange("(g p) c -> p g c", p=P), src[:, 0:3, :], after=[ok])
            SP.dma(sync.dma_start, s_dl, dst[3 * P:S, :], src[0:S - 3 * P, 3, :])
        steps_ok = s_dl.done()

        def reg_bank(eng, name):
            return [[eng.alloc_register(f"{name}{k}_{i}") for i in range(16)] for k in range(2)]

        class Offsets:

            def __init__(self, queue, eng, mult, most):
                self.q, self.eng, self.mult, self.most = queue, eng, mult, most

            def load(self, s0, after=()):
                bank = regs[self.q][(s0 // 16) % 2]
                self.q.put(self.eng.load, bank, doff[self.mult][0:1, s0:s0 + 16], sig=False, after=after)

            def at(self, s):
                r = regs[self.q][(s // 16) % 2][s % 16]
                return self.eng.snap(r, min_val=0, max_val=self.most)

        regs = {DVE: reg_bank(vec, "rv"), PE: reg_bank(ten, "rp")}

        NG = 8
        Gr = take(NG * D).rearrange("p (n d) -> p n d", n=NG)
        OHr = take(NG * P).rearrange("p (n d) -> p n d", n=NG)
        s_g = [stream(f"d_g{i}") for i in range(NG)]
        xf = X[:, :, :].rearrange("p t d -> p (t d)")
        xo = Offsets(DVE, vec, D, (NS - 1) * D)
        mmt = [None] * NG
        gts = {}
        addt = [None] * 8
        last_add = [DVE.last()]
        ready = [tab[0], tab[2], tab[3]] + tr_done

        def add_x(s, bank):
            def go():
                o = xf[:, bass.ds(xo.at(s), D)]
                return vec.tensor_tensor(o, o, bank[:, 0:D], ALU.add)
            return go

        LAG = 3
        for s in range(S + LAG):
            if s < S:
                n = s % NG
                w = [mmt[n]] if mmt[n] else []
                g = PL.dma(pool.indirect_dma_start, s_g[n], Gr[:, n, :], None, TR,
                           bass.IndirectOffsetOnAxis(ap=idx1T[:, s:s + 1], axis=0), after=ready + w)
                oh = DVE.put(vec.tensor_scalar, OHr[:, n, :], iorow[:, :], dlT[:, s:s + 1], nrmT[:, s:s + 1],
                             ALU.is_equal, ALU.mult, after=w + [tab[2], tab[3]])
                mmt[n] = PE.put(ten.matmul, B[n][:, 0:D], OHr[:, n, :], Gr[:, n, :], start=True, stop=True,
                                after=[g, oh] + fr(n))
                gts[s] = mmt[n]
            if s >= LAG:
                q = s - LAG
                if q % 16 == 0:
                    xo.load(q, after=[offs])
                n = q % NG
                last_add[0] = free[n] = DVE.put(add_x(q, B[n]), after=[gts[q], last_add[0]])
        x1 = last_add[0]

        xt = layernorm([x1])
        top[0] = base0
        gw = take(2 * R).rearrange("p (k r) -> p k r", k=2)
        gbb = take(R)
        s_gw = stream("d_gw")
        quiet = everyone() + [xt]
        SP.dma(sync.dma_start, s_gw, gw, a["L0_ffn_gate_w"].rearrange("(k p) r -> p k r", p=P), after=quiet)
        gw_in = SP.dma(sync.dma_start, s_gw, gbb, a["L0_ffn_gate_b"].rearrange("(o r) -> o r", o=1).to_broadcast([P, R]))
        lg = take(NT * R).rearrange("p (t r) -> p t r", t=NT)
        m8 = take(NT * 8).rearrange("p (t r) -> p t r", t=NT)
        i8 = take(NT * 8, dt=U32).rearrange("p (t r) -> p t r", t=NT)
        i8f = take(NT * 8).rearrange("p (t r) -> p t r", t=NT)
        t1_ = take(NT * 2).rearrange("p (t r) -> p t r", t=NT)
        disp = take(NT * R).rearrange("p (t r) -> p t r", t=NT)
        dis2 = take(NT * R).rearrange("p (t r) -> p t r", t=NT)
        W1 = take(2 * 2 * HID).rearrange("p (b k h) -> p b k h", b=2, k=2)
        W2 = take(2 * 2 * HID).rearrange("p (b k h) -> p b k h", b=2, k=2)
        W3 = take(2 * 4 * D).rearrange("p (b k d) -> p b k d", b=2, k=4)
        hid = take(2 * 4 * 512).rearrange("p (b j n) -> p b j n", b=2, j=4)
        sil = take(2 * 512).rearrange("p (b n) -> p b n", b=2)
        s_ew = [stream(f"d_ew{i}") for i in range(2)]

        def load_expert(e, after):
            b = e % 2
            SP.dma(sync.dma_start, s_ew[b], W1[:, b], a["L0_ffn_w1"][e].rearrange("(k p) h -> p k h", p=P), after=after)
            SP.dma(sync.dma_start, s_ew[b], W2[:, b], a["L0_ffn_w2"][e].rearrange("(k p) h -> p k h", p=P))
            return SP.dma(sync.dma_start, s_ew[b], W3[:, b], a["L0_ffn_w3"][e].rearrange("(k p) d -> p k d", p=P))

        ew = {0: load_expert(0, []), 1: load_expert(1, [])}
        for i in range(NT):
            for k in range(2):
                mm = PE.put(ten.matmul, B[0][:, i * R:(i + 1) * R], XT[:, k, i * P:(i + 1) * P], gw[:, k, :],
                            start=(k == 0), stop=(k == 1), after=[gw_in, xt] + fr(0), sig=(k == 1))
        v = DVE.put(vec.tensor_tensor, lg, B[0][:, 0:NT * R].rearrange("p (t r) -> p t r", t=NT),
                    gbb.rearrange("p (o r) -> p o r", o=1).to_broadcast([P, NT, R]), ALU.add, after=[mm, gw_in] + quiet)
        free[0] = v

        def softmax(x, w, tmp, after):
            v = DVE.put(vec.tensor_reduce, tmp[:, :, 0], x, AX, ALU.max, after=after)
            v = DVE.put(vec.tensor_tensor, x, x, tmp[:, :, 0:1].to_broadcast([P, NT, w]), ALU.subtract, after=[v])
            v = AC.put(act.activation, x, x, ACT.Exp, after=[v])
            v = DVE.put(vec.tensor_reduce, tmp[:, :, 0], x, AX, ALU.add, after=[v])
            v = DVE.put(vec.reciprocal, tmp[:, :, 1], tmp[:, :, 0], after=[v])
            return DVE.put(vec.tensor_tensor, x, x, tmp[:, :, 1:2].to_broadcast([P, NT, w]), ALU.mult, after=[v])

        def top2(x, after):
            v = None
            for i in range(NT):
                v = DVE.put(vec.max, m8[:, i, :], x[:, i, :], after=after)
            for i in range(NT):
                v = DVE.put(vec.max_index, i8[:, i, :], m8[:, i, :], x[:, i, :], after=[v])
            return DVE.put(vec.tensor_copy, i8f, i8, after=[v])

        def spread(w, wide, dst, tmp, after):
            io = iorow[:, 0:wide].rearrange("p (o r) -> p o r", o=1).to_broadcast([P, NT, wide])
            u = []
            for j, o in enumerate((dst, tmp)):
                v = DVE.put(vec.tensor_tensor, o, io, i8f[:, :, j:j + 1].to_broadcast([P, NT, wide]), ALU.is_equal, after=after)
                u.append(DVE.put(vec.tensor_tensor, o, o, w[:, :, j:j + 1].to_broadcast([P, NT, wide]), ALU.mult, after=[v]))
            return DVE.put(vec.tensor_tensor, dst, dst, tmp, ALU.add, after=u)

        v = softmax(lg, R, t1_, [v])
        v = top2(lg, [v])
        v = DVE.put(vec.tensor_tensor, t1_[:, :, 0], m8[:, :, 0], m8[:, :, 1], ALU.add, after=[v])
        v = DVE.put(vec.reciprocal, t1_[:, :, 1], t1_[:, :, 0], after=[v])
        v = DVE.put(vec.tensor_tensor, m8[:, :, 0:2], m8[:, :, 0:2], t1_[:, :, 1:2].to_broadcast([P, NT, 2]), ALU.mult, after=[v])
        gate = spread(m8, R, disp, dis2, [v])

        hid_free = [None, None]
        sil_free = [None, None]
        e_done = {}
        nh = 0
        for e in range(R):
            wb = e % 2
            for tc in range(7):
                n0 = tc * 512
                nn = min(512, NP - n0)
                hb = tc % 2
                hs = []
                for j in range(4):
                    p1, p2 = 2 * (nh % 2), 2 * (nh % 2) + 1
                    for pb, W in ((p1, W1), (p2, W2)):
                        for k in range(2):
                            mm = PE.put(ten.matmul, B[pb][:, 0:nn], W[:, wb, k, j * P:(j + 1) * P], XT[:, k, n0:n0 + nn],
                                        start=(k == 0), stop=(k == 1), after=[ew[e]] + fr(pb), sig=(k == 1))
                    w = [t for t in [sil_free[nh % 2]] if t]
                    sl = free[p1] = AC.put(act.activation, sil[:, nh % 2, 0:nn], B[p1][:, 0:nn], ACT.Silu, after=[mm] + w + quiet)
                    w = [t for t in [hid_free[hb]] if t]
                    h = DVE.put(vec.tensor_tensor, hid[:, hb, j, 0:nn], sil[:, nh % 2, 0:nn], B[p2][:, 0:nn], ALU.mult,
                                after=[sl] + w)
                    free[p2] = sil_free[nh % 2] = h
                    hs.append(h)
                    nh += 1
                for q in range(nn // P):
                    i = tc * 4 + q
                    pb = 4 + i % 4
                    for j in range(4):
                        mm = PE.put(ten.matmul, B[pb][:, 0:D], hid[:, hb, j, q * P:(q + 1) * P], W3[:, wb, j, :],
                                    start=(j == 0), stop=(j == 3), after=[hs[-1]] + fr(pb), sig=(j == 3))
                    free[pb] = DVE.put(vec.scalar_tensor_tensor, X[:, i, :], B[pb][:, 0:D], disp[:, i, e:e + 1],
                                       X[:, i, :], ALU.mult, ALU.add, after=[mm, gate] + ([e_done[i]] if i in e_done else []))
                    e_done[i] = free[pb]
                hid_free[hb] = mm
            if e + 2 < R:
                ew[e + 2] = load_expert(e + 2, [mm])

        xt = layernorm([DVE.last()])
        top[0] = base0
        rep = take(2 * NCH * P).rearrange("p (g c) -> p g c", c=P)
        ACC = take(NS * MSG)
        acc3 = ACC.rearrange("p (n c) -> p n c", c=HW)
        wx = take(2 * 272).rearrange("p (k c) -> p k c", k=2)
        bb = take(D)
        tad = take(NS * 8)
        M = take(NS * 8)
        Mo = take(NS * 8)
        ln_ = take(NS * 8)
        lo_ = take(NS * 8)
        ft = take(NS * 8)
        TB = take(NS * 24, dt=BF16)
        TB3 = TB.rearrange("p (n c) -> p n c", c=48)
        tmid = take(NS * 8)
        G = [take(CH * ROW).rearrange("p (s c) -> p s c", c=ROW) for _ in range(2)]
        OH = XT[:, 0:2, :].rearrange("p k n -> p (k n)")[:, 0:CH * P].rearrange("p (s c) -> p s c", c=P)
        OT = XT[:, 0:2, :].rearrange("p k n -> p (k n)")[:, CH * P:CH * P + CH * P // 2].bitcast(BF16)
        g1 = G[1].rearrange("p s c -> p (s c)")
        hst = g1[:, 0:4 * ROW].rearrange("p (b c) -> p b c", b=4)
        avb = g1[:, 4 * ROW:4 * ROW + 2 * D].rearrange("p (s c) -> p s c", s=2)
        wtmp = g1[:, 4 * ROW + 2 * D:4 * ROW + 3 * D]
        AS = take(256).rearrange("p (g c) -> p g c", g=2)
        SC = take(256).rearrange("p (g c) -> p g c", g=2)
        SM = take(CH * 9).rearrange("p (s c) -> p s c", c=9)
        VV = take(CH * 8).rearrange("p (s c) -> p s c", c=8)
        vp = take(CH)
        EE = take(CH * 8).rearrange("p (s c) -> p s c", c=8)
        LL = take(CH * 8).rearrange("p (s c) -> p s c", c=8)
        EX = take(CH * 8).rearrange("p (s c) -> p s c", c=8)
        O = G[0].rearrange("p s c -> p (s c)")[:, 0:5 * D].rearrange("p (t c) -> p t c", c=D)
        O2 = G[0].rearrange("p s c -> p (s c)")[:, 5 * D:10 * D].rearrange("p (t c) -> p t c", c=D)
        s_rep = stream("d_rep")
        s_gat = [stream(f"d_gat{i}") for i in range(2)]
        s_ot = stream("d_ot")
        s_ht = [stream(f"d_ht{i}") for i in range(4)]
        s_gp = stream("d_gp")
        quiet = everyone() + [xt]
        rep_in = None
        for g in range(2 * NCH):
            rep_in = SP.dma(sync.dma_start, s_rep, rep[:, g, :],
                            RD[g * 16:(g + 1) * 16, :].rearrange("s (o c) -> s o c", o=1).to_broadcast([16, 8, P]),
                            after=quiet + [steps_ok])
        mo_ = Offsets(DVE, vec, 8, (NS - 1) * 8)
        ao_ = Offsets(DVE, vec, MSG, (NS - 1) * MSG)
        to_ = Offsets(PE, ten, 48, (NS - 1) * 48)

        def max_m(s, j):
            def go():
                o = M[:, bass.ds(mo_.at(s), 8)]
                return vec.tensor_tensor(o, o, VV[:, j, :], ALU.max)
            return go

        def add_acc(s, bank):
            def go():
                o = ACC[:, bass.ds(ao_.at(s), MSG)]
                return vec.tensor_tensor(o, o, bank[:, 0:MSG], ALU.add)
            return go

        def expand(s, j, b, k):
            def go():
                t = TB[:, bass.ds(to_.at(s), 48)][:, 16 * k:16 * k + 16]
                return ten.matmul(B[5][:, 16 * j:16 * j + 16], OT[:, j * P:(j + 1) * P], t,
                                  start=(k == 0), stop=(k == 2))
            return go

        def leaky(dst, src, after):
            return DVE.put(vec.scalar_tensor_tensor, dst, src, 0.2, src, ALU.mult, ALU.max, after=after)

        def gat(layer, xt, quiet):
            W, asrc, adst, bias = (a[f"L1_gnn_{n}{layer + 1}"] for n in ("W", "a_src", "a_dst", "b"))
            SP.dma(sync.dma_start, s_gp, wx[:, :, 0:D], W.rearrange("(k p) c -> p k c", p=P), after=quiet)
            for n, v in enumerate((asrc, adst)):
                SP.dma(sync.dma_start, s_gp, avb[:, n, :],
                       v.rearrange("h c -> (h c)").rearrange("(o c) -> o c", o=1).to_broadcast([P, D]))
            SP.dma(sync.dma_start, s_gp, bb, bias.rearrange("(o c) -> o c", o=1).to_broadcast([P, D]))
            p_in = s_gp.done()
            v = None
            for k in range(2):
                for n in range(2):
                    v = DVE.put(vec.tensor_tensor, wtmp, wx[:, k, 0:D], avb[:, n, :], ALU.mult,
                                after=[p_in] + ([v] if v else quiet))
                    v = DVE.put(vec.tensor_reduce, wx[:, k, D + 8 * n:D + 8 * n + 8],
                                wtmp.rearrange("p (h c) -> p h c", h=8), AX, ALU.add, after=[v])
            wx_ok = v
            z1 = DVE.put(vec.memset, tad[:, NT * 8:NS * 8], 0.0, after=quiet)
            z2 = DVE.put(vec.memset, hst, 1.0, after=quiet)
            DVE.put(vec.memset, ACC, 0.0)
            minit = DVE.put(vec.memset, M, -BIG)
            hfree = [None] * 4
            ad_ok = None
            for i in range(NT):
                b = i % 4
                for k in range(2):
                    mm = PE.put(ten.matmul, B[b][:, 0:272], XT[:, k, i * P:(i + 1) * P], wx[:, k, :],
                                start=(k == 0), stop=(k == 1), after=[xt, wx_ok] + fr(b), sig=(k == 1))
                w = [t for t in [hfree[b]] if t]
                AC.put(act.copy, hst[:, b, 0:MSG].rearrange("p (h c) -> p h c", c=HW)[:, :, 0:32],
                       B[b][:, 0:D].rearrange("p (h c) -> p h c", c=32), after=[mm, z2] + w)
                cp = AC.put(act.copy, hst[:, b, MSG:ROW], B[b][:, D:D + 8])
                ad_ok = free[b] = AC.put(act.copy, tad[:, i * 8:(i + 1) * 8], B[b][:, D + 8:D + 16], after=[z1])
                hfree[b] = SP.dma(sync.dma_start, s_ht[b], HT[layer][i * P:(i + 1) * P, :], hst[:, b, :], after=[cp])
            ht_ok = [s.done() for s in s_ht]
            ad3 = tad.rearrange("p (n h) -> p n h", h=8)

            def split(src, c, after):
                s3 = src.rearrange("p (n h) -> p n h", h=8)
                m3 = tmid.rearrange("p (n h) -> p n h", h=8)
                v = DVE.put(vec.tensor_copy, TB3[:, :, c:c + 8], s3, after=after)
                v = DVE.put(vec.tensor_tensor, m3, s3, TB3[:, :, c:c + 8], ALU.subtract, after=[v])
                v = DVE.put(vec.tensor_copy, TB3[:, :, c + 16:c + 24], m3, after=[v])
                v = DVE.put(vec.tensor_tensor, m3, m3, TB3[:, :, c + 16:c + 24], ALU.subtract, after=[v])
                return DVE.put(vec.tensor_copy, TB3[:, :, c + 32:c + 40], m3, after=[v])

            sp_ad = split(tad, 0, [ad_ok])
            use = [None, None]
            oh_free = None
            ot_free = None
            exp_last = None
            for c in range(NCH):
                b = c % 2
                w = [use[b]] if use[b] else quiet
                for j in range(CH):
                    s = c * CH + j
                    g_in = PL.dma(pool.indirect_dma_start, s_gat[b], G[b][:, j, :], None, HT[layer],
                                  bass.IndirectOffsetOnAxis(ap=srcT[:, s:s + 1], axis=0), after=ht_ok + w)
                w = [ot_free] if ot_free else ht_ok
                ot_in = SP.dma(sync.dma_start, s_ot, OT,
                               DLD[c * CH:(c + 1) * CH, :].rearrange("s c -> (s c)").rearrange("(o n) -> o n", o=1)
                               .to_broadcast([P, CH * P]), after=w)
                ot = DVE.put(vec.tensor_scalar, OT, OT, iocol[:, 0:1], None, ALU.is_equal, after=[ot_in])
                oh = DVE.put(vec.tensor_tensor, OH,
                             dlT[:, c * CH:(c + 1) * CH].rearrange("p (s o) -> p s o", o=1).to_broadcast([P, CH, P]),
                             iorow[:, :].rearrange("p (o c) -> p o c", o=1).to_broadcast([P, CH, P]), ALU.is_equal,
                             after=([oh_free] if oh_free else ht_ok))
                cp = DVE.put(vec.tensor_copy, AS.rearrange("p g (s h) -> p (g s) h", h=8), G[b][:, :, MSG:ROW], after=[g_in])
                sms = None
                scs = []
                for g in range(2):
                    tp = PE.put(ten.transpose, B[4][:, g * P:(g + 1) * P], AS[:, g, :], ident[:, :], after=[cp] + fr(4))
                for g in range(2):
                    scs.append(DVE.put(vec.tensor_tensor_scan, SC[:, g, :], rep[:, 2 * c + g, :], B[4][:, g * P:(g + 1) * P],
                                       -BIG, ALU.add, ALU.max, after=[tp, rep_in]))
                for g in range(2):
                    tp = PE.put(ten.transpose, B[7][:, g * P:(g + 1) * P], SC[:, g, :], ident[:, :], after=scs + fr(7))
                la = laT[:, c * CH:(c + 1) * CH].rearrange("p (s o) -> p s o", o=1)
                sm1 = DVE.put(vec.tensor_tensor, SM[:, :, 0:8], B[7][:, 0:256].rearrange("p (s h) -> p s h", h=8),
                              la.to_broadcast([P, CH, 8]), ALU.mult, after=[tp])
                free[4], free[7] = scs[1], sm1
                sm2 = DVE.put(vec.tensor_copy, SM[:, :, 8:9], la)
                for j in range(CH):
                    mm = PE.put(ten.matmul, B[6][:, 9 * j:9 * j + 9], OH[:, j, :], SM[:, j, :], start=True, stop=True,
                                after=[oh, sm1, sm2] + fr(6), sig=(j == CH - 1))
                pm = B[6][:, 0:9 * CH].rearrange("p (s c) -> p s c", c=9)
                v = DVE.put(vec.tensor_scalar, vp, pm[:, :, 8], -1.0, BIG, ALU.add, ALU.mult, after=[mm])
                vv = free[6] = DVE.put(vec.tensor_tensor, VV, pm[:, :, 0:8],
                                       vp.rearrange("p (s o) -> p s o", o=1).to_broadcast([P, CH, 8]), ALU.add, after=[v])
                mx = DVE.put(vec.tensor_copy, Mo, M, after=[minit])
                mx = vv if vv[1] > mx[1] else mx
                for j in range(CH):
                    s = c * CH + j
                    if s % 16 == 0:
                        mo_.load(s)
                    mx = DVE.put(max_m(s, j), after=[mx])
                v = DVE.put(vec.tensor_tensor, lo_, Mo, tad, ALU.add, after=[mx, sp_ad])
                v1 = leaky(lo_, lo_, [v])
                v = DVE.put(vec.tensor_tensor, ln_, M, tad, ALU.add, after=[mx] + ([exp_last] if exp_last else []))
                v2 = leaky(ln_, ln_, [v])
                v = DVE.put(vec.tensor_tensor, ft, lo_, ln_, ALU.subtract, after=[v1, v2])
                fx = AC.put(act.activation, ft, ft, ACT.Exp, after=[v])
                sp = split(ln_, 8, [v2] + ([exp_last] if exp_last else []))
                for j in range(CH):
                    s = c * CH + j
                    if s % 16 == 0:
                        to_.load(s)
                    for k in range(3):
                        mm = PE.put(expand(s, j, b, k), after=[sp, ot] + fr(5), sig=(j == CH - 1 and k == 2))
                exp_last = ot_free = mm
                pe = B[5][:, :].rearrange("p (s c) -> p s c", c=16)
                rs = DVE.put(vec.tensor_tensor, acc3, acc3,
                             ft.rearrange("p (n o) -> p n o", o=1).to_broadcast([P, NS * 8, HW]), ALU.mult,
                             after=[fx, DVE.last()])
                v = DVE.put(vec.tensor_tensor, EE, G[b][:, :, MSG:ROW], pe[:, :, 0:8], ALU.add, after=[mm])
                v = leaky(LL, EE, [v])
                v = DVE.put(vec.tensor_tensor, EE, LL, pe[:, :, 8:16], ALU.subtract, after=[v])
                free[5] = v
                v = DVE.put(vec.tensor_scalar, EE, EE, 0.0, None, ALU.min, after=[v])
                ex = AC.put(act.activation, EX, EE, ACT.Exp, after=[v])
                gm = G[b][:, :, 0:MSG].rearrange("p s (h c) -> p s h c", c=HW)
                ms = DVE.put(vec.tensor_tensor, gm, gm, EX.rearrange("p s (h o) -> p s h o", o=1).to_broadcast([P, CH, 8, HW]),
                             ALU.mult, after=[ex])
                ad = rs
                for j in range(CH):
                    s = c * CH + j
                    n = j % 4
                    mm = PE.put(ten.matmul, B[n][:, 0:MSG], OH[:, j, :], G[b][:, j, 0:MSG], start=True, stop=True,
                                after=[ms] + fr(n))
                    if s % 16 == 0:
                        ao_.load(s)
                    ad = free[n] = DVE.put(add_acc(s, B[n]), after=[mm, ad])
                use[b] = oh_free = mm
            return ad

        def heads(t0, t1, dst, after):
            k = t1 - t0
            num = acc3[:, t0 * 8:t1 * 8, 0:32]
            v = DVE.put(vec.tensor_tensor, dst.rearrange("p t (h c) -> p (t h) c", c=32), num,
                        ft[:, t0 * 8:t1 * 8].rearrange("p (n o) -> p n o", o=1).to_broadcast([P, 8 * k, 32]), ALU.mult,
                        after=after)
            return DVE.put(vec.tensor_tensor, dst, dst, bb.rearrange("p (o c) -> p o c", o=1).to_broadcast([P, k, D]),
                           ALU.add, after=[v])

        def denominators(after):
            v = DVE.put(vec.tensor_scalar, ft, acc3[:, :, 32], 1e-16, None, ALU.add, after=after)
            return DVE.put(vec.reciprocal, ft, ft, after=[v])

        ad = gat(0, xt, quiet)
        den = denominators([ad])
        v = PE.last()
        for t0 in range(0, NT, 5):
            v = heads(t0, t0 + 5, O, [den, v])
            v1 = DVE.put(vec.tensor_scalar, O2, O, 0.0, None, ALU.min, after=[v])
            v1 = AC.put(act.activation, O2, O2, ACT.Exp, after=[v1])
            v = DVE.put(vec.scalar_tensor_tensor, O, O, 0.0, O2, ALU.max, ALU.add, after=[v1])
            v = DVE.put(vec.tensor_scalar, O, O, -1.0, None, ALU.add, after=[v])
            for i in range(t0, t0 + 5):
                tp, xt = transpose_into_xt(i, O[:, i - t0, :], v, [])
            v = tp
        ad = gat(1, xt, everyone() + [xt])
        den = denominators([ad])
        v = DVE.last()
        for t0 in range(0, NT, 5):
            v = heads(t0, t0 + 5, O, [den, v])
            v = DVE.put(vec.tensor_tensor, X[:, t0:t0 + 5, :], X[:, t0:t0 + 5, :], O, ALU.add, after=[v])

        xt = layernorm([v])
        quiet = everyone() + [xt]
        top[0] = base0
        s_fw = stream("d_fw")

        def load(view, src, **kw):
            return SP.dma(sync.dma_start, s_fw, view, src, after=quiet, **kw)

        sW1 = take(2 * D).rearrange("p (k c) -> p k c", k=2)
        sW2 = take(2 * P).rearrange("p (k c) -> p k c", k=2)
        sW3 = take(D)
        eW1 = take(2 * 4 * P).rearrange("p (k e c) -> p k e c", k=2, e=4)
        eW2 = take(4 * 64).rearrange("p (e c) -> p e c", e=4)
        eW3 = take(4 * D).rearrange("p (e c) -> p e c", e=4)
        gW = take(2 * 4).rearrange("p (k c) -> p k c", k=2)
        gB = take(4)
        sb1 = take(2)
        sb2 = take(1)
        eb1 = take(4)
        eb2 = take(4)
        B5 = take(D)
        z = DVE.put(vec.memset, B5[0:8, :], 0.0, after=quiet)
        load(sW1, a["L1_ffn_sW1"].rearrange("(k p) c -> p k c", p=P))
        load(sW2, a["L1_ffn_sW2"].rearrange("(k p) c -> p k c", p=P))
        load(sW3, a["L1_ffn_sW3"])
        for k in range(2):
            load(eW1[:, k], a["L1_ffn_eW1"][:, k * P:(k + 1) * P, :].rearrange("e p c -> p e c"))
        load(eW2, a["L1_ffn_eW2"].rearrange("e p c -> p e c"))
        load(eW3[0:64], a["L1_ffn_eW3"].rearrange("e p c -> p e c"))
        load(gW, a["L1_ffn_gW"].rearrange("(k p) c -> p k c", p=P))
        load(gB, a["L1_ffn_gb"].rearrange("(o c) -> o c", o=1).to_broadcast([P, 4]))
        load(sb1, a["L1_ffn_sb1"].rearrange("(k p) -> p k", p=P), allow_slow_non_contiguous=True)
        load(sb2, a["L1_ffn_sb2"].rearrange("(p o) -> p o", o=1), allow_slow_non_contiguous=True)
        load(eb1, a["L1_ffn_eb1"].rearrange("e p -> p e"), allow_slow_non_contiguous=True)
        load(eb2[0:64], a["L1_ffn_eb2"].rearrange("e p -> p e"), allow_slow_non_contiguous=True)
        SP.dma(sync.dma_start, s_fw, B5[0:4, :], a["L1_ffn_eb3"], after=[z])
        w_in = SP.dma(sync.dma_start, s_fw, B5[4:5, :], a["L1_ffn_sb3"].rearrange("(o c) -> o c", o=1))

        lg4 = take(NT * 8).rearrange("p (t r) -> p t r", t=NT)
        m8 = take(NT * 8).rearrange("p (t r) -> p t r", t=NT)
        i8 = take(NT * 8, dt=U32).rearrange("p (t r) -> p t r", t=NT)
        i8f = take(NT * 8).rearrange("p (t r) -> p t r", t=NT)
        t2_ = take(NT * 2).rearrange("p (t r) -> p t r", t=NT)
        wts = take(NT * 8).rearrange("p (t r) -> p t r", t=NT)
        wt2 = take(NT * 8).rearrange("p (t r) -> p t r", t=NT)
        wT = take(NP)
        H1 = take(2 * 2 * 512).rearrange("p (b k n) -> p b k n", b=2, k=2)
        H2 = take(2 * 512).rearrange("p (b n) -> p b n", b=2)
        E1 = take(4 * 512).rearrange("p (b n) -> p b n", b=4)
        E2 = take(8 * 512).rearrange("p (b n) -> p b n", b=8)
        for i in range(NT):
            for k in range(2):
                mm = PE.put(ten.matmul, B[0][:, i * 4:(i + 1) * 4], XT[:, k, i * P:(i + 1) * P], gW[:, k, :],
                            start=(k == 0), stop=(k == 1), after=[w_in, xt] + fr(0), sig=(k == 1))
        z = DVE.put(vec.memset, lg4, -1.0, after=quiet)
        v = free[0] = DVE.put(vec.tensor_tensor, lg4[:, :, 0:4], B[0][:, 0:NT * 4].rearrange("p (t r) -> p t r", t=NT),
                              gB.rearrange("p (o r) -> p o r", o=1).to_broadcast([P, NT, 4]), ALU.add, after=[mm, z, w_in])
        v = softmax(lg4[:, :, 0:4], 4, t2_, [v])
        v = top2(lg4, [v])
        v = DVE.put(vec.tensor_tensor, t2_[:, :, 0], m8[:, :, 1], m8[:, :, 0], ALU.subtract, after=[v])
        v = AC.put(act.activation, m8[:, :, 1], t2_[:, :, 0], ACT.Exp, after=[v])
        v = DVE.put(vec.tensor_scalar, t2_[:, :, 0], m8[:, :, 1], 1.0, None, ALU.add, after=[v])
        v = DVE.put(vec.reciprocal, m8[:, :, 0], t2_[:, :, 0], after=[v])
        v = DVE.put(vec.tensor_tensor, m8[:, :, 1], m8[:, :, 1], m8[:, :, 0], ALU.mult, after=[v])
        v = spread(m8, 8, wts, wt2, [v])
        gate = DVE.put(vec.memset, wts[:, :, 4:5], 1.0, after=[v])
        for i in range(NT):
            b = i % 2
            tp = PE.put(ten.transpose, B[b][0:8, 0:P], wts[:, i, :], ident[:, :], after=[gate] + fr(b))
            wt_ok = free[b] = AC.put(act.copy, wT[0:8, i * P:(i + 1) * P], B[b][0:8, 0:P], after=[tp] + quiet)

        h1_free, h2_free, e1_free, e2_free = [None] * 2, [None] * 2, [None] * 4, [None] * 8
        ne_ = 0
        nb = 0
        final = {}

        def opt(t):
            return [t] if t else []

        for tc in range(7):
            n0 = tc * 512
            nn = min(512, NP - n0)
            hb = tc % 2

            def layer(dst, parts, lhs, rhs, bias, after, width=P):
                nonlocal nb
                b = nb % 4
                nb += 1
                for k in range(parts):
                    mm = PE.put(ten.matmul, B[b][0:width, 0:nn], lhs(k), rhs(k), start=(k == 0), stop=(k == parts - 1),
                                after=[w_in] + after + fr(b), sig=(k == parts - 1))
                free[b] = AC.put(act.activation, dst, B[b][0:width, 0:nn], ACT.Relu, bias=bias, after=[mm])
                return mm, free[b]

            def xr(k):
                return XT[:, k, n0:n0 + nn]

            r = []
            for m in range(2):
                r.append(layer(H1[:, hb, m, 0:nn], 2, lambda k: sW1[:, k, m * P:(m + 1) * P], xr, sb1[:, m:m + 1],
                               opt(h1_free[hb]))[1])
            h1_free[hb], h2 = layer(H2[:, hb, 0:nn], 2, lambda k: sW2[:, k, :], lambda k: H1[:, hb, k, 0:nn], sb2[:, 0:1],
                                    r + opt(h2_free[hb]))
            e2 = []
            for e in range(4):
                _, t = layer(E1[:, e, 0:nn], 2, lambda k: eW1[:, k, e, :], xr, eb1[:, e:e + 1], opt(e1_free[e]))
                e1_free[e], t = layer(E2[0:64, hb * 4 + e, 0:nn], 1, lambda k: eW2[:, e, :], lambda k: E1[:, e, 0:nn],
                                      eb2[0:64, e:e + 1], [t] + opt(e2_free[hb * 4 + e]), width=64)
                e2.append(t)
            for q in range(nn // P):
                i = tc * 4 + q
                b = 4 + ne_ % 4
                ne_ += 1
                PE.put(ten.matmul, B[b][:, 0:D], H2[:, hb, q * P:(q + 1) * P], sW3, start=True, stop=False,
                       after=[h2, wt_ok] + fr(b), sig=False)
                mm = PE.put(ten.matmul, B[b][:, 0:D], wT[0:8, i * P:(i + 1) * P], B5[0:8, :], start=False, stop=True)
                v = free[b] = DVE.put(vec.tensor_tensor, X[:, i, :], X[:, i, :], B[b][:, 0:D], ALU.add, after=[mm])
                h2_free[hb] = mm
                for e in range(4):
                    b = 4 + ne_ % 4
                    ne_ += 1
                    mm = PE.put(ten.matmul, B[b][:, 0:D], E2[0:64, hb * 4 + e, q * P:(q + 1) * P], eW3[0:64, e, :],
                                start=True, stop=True, after=[e2[e]] + fr(b))
                    e2_free[hb * 4 + e] = mm
                    v = free[b] = DVE.put(vec.scalar_tensor_tensor, X[:, i, :], B[b][:, 0:D], wts[:, i, e:e + 1],
                                          X[:, i, :], ALU.mult, ALU.add, after=[mm, v])
            k = nn // P
            if tc < 6:
                SP.dma(sync.dma_start, s_out, out[n0:n0 + nn, :].rearrange("(t p) d -> p t d", p=P),
                       X[:, tc * 4:tc * 4 + 4, :], after=[v])
            else:
                SP.dma(sync.dma_start, s_out, out[n0:N, :], X[0:N - n0, NT - 1, :], after=[v])

        block = ctx.enter_context(nc.Block())

        @block.sync
        def _(eng):
            SP.play(eng)
            eng.wait_ge(s_out.sem, s_out.n)

        @block.gpsimd
        def _(eng):
            PL.play(eng)

        @block.scalar
        def _(eng):
            AC.play(eng)

        @block.tensor
        def _(eng):
            PE.play(eng)

        @block.vector
        def _(eng):
            DVE.play(eng)


_INS = ['x', 'src', 'dst', 'edge_type_16', 'edge_weight1', 'L0_gnn_weight', 'L0_ffn_gate_w', 'L0_ffn_gate_b',
        'L0_ffn_w1', 'L0_ffn_w2', 'L0_ffn_w3', 'L1_gnn_W1', 'L1_gnn_a_src1', 'L1_gnn_a_dst1', 'L1_gnn_b1',
        'L1_gnn_W2', 'L1_gnn_a_src2', 'L1_gnn_a_dst2', 'L1_gnn_b2', 'L1_ffn_sW1', 'L1_ffn_sb1', 'L1_ffn_sW2',
        'L1_ffn_sb2', 'L1_ffn_sW3', 'L1_ffn_sb3', 'L1_ffn_eW1', 'L1_ffn_eb1', 'L1_ffn_eW2', 'L1_ffn_eb2',
        'L1_ffn_eW3', 'L1_ffn_eb3', 'L1_ffn_gW', 'L1_ffn_gb']


def kernel(**inputs):
    import numpy as _np
    import concourse.bacc as _bacc
    from concourse.bass_utils import run_bass_kernel_spmd as _run

    nc = _bacc.Bacc("TRN2", target_bir_lowering=False, num_devices=1)
    arrays, aps = {}, {}
    for name in _INS:
        v = _np.ascontiguousarray(inputs[name])
        arrays[f"in_{name}_dram"] = v
        aps[name] = nc.dram_tensor(f"in_{name}_dram", v.shape, mybir.dt.from_np(v.dtype), kind="ExternalInput").ap()
    out = nc.dram_tensor("out_0_dram", (N, D), F32, kind="ExternalOutput").ap()
    build(nc, aps, out)
    r = _run(nc, [arrays], core_ids=[0])
    return r.results[0]["out_0_dram"]
```

```python
from contextlib import ExitStack

import concourse.bass as bass
from concourse import mybir

F32 = mybir.dt.float32
BF16 = mybir.dt.bfloat16
I32 = mybir.dt.int32
U32 = mybir.dt.uint32
ALU = mybir.AluOpType
ACT = mybir.ActivationFunctionType
AX = mybir.AxisListType.X

P = 128
N = 3125
NT = 25
NP = NT * P
E = 50000
ET = 391
S = 416
NS = NT + 1
D = 256
R = 16
BIG = 1.0e30
CH = 16
NG4 = 4
NCH = S // CH
HW = 33
MSG = 8 * HW
ROW = MSG + 8
HID = 512
MT = (2 * NP + R * (P - 1)) // P


class Engine:

    def __init__(self, sem):
        self.sem = sem
        self.n = 0
        self.ops = []

    def put(self, fn, *args, after=(), sig=True, late=False, **kw):
        if sig:
            self.n += 1
        self.ops.append((fn, args, kw, tuple(after), (self.sem, 1) if sig else None, late))
        return (self.sem, self.n)

    def dma(self, fn, stream, *args, after=(), **kw):
        stream.n += 16
        self.ops.append((fn, args, kw, tuple(after), (stream.sem, 16), False))
        return (stream.sem, stream.n)

    def last(self):
        return (self.sem, self.n)

    def play(self, eng):
        seen = {}
        for fn, args, kw, after, inc, late in self.ops:
            need = {}
            for sem, v in after:
                if v > seen.get(id(sem), 0):
                    need[id(sem)] = (sem, v)
                    seen[id(sem)] = v
            need = list(need.values())
            own = need.pop() if late and need else None
            for sem, v in need:
                eng.wait_ge(sem, v)
            ins = fn(*args, **kw)
            if own is not None:
                ins.wait_op(*own, "sem-ge")
            if inc is not None:
                ins.then_inc(*inc)


class Stream:

    def __init__(self, sem):
        self.sem = sem
        self.n = 0

    def done(self):
        return (self.sem, self.n)


def build(nc, a, out):
    with ExitStack() as ctx:
        def sb(name, shape, dt=F32):
            return ctx.enter_context(nc.sbuf_tensor(name, shape, dt))

        def stream(name):
            return Stream(ctx.enter_context(nc.semaphore(name)))

        PE, DVE, AC, PL, SP = (Engine(ctx.enter_context(nc.semaphore("s_" + n)))
                               for n in ("pe", "dve", "act", "pool", "sp"))
        vec, act, ten, pool, sync = nc.vector, nc.scalar, nc.tensor, nc.gpsimd, nc.sync
        PS = ctx.enter_context(nc.psum_tensor("banks", [P, 8, 512], F32))
        B = [PS[:, i, :] for i in range(8)]

        XG = nc.dram_tensor("xg", [MT * P, D], F32, kind="Internal").ap()
        YG = nc.dram_tensor("yg", [MT * P, D], F32, kind="Internal").ap()
        TR = nc.dram_tensor("tr", [NP * R, D], F32, kind="Internal").ap()
        HT = [nc.dram_tensor(f"ht{i}", [NP, ROW], F32, kind="Internal").ap() for i in range(2)]
        SE = {k: nc.dram_tensor("se_" + k, [ET, P], F32 if k == "nrm" else I32, kind="Internal").ap()
              for k in ("src", "dst", "rel", "nrm")}
        RD = nc.dram_tensor("rd", [S, P], F32, kind="Internal").ap()
        DLD = nc.dram_tensor("dld", [S, P], BF16, kind="Internal").ap()

        X = sb("X", [P, NS, D])
        XT = sb("XT", [P, 2, NP])
        ident = sb("ident", [P, P])
        iorow = sb("iorow", [P, P])
        iocol = sb("iocol", [P, 1])
        iorowb = sb("iorowb", [P, P], BF16)
        dlTb = sb("dlTb", [P, 512], BF16)
        epsc = sb("epsc", [P, 1])
        ioi = sb("ioi", [P, P], I32)
        idx1T = sb("idx1T", [P, 512], I32)
        srcT = sb("srcT", [P, 512], I32)
        nrmT = sb("nrmT", [P, 512])
        dlT = sb("dlT", [P, 512])
        laT = sb("laT", [P, 512])
        doff = {m: sb(f"doff{m}", [1, S], I32) for m in (8, 48, D, MSG)}
        bns = sb("bns", [P, 4, 6])
        mv = sb("mv", [P, NT, 2])
        rstd = sb("rstd", [P, NT])
        xn = sb("xn", [P, 4, D])
        ARENA = 34050
        arena = sb("arena", [P, ARENA])
        top = [0]

        def take(n, shape=None, dt=F32):
            v = arena[:, top[0]:top[0] + n]
            top[0] += n
            assert top[0] <= ARENA, top[0]
            return v if dt == F32 else v.bitcast(dt)

        s_x = stream("d_x")
        s_x2 = stream("d_x2")
        s_out = stream("d_out")

        def everyone():
            return [q.last() for q in (PE, DVE, AC, PL, SP)]

        c0 = PL.put(pool.memset, ident[:, :], 0.0)
        c1 = PL.put(pool.affine_select, out=ident[:, :], in_=ident[:, :], compare_op=ALU.not_equal, fill=1.0,
                    base=0, pattern=[[-1, P]], channel_multiplier=1, after=[c0])
        c2 = PL.put(pool.iota, ioi[:, :], [[1, P]], base=0, channel_multiplier=0)
        k1 = DVE.put(vec.tensor_copy, iorow[:, :], ioi[:, :], after=[c2])
        c3 = PL.put(pool.iota, ioi[:, 0:1], [[0, 1]], base=0, channel_multiplier=1, after=[k1])
        k2 = DVE.put(vec.tensor_copy, iocol[:, :], ioi[:, 0:1], after=[c3])
        c4 = PL.put(pool.iota, ioi[:, 0:4], [[P, 4]], base=0, channel_multiplier=1, after=[k2])
        DVE.put(vec.tensor_copy, iorowb[:, :], iorow[:, :], after=[k1])
        k3 = DVE.put(vec.memset, epsc[:, :], 1e-5)
        xz = DVE.put(vec.memset, X[:, NT - 1:NS, :], 0.0)
        const = [c1, k1, k2, k3]

        x_main = SP.dma(sync.dma_start, s_x, X[:, 0:NT - 1, :],
                        a["x"][0:(NT - 1) * P, :].rearrange("(t p) d -> p t d", p=P))
        x_tail = SP.dma(sync.dma_start, s_x2, X[0:N - (NT - 1) * P, NT - 1, :], a["x"][(NT - 1) * P:N, :], after=[xz])

        free = [None] * 8

        def fr(b):
            return [free[b]] if free[b] else []

        def transpose_into_xt(i, src, ready, reuse):
            b = 6 + i % 2
            PE.put(ten.transpose, B[b][:, 0:P], src[:, 0:P], ident[:, :], after=[ready] + fr(b) + const, sig=False)
            t = PE.put(ten.transpose, B[b][:, P:2 * P], src[:, P:2 * P], ident[:, :])
            free[b] = AC.put(act.copy, XT[:, :, i * P:(i + 1) * P], B[b][:, 0:2 * P].rearrange("p (k c) -> p k c", k=2),
                             after=[t] + reuse)
            return t, free[b]

        xn_free = [None] * 4

        def layernorm(after, keep=None):
            reuse = [PE.last()]
            ag = None
            bs = [None] * 4
            for i in range(NT):
                st = DVE.put(vec.bn_stats, bns[:, i % 4, :], X[:, i, :], after=after + [t for t in [bs[i % 4]] if t])
                ag = bs[i % 4] = DVE.put(vec.bn_aggr, mv[:, i, :], bns[:, i % 4, :], after=[st])
            sq = AC.put(act.activation, rstd[:, :], mv[:, :, 1], ACT.Sqrt, bias=epsc[:, 0:1], after=[ag] + const)
            rc = DVE.put(vec.reciprocal, rstd[:, :], rstd[:, :], after=[sq])
            done = None
            for i in range(NT):
                w = [t for t in [xn_free[i % 4]] if t and keep is None]
                dst = xn[:, i % 4, :] if keep is None else keep[:, i, :]
                n = DVE.put(vec.tensor_scalar, dst, X[:, i, :], mv[:, i, 0:1], rstd[:, i:i + 1],
                            ALU.subtract, ALU.mult, after=[rc] + w)
                tp, done = transpose_into_xt(i, dst, n, reuse)
                if keep is None:
                    xn_free[i % 4] = tp
            return done

        xt = layernorm([x_main, x_tail])

        base0 = top[0]
        wrel = take(2 * R * D).rearrange("p (k r d) -> p k r d", k=2, r=R)
        stage = take(2 * R * D).rearrange("p (b n) -> p b n", b=2)
        s_w = stream("d_w")
        s_tr = [stream(f"d_tr{i}") for i in range(2)]
        for k in range(2):
            w_in = SP.dma(sync.dma_start, s_w, wrel[:, k, :, :],
                          a["L0_gnn_weight"][:, k * P:(k + 1) * P, :].rearrange("r p d -> p r d"))
        st_free = [None] * 2
        tr_rows = TR.rearrange("(n r) d -> n (r d)", r=R)
        for i in range(NT):
            cps = []
            for j in range(8):
                b = j % 6
                for k in range(2):
                    mm = PE.put(ten.matmul, B[b][:, :], XT[:, k, i * P:(i + 1) * P],
                                wrel[:, k, 2 * j:2 * j + 2, :].rearrange("p r d -> p (r d)"),
                                start=(k == 0), stop=(k == 1), after=[xt, w_in] + fr(b), sig=(k == 1))
                w = [t for t in [st_free[i % 2]] if t]
                free[b] = AC.put(act.copy, stage[:, i % 2, j * 512:(j + 1) * 512], B[b][:, :], after=[mm] + w)
            st_free[i % 2] = SP.dma(sync.dma_start, s_tr[i % 2], tr_rows[i * P:(i + 1) * P, :], stage[:, i % 2, :],
                                    after=[free[b]])
        tr_done = list(st_free)

        names = ("src", "dst", "rel", "nrm")
        inputs = {"src": a["src"], "dst": a["dst"], "rel": a["edge_type_16"],
                  "nrm": a["edge_weight1"].rearrange("e o -> (e o)")}
        full = (ET - 1) * P
        rest = E - full
        padi = take(P, dt=I32)
        padf = take(P)
        s_cp = stream("d_cp")
        pz = [DVE.put(vec.memset, padi[0:1, 0:64], 0), DVE.put(vec.memset, padi[0:1, 64:P], 1000000),
              DVE.put(vec.memset, padf[0:1, :], 0.0)]
        for k in names:
            PL.dma(pool.dma_start, s_cp, SE[k][0:ET - 1, :], inputs[k][0:full].rearrange("(t c) -> t c", c=P))
            PL.dma(pool.dma_start, s_cp, SE[k][ET - 1:ET, 0:rest], inputs[k][full:E].rearrange("(t c) -> t c", t=1))
            pad = {"src": padi[0:1, 0:P - rest], "rel": padi[0:1, 0:P - rest],
                   "dst": padi[0:1, 64:64 + P - rest], "nrm": padf[0:1, 0:P - rest]}[k]
            PL.dma(pool.dma_start, s_cp, SE[k][ET - 1:ET, rest:P], pad, after=pz)
        edges = s_cp.done()

        fi = take(4, dt=I32)
        ff = take(4)
        sio = take(4)
        thr = take(4)
        cnt = take(4)
        tf = take(4)
        ti = take(4, dt=I32)
        df = take(4)
        d128 = take(4)
        drow = take(512)
        diag = take(512).rearrange("p (g c) -> p g c", g=4)
        ones = take(P)
        junk = take(512)
        s_f = stream("d_f")
        z = DVE.put(vec.memset, fi, 1000000)
        PL.dma(pool.dma_start, s_f, fi[:, 0:3], SE["dst"][0:3 * P, 0:1].rearrange("(g p) o -> p (g o)", p=P),
               after=[edges, z], allow_slow_non_contiguous=True)
        f_in = PL.dma(pool.dma_start, s_f, fi[0:ET - 3 * P, 3:4], SE["dst"][3 * P:ET, 0:1], allow_slow_non_contiguous=True)
        o1 = DVE.put(vec.memset, ones, 1.0)
        v = DVE.put(vec.tensor_copy, sio, ioi[:, 0:4], after=[c4])
        t1 = DVE.put(vec.tensor_scalar, thr, sio, float(P), float(P), ALU.mult, ALU.add, after=[v])
        f1 = DVE.put(vec.tensor_copy, ff, fi, after=[f_in])
        f2 = DVE.put(vec.scalar_tensor_tensor, ff, sio, float(P), ff, ALU.mult, ALU.add, after=[f1])
        mm = None
        for g in range(4):
            q = DVE.put(vec.tensor_scalar, diag[:, g, :], ident[:, :], ff[:, g:g + 1], None, ALU.mult, after=[f2] + const)
            mm = PE.put(ten.matmul, B[0][:, g * P:(g + 1) * P], ones, diag[:, g, :], start=True, stop=True,
                        after=[q, o1] + fr(0))
        ct = None
        for g in range(4):
            w = [ct] if ct else []
            ct = DVE.put(vec.tensor_scalar, junk[:, 0:ET], B[0][:, 0:ET], thr[:, g:g + 1], None, ALU.is_lt, ALU.add,
                         accum_out=cnt[:, g:g + 1], after=[mm, t1] + w)
        free[0] = ct
        u = DVE.put(vec.tensor_scalar, tf, cnt, -1.0, 0.0, ALU.add, ALU.max, after=[ct])
        ti_ok = DVE.put(vec.tensor_copy, ti, tf, after=[u])
        u = DVE.put(vec.tensor_tensor, df, sio, tf, ALU.subtract, after=[u])
        d_ok = DVE.put(vec.tensor_scalar, d128, df, float(P), None, ALU.mult, after=[u])
        for g in range(4):
            mm = PE.put(ten.matmul, B[1][0:1, g * P:(g + 1) * P], df[:, g:g + 1], ident[:, :], start=True, stop=True,
                        after=[d_ok] + fr(1))
        u = DVE.put(vec.tensor_copy, drow[0:1, :], B[1][0:1, :], after=[mm])
        free[1] = u
        offs = None
        for m in doff:
            offs = DVE.put(vec.tensor_scalar, doff[m][:, :], drow[0:1, 0:S], float(m), None, ALU.mult, after=[u])

        rows = {k: take(512, dt=(F32 if k == "nrm" else I32)).rearrange("p (g c) -> p g c", g=4) for k in names}
        s_rw = stream("d_rw")
        zr = None
        for k in names:
            zr = DVE.put(vec.memset, rows[k][:, 3, :], 0.0 if k == "nrm" else 0)
        for k in names:
            for g in range(4):
                m = P if g < 3 else S - 3 * P
                PL.dma(pool.indirect_dma_start, s_rw, rows[k][0:m, g, :], None, SE[k],
                       bass.IndirectOffsetOnAxis(ap=ti[0:m, g:g + 1], axis=0), after=[ti_ok, edges, zr])
        got = s_rw.done()
        i1 = take(512).rearrange("p (g c) -> p g c", g=4)
        sf = take(512).rearrange("p (g c) -> p g c", g=4)
        dl = take(512).rearrange("p (g c) -> p g c", g=4)
        dlb = take(256, dt=BF16).rearrange("p (g c) -> p g c", g=4)
        ne = take(4 * (P + 1)).rearrange("p (g c) -> p g c", g=4)
        rr = take(512).rearrange("p (g c) -> p g c", g=4)
        q1 = DVE.put(vec.scalar_tensor_tensor, i1, rows["src"], float(R), rows["rel"], ALU.mult, ALU.add, after=[got])
        q2 = DVE.put(vec.tensor_copy, sf, rows["src"])
        for g in range(4):
            q3 = DVE.put(vec.tensor_scalar, dl[:, g, :], rows["dst"][:, g, :], d128[:, g:g + 1], None, ALU.subtract,
                         after=[d_ok])
        q4 = DVE.put(vec.tensor_copy, dlb, dl, after=[q3])
        DVE.put(vec.memset, ne[:, :, 0:1], 1.0)
        DVE.put(vec.memset, ne[:, :, P:P + 1], 1.0)
        q5 = DVE.put(vec.tensor_tensor, ne[:, :, 1:P], dl[:, :, 1:P], dl[:, :, 0:P - 1], ALU.not_equal)
        q6 = DVE.put(vec.tensor_scalar, rr, ne[:, :, 0:P], -BIG, None, ALU.mult, after=[q5])
        tabs = [(i1, idx1T, q1), (sf, srcT, q2), (rows["nrm"], nrmT, got), (dl, dlT, q3), (ne[:, :, 1:P + 1], laT, q5)]
        tab = {}
        for n, (src, dst, ok) in enumerate(tabs):
            b = 2 + n % 4
            for g in range(4):
                mm = PE.put(ten.transpose, B[b][:, g * P:(g + 1) * P], src[:, g, :], ident[:, :],
                            after=[ok] + fr(b) + const)
            tab[n] = free[b] = DVE.put(vec.tensor_copy, dst[:, :], B[b][:, :], after=[mm])
        tab[5] = DVE.put(vec.tensor_copy, dlTb[:, :], dlT[:, :], after=[tab[3]])
        s_dl = stream("d_dl")
        for src, dst, ok in ((rr, RD, q6), (dlb, DLD, q4)):
            SP.dma(sync.dma_start, s_dl, dst[0:3 * P, :].rearrange("(g p) c -> p g c", p=P), src[:, 0:3, :], after=[ok])
            SP.dma(sync.dma_start, s_dl, dst[3 * P:S, :], src[0:S - 3 * P, 3, :])
        steps_ok = s_dl.done()

        def reg_bank(eng, name):
            return [[eng.alloc_register(f"{name}{k}_{i}") for i in range(16)] for k in range(2)]

        class Offsets:

            def __init__(self, queue, eng, mult, most):
                self.q, self.eng, self.mult, self.most = queue, eng, mult, most

            def load(self, s0, after=()):
                bank = regs[self.q, self.mult == 8][(s0 // 16) % 2]
                self.q.put(self.eng.load, bank, doff[self.mult][0:1, s0:s0 + 16], sig=False, after=after)

            def at(self, s):
                r = regs[self.q, self.mult == 8][(s // 16) % 2][s % 16]
                return self.eng.snap(r, min_val=0, max_val=self.most)

        regs = {(DVE, False): reg_bank(vec, "rv"), (DVE, True): reg_bank(vec, "rm"), (PE, False): reg_bank(ten, "rp")}

        NG = 8
        Gr = take(NG * D).rearrange("p (n d) -> p n d", n=NG)
        OHr = take(NG * P).rearrange("p (n d) -> p n d", n=NG)
        s_g = [stream(f"d_g{i}") for i in range(NG)]
        xf = X[:, :, :].rearrange("p t d -> p (t d)")
        xo = Offsets(DVE, vec, D, (NS - 1) * D)
        mmt = [None] * NG
        gts = {}
        addt = [None] * 8
        last_add = [DVE.last()]
        ready = [tab[0], tab[2], tab[3]] + tr_done

        def add_x(s, bank):
            def go():
                o = xf[:, bass.ds(xo.at(s), D)]
                return vec.tensor_tensor(o, o, bank[:, 0:D], ALU.add)
            return go

        LAG = 3
        for s in range(S + LAG):
            if s < S:
                n = s % NG
                w = [mmt[n]] if mmt[n] else []
                g = PL.dma(pool.indirect_dma_start, s_g[n], Gr[:, n, :], None, TR,
                           bass.IndirectOffsetOnAxis(ap=idx1T[:, s:s + 1], axis=0), after=ready + w)
                oh = DVE.put(vec.tensor_scalar, OHr[:, n, :], iorow[:, :], dlT[:, s:s + 1], nrmT[:, s:s + 1],
                             ALU.is_equal, ALU.mult, after=w + [tab[2], tab[3]])
                mmt[n] = PE.put(ten.matmul, B[n][:, 0:D], OHr[:, n, :], Gr[:, n, :], start=True, stop=True,
                                after=[g, oh] + fr(n))
                gts[s] = mmt[n]
            if s >= LAG:
                q = s - LAG
                if q % 16 == 0:
                    xo.load(q, after=[offs])
                n = q % NG
                last_add[0] = free[n] = DVE.put(add_x(q, B[n]), after=[gts[q], last_add[0]], late=True)
        x1 = last_add[0]

        quiet = everyone() + [x1]
        top[0] = base0
        XN = take(NT * D).rearrange("p (t d) -> p t d", t=NT)
        zer = take(D)
        s_zg = stream("d_zg")
        z = DVE.put(vec.memset, zer, 0.0, after=quiet)
        for j in range(0, MT, 13):
            zg = SP.dma(sync.dma_start, s_zg, XG[j * P:(j + 13) * P, :].rearrange("(t p) d -> p t d", p=P),
                        zer.rearrange("p (o d) -> p o d", o=1).to_broadcast([P, 13, D]), after=[z])
        gw = take(2 * R).rearrange("p (k r) -> p k r", k=2)
        gbb = take(R)
        s_gw = stream("d_gw")
        SP.dma(sync.dma_start, s_gw, gw, a["L0_ffn_gate_w"].rearrange("(k p) r -> p k r", p=P), after=quiet)
        gw_in = SP.dma(sync.dma_start, s_gw, gbb, a["L0_ffn_gate_b"].rearrange("(o r) -> o r", o=1).to_broadcast([P, R]))
        lg = take(NT * R).rearrange("p (t r) -> p t r", t=NT)
        m8 = take(NT * 8).rearrange("p (t r) -> p t r", t=NT)
        i8 = take(NT * 8, dt=U32).rearrange("p (t r) -> p t r", t=NT)
        i8f = take(NT * 8).rearrange("p (t r) -> p t r", t=NT)
        t1_ = take(NT * 2).rearrange("p (t r) -> p t r", t=NT)
        oh2 = [take(NT * R).rearrange("p (t r) -> p t r", t=NT) for _ in range(2)]
        A_ = take(NT * R)
        A3 = A_.rearrange("p (t r) -> p t r", t=NT)
        totT = take(NT * R)
        inc = take(NT * R)
        msk = take(NT * R)
        cmp_ = take(MT * R)
        nt_ = take(R)
        ts_ = take(R)
        ej = take(MT + 1)
        eji = take(MT + 15, dt=I32)
        posf = take(2 * NT).rearrange("p (k t) -> p k t", k=2)
        posi = take(2 * NT, dt=I32).rearrange("p (k t) -> p k t", k=2)
        upper = take(P)
        ones = take(P)
        NW = 3
        W1 = [take(2 * HID).rearrange("p (k h) -> p k h", k=2) for _ in range(NW)]
        W2 = [take(2 * HID).rearrange("p (k h) -> p k h", k=2) for _ in range(NW)]
        W3 = [take(4 * D).rearrange("p (k d) -> p k d", k=4) for _ in range(NW)]
        XGt = [take(D) for _ in range(NW)]
        xTt = [take(2 * P).rearrange("p (k c) -> p k c", k=2) for _ in range(2)]
        sil = [take(512) for _ in range(2)]
        hid = [take(512) for _ in range(2)]
        yst = [take(D) for _ in range(2)]
        YB = [take(2 * D).rearrange("p (k d) -> p k d", k=2) for _ in range(4)]

        xt = layernorm([x1], keep=XN)
        o1 = DVE.put(vec.memset, ones, 1.0, after=quiet)
        u0 = PL.put(pool.memset, upper, 1.0, after=quiet)
        u0 = PL.put(pool.affine_select, out=upper, in_=upper, compare_op=ALU.is_gt, fill=0.0, base=0,
                    pattern=[[1, P]], channel_multiplier=-1, after=[u0])
        DVE.put(vec.memset, msk, 1.0)
        mk = DVE.put(vec.memset, msk.rearrange("p (r t) -> p r t", r=R)[:, :, 0:1], 0.0, after=[DVE.last()])
        for i in range(NT):
            for k in range(2):
                mm = PE.put(ten.matmul, B[0][:, i * R:(i + 1) * R], XT[:, k, i * P:(i + 1) * P], gw[:, k, :],
                            start=(k == 0), stop=(k == 1), after=[gw_in, xt] + fr(0), sig=(k == 1))
        v = DVE.put(vec.tensor_tensor, lg, B[0][:, 0:NT * R].rearrange("p (t r) -> p t r", t=NT),
                    gbb.rearrange("p (o r) -> p o r", o=1).to_broadcast([P, NT, R]), ALU.add, after=[mm, gw_in])
        free[0] = v

        def softmax(x, w, tmp, after):
            v = DVE.put(vec.tensor_reduce, tmp[:, :, 0], x, AX, ALU.max, after=after)
            v = DVE.put(vec.tensor_tensor, x, x, tmp[:, :, 0:1].to_broadcast([P, NT, w]), ALU.subtract, after=[v])
            v = AC.put(act.activation, x, x, ACT.Exp, after=[v])
            v = DVE.put(vec.tensor_reduce, tmp[:, :, 0], x, AX, ALU.add, after=[v])
            v = DVE.put(vec.reciprocal, tmp[:, :, 1], tmp[:, :, 0], after=[v])
            return DVE.put(vec.tensor_tensor, x, x, tmp[:, :, 1:2].to_broadcast([P, NT, w]), ALU.mult, after=[v])

        def top2(x, after):
            v = None
            for i in range(NT):
                v = DVE.put(vec.max, m8[:, i, :], x[:, i, :], after=after)
            for i in range(NT):
                v = DVE.put(vec.max_index, i8[:, i, :], m8[:, i, :], x[:, i, :], after=[v])
            return DVE.put(vec.tensor_copy, i8f, i8, after=[v])

        def spread(w, wide, dst, tmp, after):
            io = iorow[:, 0:wide].rearrange("p (o r) -> p o r", o=1).to_broadcast([P, NT, wide])
            u = []
            for j, o in enumerate((dst, tmp)):
                v = DVE.put(vec.tensor_tensor, o, io, i8f[:, :, j:j + 1].to_broadcast([P, NT, wide]), ALU.is_equal, after=after)
                u.append(DVE.put(vec.tensor_tensor, o, o, w[:, :, j:j + 1].to_broadcast([P, NT, wide]), ALU.mult, after=[v]))
            return DVE.put(vec.tensor_tensor, dst, dst, tmp, ALU.add, after=u)

        v = softmax(lg, R, t1_, [v])
        v = tops = top2(lg, [v])
        io = iorow[:, 0:R].rearrange("p (o r) -> p o r", o=1).to_broadcast([P, NT, R])
        u = [DVE.put(vec.tensor_tensor, oh2[k], io, i8f[:, :, k:k + 1].to_broadcast([P, NT, R]), ALU.is_equal, after=[v])
             for k in range(2)]
        v = DVE.put(vec.tensor_tensor, A3, oh2[0], oh2[1], ALU.add, after=u)
        mp = PE.put(ten.matmul, B[1][:, 0:NT * R], upper, A_, start=True, stop=True, after=[v, u0] + fr(1))
        mt = PE.put(ten.matmul, B[2][:, 0:NT * R], ones, A_, start=True, stop=True, after=[o1] + fr(2))
        v = DVE.put(vec.tensor_tensor, t1_[:, :, 0], m8[:, :, 0], m8[:, :, 1], ALU.add, after=[tops])
        v = DVE.put(vec.reciprocal, t1_[:, :, 1], t1_[:, :, 0], after=[v])
        gate = DVE.put(vec.tensor_tensor, m8[:, :, 0:2], m8[:, :, 0:2], t1_[:, :, 1:2].to_broadcast([P, NT, 2]), ALU.mult,
                       after=[v])
        tot3 = totT.rearrange("p (r t) -> p r t", r=R)
        inc3 = inc.rearrange("p (r t) -> p r t", r=R)
        v = DVE.put(vec.tensor_copy, tot3, B[2][:, 0:NT * R].rearrange("p (t r) -> p r t", t=NT), after=[mt])
        free[2] = v
        vi = DVE.put(vec.tensor_tensor_scan, inc, msk, totT, 0.0, ALU.mult, ALU.add, after=[v, mk])
        cm3 = cmp_[:, 0:NT * R].rearrange("p (r t) -> p r t", r=R)
        v = DVE.put(vec.tensor_scalar, cm3, iorow[:, 0:NT].rearrange("p (o t) -> p o t", o=1).to_broadcast([P, R, NT]),
                    float(P), None, ALU.mult, after=quiet)
        v = DVE.put(vec.tensor_tensor, cm3, inc3[:, :, NT - 1:NT].to_broadcast([P, R, NT]), cm3, ALU.is_gt, after=[vi, v])
        v = DVE.put(vec.tensor_reduce, nt_, cm3, AX, ALU.add, after=[v])
        v = DVE.put(vec.tensor_tensor_scan, ts_, ones[:, 0:R], nt_, 0.0, ALU.mult, ALU.add, after=[v, o1])
        v = vts = DVE.put(vec.tensor_tensor, ts_, ts_, nt_, ALU.subtract, after=[v])
        v2 = DVE.put(vec.tensor_tensor, inc, inc, totT, ALU.subtract, after=[v])
        v = DVE.put(vec.scalar_tensor_tensor, inc3, ts_.rearrange("p (r o) -> p r o", o=1).to_broadcast([P, R, NT]), float(P),
                    inc3, ALU.mult, ALU.add, after=[v2])
        v = DVE.put(vec.tensor_tensor, A3, B[1][:, 0:NT * R].rearrange("p (t r) -> p t r", t=NT),
                    inc.rearrange("p (r t) -> p t r", r=R), ALU.add, after=[v, mp, mt])
        free[1] = v
        u = []
        for k in range(2):
            w = DVE.put(vec.tensor_tensor, oh2[k], oh2[k], A3, ALU.mult, after=[v])
            u.append(DVE.put(vec.tensor_reduce, posf[:, k, :], oh2[k], AX, ALU.add, after=[w]))
        pos_ok = DVE.put(vec.tensor_copy, posi, posf, after=u)
        cj = cmp_.rearrange("p (j r) -> p j r", r=R)
        v = DVE.put(vec.tensor_tensor, cj[0:1], ts_[0:1].rearrange("p (o r) -> p o r", o=1).to_broadcast([1, MT, R]),
                    iorow[0:1, 0:MT].rearrange("p (j o) -> p j o", o=1).to_broadcast([1, MT, R]), ALU.is_le, after=[vts])
        v = DVE.put(vec.tensor_reduce, ej[0:1, 0:MT], cj[0:1], AX, ALU.add, after=[v])
        v = DVE.put(vec.tensor_scalar, ej[0:1, 0:MT], ej[0:1, 0:MT], -1.0, None, ALU.add, after=[v])
        z = DVE.put(vec.memset, eji[0:1, :], 0, after=quiet)
        ej_ok = DVE.put(vec.tensor_copy, eji[0:1, 0:MT], ej[0:1, 0:MT], after=[v, z])

        s_sc = stream("d_sc")
        for i in range(NT):
            for k in range(2):
                sc = PL.dma(pool.indirect_dma_start, s_sc, XG, bass.IndirectOffsetOnAxis(ap=posi[:, k, i:i + 1], axis=0),
                            XN[:, i, :], None, after=[pos_ok, zg, xt])

        s_ew = [stream(f"d_ew{i}") for i in range(NW)]
        s_xg = [stream(f"d_xg{i}") for i in range(NW)]
        s_yg = [stream(f"d_yg{i}") for i in range(2)]
        rsp = [[sync.alloc_register(f"rs{k}_{i}") for i in range(16)] for k in range(2)]
        wv = [a[n].rearrange("e (k p) h -> p e k h", p=P) for n in ("L0_ffn_w1", "L0_ffn_w2", "L0_ffn_w3")]

        def weights(j, n, dst):
            def go():
                e = sync.snap(rsp[(j // 16) % 2][j % 16], min_val=0, max_val=R - 1)
                return sync.dma_start(dst.rearrange("p (o k) h -> p o k h", o=1), wv[n][:, bass.ds(e, 1), :, :])
            return go

        w_free = [None] * NW
        g_free = [None] * NW
        ew, xg = {}, {}

        def opt(t):
            return [t] if t else []

        def load_tile(j):
            b = j % NW
            if j % 16 == 0:
                SP.put(sync.load, rsp[(j // 16) % 2], eji[0:1, j:j + 16], sig=False, after=[ej_ok])
            for n, W in enumerate((W1, W2, W3)):
                ew[j] = SP.dma(weights(j, n, W[b]), s_ew[b], after=opt(w_free[b]) + [ej_ok] + quiet)

        def load_rows(j):
            b = j % NW
            xg[j] = SP.dma(sync.dma_start, s_xg[b], XGt[b], XG[j * P:(j + 1) * P, :], after=[sc] + opt(g_free[b]))

        for j in range(NW):
            load_tile(j)
        for j in range(NW):
            load_rows(j)
        xt_free, sil_free, hid_free, y_free = [None] * 2, [None] * 2, [None] * 2, [None] * 2
        xt_ok, hid_ok = {}, {}

        def turn(j):
            b, c = j % NW, j % 2
            for k in range(2):
                t = PE.put(ten.transpose, B[6 + c][:, k * P:(k + 1) * P], XGt[b][:, k * P:(k + 1) * P], ident[:, :],
                           after=[xg[j]] + fr(6 + c))
            g_free[b] = t
            xt_ok[j] = free[6 + c] = AC.put(act.copy, xTt[c], B[6 + c][:, 0:2 * P].rearrange("p (k c) -> p k c", k=2),
                                            after=[t] + opt(xt_free[c]) + quiet)
            if j + NW < MT:
                load_rows(j + NW)

        def up(j):
            b, c = j % NW, j % 2
            for bank, W in ((c, W1), (2 + c, W2)):
                for h in range(4):
                    for k in range(2):
                        mm = PE.put(ten.matmul, B[bank][:, h * P:(h + 1) * P], W[b][:, k, h * P:(h + 1) * P], xTt[c][:, k, :],
                                    start=(k == 0), stop=(k == 1), after=[ew[j], xt_ok[j]] + fr(bank), sig=(h == 3 and k == 1))
                if bank == c:
                    sl = free[bank] = AC.put(act.activation, sil[c], B[bank][:, :], ACT.Silu, after=[mm] + opt(sil_free[c]) + quiet)
            xt_free[c] = mm
            hid_ok[j] = free[2 + c] = sil_free[c] = DVE.put(vec.tensor_tensor, hid[c], sil[c], B[2 + c][:, :], ALU.mult,
                                                            after=[mm, sl] + opt(hid_free[c]))

        def down(j):
            b, c = j % NW, j % 2
            for h in range(4):
                mm = PE.put(ten.matmul, B[4 + c][:, 0:D], hid[c][:, h * P:(h + 1) * P], W3[b][:, h, :],
                            start=(h == 0), stop=(h == 3), after=[hid_ok[j]] + fr(4 + c), sig=(h == 3))
            hid_free[c] = w_free[b] = mm
            y = free[4 + c] = DVE.put(vec.tensor_copy, yst[c], B[4 + c][:, 0:D], after=[mm] + opt(y_free[c]))
            y_free[c] = AC.dma(act.dma_start, s_yg[c], YG[j * P:(j + 1) * P, :], yst[c], after=[y])
            if j + NW < MT:
                load_tile(j + NW)

        turn(0)
        for j in range(MT):
            if j + 1 < MT:
                turn(j + 1)
            up(j)
            if j:
                down(j - 1)
        down(MT - 1)

        s_yb = [stream(f"d_yb{i}") for i in range(4)]
        yb_free = [None] * 4
        for i in range(NT):
            b = i % 4
            for k in range(2):
                g = PL.dma(pool.indirect_dma_start, s_yb[b], YB[b][:, k, :], None, YG,
                           bass.IndirectOffsetOnAxis(ap=posi[:, k, i:i + 1], axis=0),
                           after=y_free + opt(yb_free[b]) + [pos_ok] + quiet)
            v = DVE.put(vec.scalar_tensor_tensor, X[:, i, :], YB[b][:, 0, :], m8[:, i, 0:1], X[:, i, :], ALU.mult, ALU.add,
                        after=[g, gate])
            v = yb_free[b] = DVE.put(vec.scalar_tensor_tensor, X[:, i, :], YB[b][:, 1, :], m8[:, i, 1:2], X[:, i, :],
                                     ALU.mult, ALU.add, after=[v])

        xt = layernorm([DVE.last()])
        top[0] = base0
        rep = [dlT[:, i * P:(i + 1) * P] for i in range(2)]
        AS, SC = xn[:, 0, 0:P], xn[:, 1, 0:P]
        SM, EE, VV = (xn[:, 2, 0:P], xn[:, 3, 0:P], nrmT[:, 0:P])
        SM, EE, VV = (v.rearrange("p (s c) -> p s c", c=8) for v in (SM, EE, VV))
        EX = [nrmT[:, (1 + i) * P:(2 + i) * P].rearrange("p (s c) -> p s c", c=8) for i in range(2)]
        ACC = take(NS * MSG)
        acc3 = ACC.rearrange("p (n c) -> p n c", c=HW)
        wx = take(2 * 272).rearrange("p (k c) -> p k c", k=2)
        bb = take(D)
        tad = take(NS * 8)
        M = take(NS * 8)
        ln_ = take(NS * 8)
        Mo = take(8)
        lo_ = take(8)
        fc = take(8)
        ft = take(NS * 8)
        TB = take(NS * 24, dt=BF16)
        TB3 = TB.rearrange("p (n c) -> p n c", c=48)
        tmid = take(NS * 8)
        Gall = take(NG4 * CH * ROW)
        G = [Gall[:, i * CH * ROW:(i + 1) * CH * ROW].rearrange("p (s c) -> p s c", c=ROW) for i in range(NG4)]
        xtf = XT[:, :, :].rearrange("p k n -> p (k n)")
        OH = [xtf[:, i * CH * P:(i + 1) * CH * P].rearrange("p (s c) -> p s c", c=P) for i in range(2)]
        OT = [xtf[:, (4 + i) * CH * P // 2:(5 + i) * CH * P // 2].bitcast(BF16) for i in range(2)]
        g1 = Gall[:, 3 * CH * ROW:4 * CH * ROW]
        g1 = G[1].rearrange("p s c -> p (s c)")
        hst = g1[:, 0:4 * ROW].rearrange("p (b c) -> p b c", b=4)
        avb = g1[:, 4 * ROW:4 * ROW + 2 * D].rearrange("p (s c) -> p s c", s=2)
        wtmp = g1[:, 4 * ROW + 2 * D:4 * ROW + 3 * D]
        SB = take(CH * 13, dt=BF16).rearrange("p (s c) -> p s c", c=26)
        OHb = [take(CH * P // 2, dt=BF16).rearrange("p (s c) -> p s c", c=P) for _ in range(2)]
        vp = take(CH)
        O = Gall[:, 0:5 * D].rearrange("p (t c) -> p t c", c=D)
        O2 = Gall[:, 5 * D:10 * D].rearrange("p (t c) -> p t c", c=D)
        s_rep = [stream(f"d_rep{i}") for i in range(2)]
        s_gat = [stream(f"d_gat{i}") for i in range(NG4)]
        s_ot = [stream(f"d_ot{i}") for i in range(2)]
        s_ht = [stream(f"d_ht{i}") for i in range(4)]
        s_gp = stream("d_gp")
        quiet = everyone() + [xt]
        mo_ = Offsets(DVE, vec, 8, (NS - 1) * 8)
        ao_ = Offsets(DVE, vec, MSG, (NS - 1) * MSG)
        to_ = Offsets(PE, ten, 48, (NS - 1) * 48)

        def keep_m(s):
            return lambda: vec.tensor_copy(Mo, M[:, bass.ds(mo_.at(s), 8)])

        def old_m(s):
            return lambda: vec.tensor_tensor(lo_, Mo, tad[:, bass.ds(mo_.at(s), 8)], ALU.add)

        def drop_m(s):
            return lambda: vec.tensor_tensor(fc, lo_, ln_[:, bass.ds(mo_.at(s), 8)], ALU.subtract)

        def rescale(s):
            def go():
                o = ACC[:, bass.ds(ao_.at(s), MSG)].rearrange("p (h c) -> p h c", c=HW)
                return vec.tensor_tensor(o, o, fc.rearrange("p (h o) -> p h o", o=1).to_broadcast([P, 8, HW]), ALU.mult)
            return go

        def max_m(s, j):
            def go():
                o = M[:, bass.ds(mo_.at(s), 8)]
                return vec.tensor_tensor(o, o, VV[:, j, :], ALU.max)
            return go

        def add_acc(s, bank):
            def go():
                o = ACC[:, bass.ds(ao_.at(s), MSG)]
                return vec.tensor_tensor(o, o, bank[:, 0:MSG], ALU.add)
            return go

        def expand(s, j, b):
            def go():
                t = TB[:, bass.ds(to_.at(s), 48)]
                return ten.matmul(B[4 + j // 8][:, 48 * (j % 8):48 * (j % 8) + 48], OT[b][:, j * P:(j + 1) * P], t,
                                  start=True, stop=True)
            return go

        def leaky(dst, src, after):
            return DVE.put(vec.scalar_tensor_tensor, dst, src, 0.2, src, ALU.mult, ALU.max, after=after)

        def gat(layer, xt, quiet):
            W, asrc, adst, bias = (a[f"L1_gnn_{n}{layer + 1}"] for n in ("W", "a_src", "a_dst", "b"))
            SP.dma(sync.dma_start, s_gp, wx[:, :, 0:D], W.rearrange("(k p) c -> p k c", p=P), after=quiet)
            for n, v in enumerate((asrc, adst)):
                SP.dma(sync.dma_start, s_gp, avb[:, n, :],
                       v.rearrange("h c -> (h c)").rearrange("(o c) -> o c", o=1).to_broadcast([P, D]))
            SP.dma(sync.dma_start, s_gp, bb, bias.rearrange("(o c) -> o c", o=1).to_broadcast([P, D]))
            p_in = s_gp.done()
            v = None
            for k in range(2):
                for n in range(2):
                    v = DVE.put(vec.tensor_tensor, wtmp, wx[:, k, 0:D], avb[:, n, :], ALU.mult,
                                after=[p_in] + ([v] if v else quiet))
                    v = DVE.put(vec.tensor_reduce, wx[:, k, D + 8 * n:D + 8 * n + 8],
                                wtmp.rearrange("p (h c) -> p h c", h=8), AX, ALU.add, after=[v])
            wx_ok = v
            z1 = DVE.put(vec.memset, tad[:, NT * 8:NS * 8], 0.0, after=quiet)
            z2 = DVE.put(vec.memset, hst, 1.0, after=quiet)
            DVE.put(vec.memset, ACC, 0.0)
            minit = DVE.put(vec.memset, M, -BIG)
            hfree = [None] * 4
            ad_ok = None
            for i in range(NT):
                b = i % 4
                for k in range(2):
                    mm = PE.put(ten.matmul, B[b][:, 0:272], XT[:, k, i * P:(i + 1) * P], wx[:, k, :],
                                start=(k == 0), stop=(k == 1), after=[xt, wx_ok] + fr(b), sig=(k == 1))
                w = [t for t in [hfree[b]] if t]
                AC.put(act.copy, hst[:, b, 0:MSG].rearrange("p (h c) -> p h c", c=HW)[:, :, 0:32],
                       B[b][:, 0:D].rearrange("p (h c) -> p h c", c=32), after=[mm, z2] + w)
                cp = AC.put(act.copy, hst[:, b, MSG:ROW], B[b][:, D:D + 8])
                ad_ok = free[b] = AC.put(act.copy, tad[:, i * 8:(i + 1) * 8], B[b][:, D + 8:D + 16], after=[z1])
                hfree[b] = SP.dma(sync.dma_start, s_ht[b], HT[layer][i * P:(i + 1) * P, :], hst[:, b, :], after=[cp])
            ht_ok = [s.done() for s in s_ht]
            ad3 = tad.rearrange("p (n h) -> p n h", h=8)

            tok = {}

            def thirds(dst, c, step, src, rest, after):
                v = DVE.put(vec.tensor_copy, dst[:, :, c:c + 8], src, after=after)
                yield
                v = DVE.put(vec.tensor_tensor, rest, src, dst[:, :, c:c + 8], ALU.subtract, after=[v])
                yield
                v = DVE.put(vec.tensor_copy, dst[:, :, c + step:c + step + 8], rest, after=[v])
                yield
                v = DVE.put(vec.tensor_tensor, rest, rest, dst[:, :, c + step:c + step + 8], ALU.subtract, after=[v])
                yield
                tok["sp" if dst is TB3 else "sb"] = DVE.put(vec.tensor_copy, dst[:, :, c + 2 * step:c + 2 * step + 8], rest, after=[v])
                yield

            def split(src, c, after):
                return thirds(TB3, c, 16, src.rearrange("p (n h) -> p n h", h=8), tmid.rearrange("p (n h) -> p n h", h=8), after)

            for _ in split(tad, 0, [ad_ok]):
                pass
            sp_ad = tok["sp"]
            slots = [[None] * CH for _ in range(NG4)]
            ot_free, rep_free, oh_free = [None] * 2, [None] * 2, [None] * 2
            g_in, ot_in, rep_in, oh_ok, ob_ok, ot_ok, w_ok = {}, {}, {}, {}, {}, {}, {}
            last_max = [minit]
            last_add = [minit]

            def gathers(c):
                b = c % NG4
                for j in range(CH):
                    s = c * CH + j
                    w = opt(slots[b][j // 4 * 4 + 3]) + ht_ok + quiet
                    g_in[c] = PL.dma(pool.indirect_dma_start, s_gat[b], G[b][:, j, :], None, HT[layer],
                                     bass.IndirectOffsetOnAxis(ap=srcT[:, s:s + 1], axis=0), after=w)

            def fetch(c):
                b = c % 2
                rep_in[c] = SP.dma(sync.dma_start, s_rep[b], rep[b],
                                   RD[c * CH:(c + 1) * CH, :].rearrange("s (o c) -> s o c", o=1).to_broadcast([CH, 8, P]),
                                   after=opt(rep_free[b]) + quiet + [steps_ok])
                ot_in[c] = SP.dma(sync.dma_start, s_ot[b], OT[b],
                                  DLD[c * CH:(c + 1) * CH, :].rearrange("s c -> (s c)").rearrange("(o n) -> o n", o=1)
                                  .to_broadcast([P, CH * P]), after=opt(ot_free[b]) + ht_ok)

            def turn_scores(c):
                cp = DVE.put(vec.tensor_copy, AS.rearrange("p (s h) -> p s h", h=8), G[c % NG4][:, :, MSG:ROW], after=[g_in[c]])
                tok["t"] = PE.put(ten.transpose, B[7][:, 0:P], AS, ident[:, :], after=[cp] + fr(7))
                yield

            def masks(c):
                b = c % 2
                ob_ok[c] = DVE.put(vec.tensor_tensor, OHb[b],
                                   dlTb[:, c * CH:(c + 1) * CH].rearrange("p (s o) -> p s o", o=1).to_broadcast([P, CH, P]),
                                   iorowb[:, :].rearrange("p (o c) -> p o c", o=1).to_broadcast([P, CH, P]), ALU.is_equal,
                                   after=quiet + opt(oh_ok.get(c - 2)))
                yield
                ot_ok[c] = DVE.put(vec.tensor_scalar, OT[b], OT[b], iocol[:, 0:1], None, ALU.is_equal, after=[ot_in[c]])
                yield

            def widen(c):
                b = c % 2
                oh_ok[c] = AC.put(act.copy, OH[b], OHb[b], after=[ob_ok[c]] + opt(oh_free[b]) + ht_ok)

            def ends(c):
                b = c % 2
                sc = rep_free[b] = DVE.put(vec.tensor_tensor_scan, SC, rep[b], B[7][:, 0:P], -BIG, ALU.add, ALU.max,
                                           after=[tok["t"], rep_in[c]])
                tb = PE.put(ten.transpose, B[7][:, P:2 * P], SC, ident[:, :], after=[sc])
                yield
                la = laT[:, c * CH:(c + 1) * CH].rearrange("p (s o) -> p s o", o=1)
                DVE.put(vec.tensor_copy, SB[:, :, 24:25], la)
                yield
                v = free[7] = DVE.put(vec.tensor_tensor, SM, B[7][:, P:2 * P].rearrange("p (s h) -> p s h", h=8),
                                      la.to_broadcast([P, CH, 8]), ALU.mult, after=[tb])
                yield
                yield from thirds(SB, 0, 8, SM, SM, [v])
                v = tok["sb"]
                for j in range(CH):
                    tok["m"] = PE.put(ten.matmul, B[6][:, 25 * j:25 * j + 25], OHb[b][:, j, :], SB[:, j, 0:25],
                                      start=True, stop=True, after=[ob_ok[c], v] + fr(6), sig=(j == CH - 1))

            def values(c):
                pm = B[6][:, 0:25 * CH].rearrange("p (s c) -> p s c", c=25)
                v = DVE.put(vec.tensor_scalar, vp, pm[:, :, 24], -1.0, BIG, ALU.add, ALU.mult, after=[tok["m"]])
                yield
                v = DVE.put(vec.tensor_tensor, VV, pm[:, :, 0:8],
                            vp.rearrange("p (s o) -> p s o", o=1).to_broadcast([P, CH, 8]), ALU.add, after=[v])
                yield
                for k in (8, 16):
                    v = DVE.put(vec.tensor_tensor, VV, VV, pm[:, :, k:k + 8], ALU.add, after=[v])
                    yield
                free[6] = v
                mo_.load(c * CH)
                last_max[0] = DVE.put(keep_m(c * CH), after=[last_max[0]], late=True)
                yield
                for j in range(CH):
                    last_max[0] = DVE.put(max_m(c * CH + j, j), after=[last_max[0], v], late=True)
                    yield

            def tables(c):
                b = c % 2
                v = DVE.put(vec.tensor_tensor, ln_, M, tad, ALU.add, after=[last_max[0], sp_ad])
                yield
                v2 = leaky(ln_, ln_, [v])
                yield
                yield from split(ln_, 8, [v2])
                sp = tok["sp"]
                to_.load(c * CH)
                for j in range(CH):
                    n = 4 + j // 8
                    tok["e"] = PE.put(expand(c * CH + j, j, b), after=[sp, ot_ok[c]] + fr(n), sig=(j == CH - 1))
                ot_free[b] = tok["e"]
                if c:
                    v = DVE.put(old_m(c * CH), after=[sp], late=True)
                    yield
                    v = leaky(lo_, lo_, [v])
                    yield
                    v = DVE.put(drop_m(c * CH), after=[v], late=True)
                    tok["f"] = AC.put(act.activation, fc, fc, ACT.Exp, after=[v])
                    yield

            def weights_of(c):
                pe = PS[:, 4:6, 0:384].rearrange("p b (s c) -> p b s c", c=48)
                e4 = EE.rearrange("p (b s) c -> p b s c", b=2)
                g4 = G[c % NG4][:, :, MSG:ROW].rearrange("p (b s) c -> p b s c", b=2)
                v = DVE.put(vec.tensor_tensor, e4, pe[:, :, :, 0:8], g4, ALU.add, after=[tok["e"]])
                yield
                for k in (16, 32):
                    v = DVE.put(vec.tensor_tensor, e4, e4, pe[:, :, :, k:k + 8], ALU.add, after=[v])
                    yield
                v = leaky(EE, EE, [v])
                yield
                for k in (8, 24, 40):
                    v = DVE.put(vec.tensor_tensor, e4, e4, pe[:, :, :, k:k + 8], ALU.subtract, after=[v])
                    yield
                free[4] = free[5] = v
                v = DVE.put(vec.tensor_scalar, EE, EE, 0.0, None, ALU.min, after=[v])
                tok["x"] = AC.put(act.activation, EX[c % 2], EE, ACT.Exp, after=[v])
                yield

            def weigh(c):
                g = G[c % NG4]
                w_ok[c] = []
                for q in range(0, CH, 8):
                    gm = g[:, q:q + 8, 0:MSG].rearrange("p s (h c) -> p s h c", c=HW)
                    ex = EX[c % 2][:, q:q + 8, :].rearrange("p s (h o) -> p s h o", o=1).to_broadcast([P, 8, 8, HW])
                    w_ok[c].append(DVE.put(vec.tensor_tensor, gm, gm, ex, ALU.mult, after=[tok["x"]]))
                    yield

            def open_sums(c):
                ao_.load(c * CH)
                if c:
                    last_add[0] = DVE.put(rescale(c * CH), after=[tok["f"], last_add[0]], late=True)

            mms = {}

            def products(c, j0, j1):
                b = c % 2
                for j in range(j0, j1):
                    n = j % 4
                    mms[j] = PE.put(ten.matmul, B[n][:, 0:MSG], OH[b][:, j, :], G[c % NG4][:, j, 0:MSG], start=True, stop=True,
                                    after=[w_ok[c][j // 8], oh_ok[c]] + fr(n))
                    slots[c % NG4][j] = oh_free[b] = mms[j]

            def adds(c, j0, j1):
                for j in range(j0, j1):
                    n = j % 4
                    last_add[0] = free[n] = DVE.put(add_acc(c * CH + j, B[n]), after=[mms[j], last_add[0]], late=True)
                    yield

            def weave(*chains):
                chains = list(chains)
                while chains:
                    for g in list(chains):
                        if next(g, chains) is chains:
                            chains.remove(g)

            def none():
                return iter(())

            for c in range(NG4):
                gathers(c)
            fetch(0)
            fetch(1)
            for i in range(-2, NCH):
                c, n, q = i, i + 1, i + 2
                c_on, n_on, q_on = (0 <= k < NCH for k in (c, n, q))
                weave(turn_scores(q) if q_on else none(), tables(n) if n_on else none(), adds(c, 0, 4) if c_on else none())
                if n_on:
                    widen(n)
                if c_on:
                    products(c, 4, 8)
                if q_on:
                    weave(masks(q))
                weave(weights_of(n) if n_on else none(), ends(q) if q_on else none())
                if n_on:
                    weave(weigh(n))
                weave(adds(c, 4, 8) if c_on else none())
                if c_on:
                    products(c, 8, 12)
                w = values(q) if q_on else none()
                weave(w, adds(c, 8, 12)) if c_on else None
                if c_on:
                    products(c, 12, 16)
                weave(w, adds(c, 12, 16) if c_on else none())
                if n_on:
                    open_sums(n)
                    products(n, 0, 4)
                if n_on and n + 2 < NCH:
                    fetch(n + 2)
                if c_on and c + NG4 < NCH:
                    gathers(c + NG4)
            return last_add[0]

        def heads(t0, t1, dst, after):
            k = t1 - t0
            num = acc3[:, t0 * 8:t1 * 8, 0:32]
            v = DVE.put(vec.tensor_tensor, dst.rearrange("p t (h c) -> p (t h) c", c=32), num,
                        ft[:, t0 * 8:t1 * 8].rearrange("p (n o) -> p n o", o=1).to_broadcast([P, 8 * k, 32]), ALU.mult,
                        after=after)
            return DVE.put(vec.tensor_tensor, dst, dst, bb.rearrange("p (o c) -> p o c", o=1).to_broadcast([P, k, D]),
                           ALU.add, after=[v])

        def denominators(after):
            v = DVE.put(vec.tensor_scalar, ft, acc3[:, :, 32], 1e-16, None, ALU.add, after=after)
            return DVE.put(vec.reciprocal, ft, ft, after=[v])

        ad = gat(0, xt, quiet)
        den = denominators([ad])
        v = PE.last()
        for t0 in range(0, NT, 5):
            v = heads(t0, t0 + 5, O, [den, v])
            v1 = DVE.put(vec.tensor_scalar, O2, O, 0.0, None, ALU.min, after=[v])
            v1 = AC.put(act.activation, O2, O2, ACT.Exp, after=[v1])
            v = DVE.put(vec.scalar_tensor_tensor, O, O, 0.0, O2, ALU.max, ALU.add, after=[v1])
            v = DVE.put(vec.tensor_scalar, O, O, -1.0, None, ALU.add, after=[v])
            for i in range(t0, t0 + 5):
                tp, xt = transpose_into_xt(i, O[:, i - t0, :], v, [])
            v = tp
        ad = gat(1, xt, everyone() + [xt])
        den = denominators([ad])
        v = DVE.last()
        for t0 in range(0, NT, 5):
            v = heads(t0, t0 + 5, O, [den, v])
            v = DVE.put(vec.tensor_tensor, X[:, t0:t0 + 5, :], X[:, t0:t0 + 5, :], O, ALU.add, after=[v])

        xt = layernorm([v])
        quiet = everyone() + [xt]
        top[0] = base0
        s_fw = stream("d_fw")

        def load(view, src, **kw):
            return SP.dma(sync.dma_start, s_fw, view, src, after=quiet, **kw)

        sW1 = take(2 * D).rearrange("p (k c) -> p k c", k=2)
        sW2 = take(2 * P).rearrange("p (k c) -> p k c", k=2)
        sW3 = take(D)
        eW1 = take(2 * 4 * P).rearrange("p (k e c) -> p k e c", k=2, e=4)
        eW2 = take(4 * 64).rearrange("p (e c) -> p e c", e=4)
        eW3 = take(4 * D).rearrange("p (e c) -> p e c", e=4)
        gW = take(2 * 4).rearrange("p (k c) -> p k c", k=2)
        gB = take(4)
        sb1 = take(2)
        sb2 = take(1)
        eb1 = take(4)
        eb2 = take(4)
        B5 = take(D)
        z = DVE.put(vec.memset, B5[0:8, :], 0.0, after=quiet)
        load(sW1, a["L1_ffn_sW1"].rearrange("(k p) c -> p k c", p=P))
        load(sW2, a["L1_ffn_sW2"].rearrange("(k p) c -> p k c", p=P))
        load(sW3, a["L1_ffn_sW3"])
        for k in range(2):
            load(eW1[:, k], a["L1_ffn_eW1"][:, k * P:(k + 1) * P, :].rearrange("e p c -> p e c"))
        load(eW2, a["L1_ffn_eW2"].rearrange("e p c -> p e c"))
        load(eW3[0:64], a["L1_ffn_eW3"].rearrange("e p c -> p e c"))
        load(gW, a["L1_ffn_gW"].rearrange("(k p) c -> p k c", p=P))
        load(gB, a["L1_ffn_gb"].rearrange("(o c) -> o c", o=1).to_broadcast([P, 4]))
        load(sb1, a["L1_ffn_sb1"].rearrange("(k p) -> p k", p=P), allow_slow_non_contiguous=True)
        load(sb2, a["L1_ffn_sb2"].rearrange("(p o) -> p o", o=1), allow_slow_non_contiguous=True)
        load(eb1, a["L1_ffn_eb1"].rearrange("e p -> p e"), allow_slow_non_contiguous=True)
        load(eb2[0:64], a["L1_ffn_eb2"].rearrange("e p -> p e"), allow_slow_non_contiguous=True)
        SP.dma(sync.dma_start, s_fw, B5[0:4, :], a["L1_ffn_eb3"], after=[z])
        w_in = SP.dma(sync.dma_start, s_fw, B5[4:5, :], a["L1_ffn_sb3"].rearrange("(o c) -> o c", o=1))

        lg4 = take(NT * 8).rearrange("p (t r) -> p t r", t=NT)
        m8 = take(NT * 8).rearrange("p (t r) -> p t r", t=NT)
        i8 = take(NT * 8, dt=U32).rearrange("p (t r) -> p t r", t=NT)
        i8f = take(NT * 8).rearrange("p (t r) -> p t r", t=NT)
        t2_ = take(NT * 2).rearrange("p (t r) -> p t r", t=NT)
        wts = take(NT * 8).rearrange("p (t r) -> p t r", t=NT)
        wt2 = take(NT * 8).rearrange("p (t r) -> p t r", t=NT)
        wT = take(NP)
        H1 = take(2 * 2 * 512).rearrange("p (b k n) -> p b k n", b=2, k=2)
        H2 = take(2 * 512).rearrange("p (b n) -> p b n", b=2)
        E1 = take(4 * 512).rearrange("p (b n) -> p b n", b=4)
        E2 = take(8 * 512).rearrange("p (b n) -> p b n", b=8)
        for i in range(NT):
            for k in range(2):
                mm = PE.put(ten.matmul, B[0][:, i * 4:(i + 1) * 4], XT[:, k, i * P:(i + 1) * P], gW[:, k, :],
                            start=(k == 0), stop=(k == 1), after=[w_in, xt] + fr(0), sig=(k == 1))
        z = DVE.put(vec.memset, lg4, -1.0, after=quiet)
        v = free[0] = DVE.put(vec.tensor_tensor, lg4[:, :, 0:4], B[0][:, 0:NT * 4].rearrange("p (t r) -> p t r", t=NT),
                              gB.rearrange("p (o r) -> p o r", o=1).to_broadcast([P, NT, 4]), ALU.add, after=[mm, z, w_in])
        v = softmax(lg4[:, :, 0:4], 4, t2_, [v])
        v = top2(lg4, [v])
        v = DVE.put(vec.tensor_tensor, t2_[:, :, 0], m8[:, :, 1], m8[:, :, 0], ALU.subtract, after=[v])
        v = AC.put(act.activation, m8[:, :, 1], t2_[:, :, 0], ACT.Exp, after=[v])
        v = DVE.put(vec.tensor_scalar, t2_[:, :, 0], m8[:, :, 1], 1.0, None, ALU.add, after=[v])
        v = DVE.put(vec.reciprocal, m8[:, :, 0], t2_[:, :, 0], after=[v])
        v = DVE.put(vec.tensor_tensor, m8[:, :, 1], m8[:, :, 1], m8[:, :, 0], ALU.mult, after=[v])
        v = spread(m8, 8, wts, wt2, [v])
        gate = DVE.put(vec.memset, wts[:, :, 4:5], 1.0, after=[v])
        for i in range(NT):
            b = i % 2
            tp = PE.put(ten.transpose, B[b][0:8, 0:P], wts[:, i, :], ident[:, :], after=[gate] + fr(b))
            wt_ok = free[b] = AC.put(act.copy, wT[0:8, i * P:(i + 1) * P], B[b][0:8, 0:P], after=[tp] + quiet)

        h1_free, h2_free, e1_free, e2_free = [None] * 2, [None] * 2, [None] * 4, [None] * 8
        ne_ = 0
        nb = 0
        final = {}

        for tc in range(7):
            n0 = tc * 512
            nn = min(512, NP - n0)
            hb = tc % 2

            def layer(dst, parts, lhs, rhs, bias, after, width=P):
                nonlocal nb
                b = nb % 4
                nb += 1
                for k in range(parts):
                    mm = PE.put(ten.matmul, B[b][0:width, 0:nn], lhs(k), rhs(k), start=(k == 0), stop=(k == parts - 1),
                                after=[w_in] + after + fr(b), sig=(k == parts - 1))
                free[b] = AC.put(act.activation, dst, B[b][0:width, 0:nn], ACT.Relu, bias=bias, after=[mm])
                return mm, free[b]

            def xr(k):
                return XT[:, k, n0:n0 + nn]

            r = []
            for m in range(2):
                r.append(layer(H1[:, hb, m, 0:nn], 2, lambda k: sW1[:, k, m * P:(m + 1) * P], xr, sb1[:, m:m + 1],
                               opt(h1_free[hb]))[1])
            h1_free[hb], h2 = layer(H2[:, hb, 0:nn], 2, lambda k: sW2[:, k, :], lambda k: H1[:, hb, k, 0:nn], sb2[:, 0:1],
                                    r + opt(h2_free[hb]))
            e2 = []
            for e in range(4):
                _, t = layer(E1[:, e, 0:nn], 2, lambda k: eW1[:, k, e, :], xr, eb1[:, e:e + 1], opt(e1_free[e]))
                e1_free[e], t = layer(E2[0:64, hb * 4 + e, 0:nn], 1, lambda k: eW2[:, e, :], lambda k: E1[:, e, 0:nn],
                                      eb2[0:64, e:e + 1], [t] + opt(e2_free[hb * 4 + e]), width=64)
                e2.append(t)
            for q in range(nn // P):
                i = tc * 4 + q
                b = 4 + ne_ % 4
                ne_ += 1
                PE.put(ten.matmul, B[b][:, 0:D], H2[:, hb, q * P:(q + 1) * P], sW3, start=True, stop=False,
                       after=[h2, wt_ok] + fr(b), sig=False)
                mm = PE.put(ten.matmul, B[b][:, 0:D], wT[0:8, i * P:(i + 1) * P], B5[0:8, :], start=False, stop=True)
                v = free[b] = DVE.put(vec.tensor_tensor, X[:, i, :], X[:, i, :], B[b][:, 0:D], ALU.add, after=[mm])
                h2_free[hb] = mm
                for e in range(4):
                    b = 4 + ne_ % 4
                    ne_ += 1
                    mm = PE.put(ten.matmul, B[b][:, 0:D], E2[0:64, hb * 4 + e, q * P:(q + 1) * P], eW3[0:64, e, :],
                                start=True, stop=True, after=[e2[e]] + fr(b))
                    e2_free[hb * 4 + e] = mm
                    v = free[b] = DVE.put(vec.scalar_tensor_tensor, X[:, i, :], B[b][:, 0:D], wts[:, i, e:e + 1],
                                          X[:, i, :], ALU.mult, ALU.add, after=[mm, v])
            k = nn // P
            if tc < 6:
                SP.dma(sync.dma_start, s_out, out[n0:n0 + nn, :].rearrange("(t p) d -> p t d", p=P),
                       X[:, tc * 4:tc * 4 + 4, :], after=[v])
            else:
                SP.dma(sync.dma_start, s_out, out[n0:N, :], X[0:N - n0, NT - 1, :], after=[v])

        block = ctx.enter_context(nc.Block())

        @block.sync
        def _(eng):
            SP.play(eng)
            eng.wait_ge(s_out.sem, s_out.n)

        @block.gpsimd
        def _(eng):
            PL.play(eng)

        @block.scalar
        def _(eng):
            AC.play(eng)

        @block.tensor
        def _(eng):
            PE.play(eng)

        @block.vector
        def _(eng):
            DVE.play(eng)


_INS = ['x', 'src', 'dst', 'edge_type_16', 'edge_weight1', 'L0_gnn_weight', 'L0_ffn_gate_w', 'L0_ffn_gate_b',
        'L0_ffn_w1', 'L0_ffn_w2', 'L0_ffn_w3', 'L1_gnn_W1', 'L1_gnn_a_src1', 'L1_gnn_a_dst1', 'L1_gnn_b1',
        'L1_gnn_W2', 'L1_gnn_a_src2', 'L1_gnn_a_dst2', 'L1_gnn_b2', 'L1_ffn_sW1', 'L1_ffn_sb1', 'L1_ffn_sW2',
        'L1_ffn_sb2', 'L1_ffn_sW3', 'L1_ffn_sb3', 'L1_ffn_eW1', 'L1_ffn_eb1', 'L1_ffn_eW2', 'L1_ffn_eb2',
        'L1_ffn_eW3', 'L1_ffn_eb3', 'L1_ffn_gW', 'L1_ffn_gb']


def kernel(**inputs):
    import numpy as _np
    import concourse.bacc as _bacc
    from concourse.bass_utils import run_bass_kernel_spmd as _run

    nc = _bacc.Bacc("TRN2", target_bir_lowering=False, num_devices=1)
    arrays, aps = {}, {}
    for name in _INS:
        v = _np.ascontiguousarray(inputs[name])
        arrays[f"in_{name}_dram"] = v
        aps[name] = nc.dram_tensor(f"in_{name}_dram", v.shape, mybir.dt.from_np(v.dtype), kind="ExternalInput").ap()
    out = nc.dram_tensor("out_0_dram", (N, D), F32, kind="ExternalOutput").ap()
    build(nc, aps, out)
    r = _run(nc, [arrays], core_ids=[0])
    return r.results[0]["out_0_dram"]
```

```python
from contextlib import ExitStack
from itertools import islice

import concourse.bass as bass
from concourse import mybir

F32 = mybir.dt.float32
BF16 = mybir.dt.bfloat16
F32R = mybir.dt.float32r
I32 = mybir.dt.int32
U32 = mybir.dt.uint32
ALU = mybir.AluOpType
ACT = mybir.ActivationFunctionType
AX = mybir.AxisListType.X

P = 128
N = 3125
NT = 25
NP = NT * P
E = 50000
EW = 2 * P
ET = 196
S = 224
NS = NT + 1
SU = ET + NT
D = 256
R = 16
BIG = 1.0e30
CH = 8
CC = 2 * CH
NG4 = 4
NCH = S // CH
HW = 33
MSG = 8 * HW
ROW = MSG + 8
HID = 512
MT = (2 * NP + R * (P - 1)) // P


class Engine:

    def __init__(self, sem):
        self.sem = sem
        self.n = 0
        self.ops = []

    def put(self, fn, *args, after=(), sig=True, late=False, **kw):
        if sig:
            self.n += 1
        self.ops.append((fn, args, kw, tuple(after), (self.sem, 1) if sig else None, late))
        return (self.sem, self.n)

    def dma(self, fn, stream, *args, after=(), **kw):
        stream.n += 16
        self.ops.append((fn, args, kw, tuple(after), (stream.sem, 16), False))
        return (stream.sem, stream.n)

    def last(self):
        return (self.sem, self.n)

    def branch(self, part, flag, after):
        self.ops.append((None, (part, flag), {}, tuple(after), None, False))

    def play(self, eng):
        seen = {}
        for fn, args, kw, after, inc, late in self.ops:
            need = {}
            for sem, v in after:
                if v > seen.get(id(sem), 0):
                    need[id(sem)] = (sem, v)
                    seen[id(sem)] = v
            need = list(need.values())
            own = need.pop() if late and need else None
            for sem, v in need:
                eng.wait_ge(sem, v)
            if fn is None:
                part, flag = args
                reg = eng.alloc_register("unsorted")
                eng.load([reg], flag)
                with eng.If_ne(reg, 0):
                    part.play(eng)
                continue
            ins = fn(*args, **kw)
            if own is not None:
                ins.wait_op(*own, "sem-ge")
            if inc is not None:
                ins.then_inc(*inc)


class Stream:

    def __init__(self, sem):
        self.sem = sem
        self.n = 0

    def done(self):
        return (self.sem, self.n)


def build(nc, a, out):
    with ExitStack() as ctx:
        def sb(name, shape, dt=F32):
            return ctx.enter_context(nc.sbuf_tensor(name, shape, dt))

        def stream(name):
            return Stream(ctx.enter_context(nc.semaphore(name)))

        PE, DVE, AC, PL, SP = (Engine(ctx.enter_context(nc.semaphore("s_" + n)))
                               for n in ("pe", "dve", "act", "pool", "sp"))
        vec, act, ten, pool, sync = nc.vector, nc.scalar, nc.tensor, nc.gpsimd, nc.sync
        PS = ctx.enter_context(nc.psum_tensor("banks", [P, 8, 512], F32))
        B = [PS[:, i, :] for i in range(8)]

        XG = nc.dram_tensor("xg", [MT * P, D], F32, kind="Internal").ap()
        YG = nc.dram_tensor("yg", [MT * P, D], F32, kind="Internal").ap()
        TR = nc.dram_tensor("tr", [NP * R, D], F32, kind="Internal").ap()
        HT = [nc.dram_tensor(f"ht{i}", [NP, ROW], F32, kind="Internal").ap() for i in range(2)]
        SE = {k: nc.dram_tensor("se_" + k, [ET, EW], F32 if k == "nrm" else I32, kind="Internal").ap()
              for k in ("src", "dst", "rel", "nrm")}
        RD = nc.dram_tensor("rd", [S, EW], F32, kind="Internal").ap()
        DLD = nc.dram_tensor("dld", [S, EW], BF16, kind="Internal").ap()

        X = sb("X", [P, NS, D])
        XT = sb("XT", [P, 2, NP])
        ident = sb("ident", [P, P])
        iorow = sb("iorow", [P, P])
        iocol = sb("iocol", [P, 1])
        iorowb = sb("iorowb", [P, P], BF16)
        onec = sb("onec", [P, 1])
        epsc = sb("epsc", [P, 1])
        ioi = sb("ioi", [P, P], I32)
        idx1T = sb("idx1T", [P, 512], I32)
        srcT = sb("srcT", [P, 512], I32)
        nrmT = sb("nrmT", [P, 512])
        dlT = sb("dlT", [P, 512])
        laT = sb("laT", [P, 512])
        doff = {m: sb(f"doff{m}", [1, S], I32) for m in (8, 48, D, MSG)}
        bns = sb("bns", [P, 10, 6])
        mv = sb("mv", [P, NT, 2])
        rstd = sb("rstd", [P, NT])
        xn = sb("xn", [P, 4, D])
        ARENA = 34050
        PARTS = 2 * 2 * R * D + 4 * 2 * P
        with nc.sbuf_tensor("parts", [P, PARTS], F32R) as parts:
            pass
        arena = sb("arena", [P, ARENA])
        top = [0]

        def take(n, shape=None, dt=F32):
            v = arena[:, top[0]:top[0] + n]
            top[0] += n
            assert top[0] <= ARENA, top[0]
            return v if dt == F32 else v.bitcast(dt)

        s_out = stream("d_out")

        def everyone():
            return [q.last() for q in (PE, DVE, AC, PL, SP)]

        c0 = PL.put(pool.memset, ident[:, :], 0.0)
        c1 = PL.put(pool.affine_select, out=ident[:, :], in_=ident[:, :], compare_op=ALU.not_equal, fill=1.0,
                    base=0, pattern=[[-1, P]], channel_multiplier=1, after=[c0])
        c2 = PL.put(pool.iota, ioi[:, :], [[1, P]], base=0, channel_multiplier=0)
        k1 = DVE.put(vec.tensor_copy, iorow[:, :], ioi[:, :], after=[c2])
        c3 = PL.put(pool.iota, ioi[:, 0:1], [[0, 1]], base=0, channel_multiplier=1, after=[k1])
        k2 = DVE.put(vec.tensor_copy, iocol[:, :], ioi[:, 0:1], after=[c3])
        c4 = PL.put(pool.iota, ioi[:, 0:4], [[P, 4]], base=0, channel_multiplier=1, after=[k2])
        DVE.put(vec.tensor_copy, iorowb[:, :], iorow[:, :], after=[k1])
        k3 = DVE.put(vec.memset, epsc[:, :], 1e-5)
        DVE.put(vec.memset, onec[:, :], 1.0)
        xz = DVE.put(vec.memset, X[:, NT - 1:NS, :], 0.0)
        const = [c1, k1, k2, k3]

        GT = 5
        s_xin = [stream(f"d_x{i}") for i in range(NT // GT)]
        x_in = {}
        for t0 in range(0, NT, GT):
            t1 = min(t0 + GT, NT - 1)
            x_in[t0] = SP.dma(sync.dma_start, s_xin[t0 // GT], X[:, t0:t1, :],
                              a["x"][t0 * P:t1 * P, :].rearrange("(t p) d -> p t d", p=P))
        x_in[NT - GT] = SP.dma(sync.dma_start, s_xin[-1], X[0:N - (NT - 1) * P, NT - 1, :], a["x"][(NT - 1) * P:N, :],
                               after=[xz])

        free = [None] * 8

        def fr(b):
            return [free[b]] if free[b] else []

        def opt(t):
            return [t] if t else []

        def transpose_into_xt(i, src, ready, reuse, bias=None):
            b = 5 + i % 3
            PE.put(ten.transpose, B[b][:, 0:P], src[:, 0:P], ident[:, :], after=[ready] + fr(b) + const, sig=False)
            t = PE.put(ten.transpose, B[b][:, P:2 * P], src[:, P:2 * P], ident[:, :])
            dst, got = XT[:, :, i * P:(i + 1) * P], B[b][:, 0:2 * P].rearrange("p (k c) -> p k c", k=2)
            if bias is None:
                free[b] = AC.put(act.copy, dst, got, after=[t] + reuse)
            else:
                free[b] = AC.put(act.activation, dst, got, ACT.Identity, bias=bias, after=[t] + reuse)
            return t, free[b]

        xn_free = [None] * 4
        bn_free = [None] * 10

        def moments(t0, t1, after):
            st = {}
            for i in range(t0, t1):
                st[i] = DVE.put(vec.bn_stats, bns[:, i % 10, :], X[:, i, :], after=after + opt(bn_free[i % 10]))
            for i in range(t0, t1):
                ag = bn_free[i % 10] = DVE.put(vec.bn_aggr, mv[:, i, :], bns[:, i % 10, :], after=[st[i]])
            return AC.put(act.activation, rstd[:, t0:t1], mv[:, t0:t1, 1], ACT.Sqrt, bias=epsc[:, 0:1], after=[ag] + const)

        def layernorm(before, keep=None, then=None):
            reuse = [PE.last()]
            done, sq = {}, {}
            for t0 in range(0, NT + GT, GT):
                if t0 < NT:
                    sq[t0] = moments(t0, t0 + GT, before(t0))
                if t0 == 0:
                    continue
                rc = DVE.put(vec.reciprocal, rstd[:, t0 - GT:t0], rstd[:, t0 - GT:t0], after=[sq[t0 - GT]])
                for i in range(t0 - GT, t0):
                    w = [t for t in [xn_free[i % 4]] if t and keep is None]
                    dst = xn[:, i % 4, :] if keep is None else keep[:, i, :]
                    n = DVE.put(vec.tensor_scalar, dst, X[:, i, :], mv[:, i, 0:1], rstd[:, i:i + 1],
                                ALU.subtract, ALU.mult, after=[rc] + w)
                    tp, done[i] = transpose_into_xt(i, dst, n, reuse)
                    if keep is None:
                        xn_free[i % 4] = tp
                    if then and i > 1:
                        then(i - 2, done[i - 2])
            if then:
                for i in (NT - 2, NT - 1):
                    then(i, done[i])
            return done

        xt = layernorm(lambda t0: [x_in[t0]])

        base0 = top[0]
        take(PARTS)
        n = 2 * R * D
        whi, wlo = (parts[:, i * n:(i + 1) * n].rearrange("p (k r d) -> p k r d", k=2, r=R) for i in range(2))
        n = 2 * n
        xhi, xlo = ([parts[:, n + (2 * i + c) * 2 * P:n + (2 * i + c + 1) * 2 * P].rearrange("p (k c) -> p k c", k=2)
                     for c in range(2)] for i in range(2))
        padi = take(2 * EW, dt=I32)
        padf = take(EW)
        onesw = take(448)
        ones = take(P)
        upper = take(P)
        flagf = take(2)
        flagi = take(1, dt=I32)
        base_sort = top[0]
        stage = take(2 * R * D).rearrange("p (b n) -> p b n", b=2)
        wraw = stage.rearrange("p b n -> p (b n)").rearrange("p (k r d) -> p k r d", k=2, r=R)
        s_w = [stream(f"d_w{i}") for i in range(4)]
        s_tr = [stream(f"d_tr{i}") for i in range(2)]
        w_in = {}
        for g in range(4):
            q = slice(4 * g, 4 * g + 4)
            for k in range(2):
                ld = SP.dma(sync.dma_start, s_w[g], wraw[:, k, q, :],
                            a["L0_gnn_weight"][q, k * P:(k + 1) * P, :].rearrange("r p d -> p r d"))
            h = AC.put(act.copy, whi[:, :, q, :], wraw[:, :, q, :], after=[ld])
            Q, e = (PL, pool) if g == 2 else (DVE, vec)
            w_in[g] = Q.put(e.tensor_tensor, wlo[:, :, q, :], wraw[:, :, q, :], whi[:, :, q, :].bitcast(F32), ALU.subtract,
                             after=[h])
        names = ("src", "dst", "rel", "nrm")
        inputs = {"src": a["src"], "dst": a["dst"], "rel": a["edge_type_16"],
                  "nrm": a["edge_weight1"].rearrange("e o -> (e o)")}
        full = (ET - 1) * EW
        rest = E - full
        s_cp = stream("d_cp")
        pz = [DVE.put(vec.memset, padi[0:1, 0:EW], 0), DVE.put(vec.memset, padi[0:1, EW:2 * EW], 1000000),
              DVE.put(vec.memset, padf[0:1, :], 0.0)]
        for k in names:
            PL.dma(pool.dma_start, s_cp, SE[k][0:ET - 1, :], inputs[k][0:full].rearrange("(t c) -> t c", c=EW))
            PL.dma(pool.dma_start, s_cp, SE[k][ET - 1:ET, 0:rest], inputs[k][full:E].rearrange("(t c) -> t c", t=1))
            pad = {"src": padi[0:1, 0:EW - rest], "rel": padi[0:1, 0:EW - rest],
                   "dst": padi[0:1, EW:2 * EW - rest], "nrm": padf[0:1, 0:EW - rest]}[k]
            PL.dma(pool.dma_start, s_cp, SE[k][ET - 1:ET, rest:EW], pad, after=pz)
        edges = s_cp.done()
        DVE.put(vec.memset, onesw, 1.0)

        base1 = top[0]
        RW, RL = 125, 400
        ahead = [take(RL, dt=I32)[0:RW] for _ in range(2)]
        worse = take(RL)[0:RW]
        s_ch = stream("d_ch")
        SP.dma(sync.dma_start, s_ch, ahead[0], a["dst"].rearrange("(p j) -> p j", j=RL))
        SP.dma(sync.dma_start, s_ch, ahead[1][0:RW - 1, :], a["dst"][1:E - RL + 1].rearrange("(p j) -> p j", j=RL))
        z = SP.dma(sync.dma_start, s_ch, ahead[1][RW - 1:RW, 0:RL - 1], a["dst"][E - RL + 1:E].rearrange("(p j) -> p j", p=1))
        z = SP.dma(sync.dma_start, s_ch, ahead[1][RW - 1:RW, RL - 1:RL], a["dst"][E - 1:E].rearrange("(p j) -> p j", p=1))
        o1 = DVE.put(vec.memset, ones, 1.0)
        u0 = PL.put(pool.memset, upper, 1.0)
        u0 = PL.put(pool.affine_select, out=upper, in_=upper, compare_op=ALU.is_gt, fill=0.0, base=0,
                    pattern=[[1, P]], channel_multiplier=-1, after=[u0])
        v = DVE.put(vec.tensor_tensor, worse, ahead[0], ahead[1], ALU.is_gt, after=[z])
        worse_ok = DVE.put(vec.tensor_reduce, flagf[0:RW, 0:1], worse, AX, ALU.max, after=[v])
        top[0] = base1

        def sort_edges():
            top[0] = base_sort
            VB = 3136
            bPE, bDV, bPL = (Engine(ctx.enter_context(nc.semaphore("b_" + n))) for n in ("pe", "dve", "pool"))
            s_in, s_rec, s_back, s_se = (stream("d_b" + n) for n in ("in", "rec", "back", "se"))
            REC = nc.dram_tensor("rec", [RW * RL, 4], I32, kind="Internal").ap()
            V, H, cur, got = (take(VB) for _ in range(4))
            Vi = got.bitcast(I32)
            raw = {k: take(RL, dt=(F32 if k == "nrm" else I32))[0:RW] for k in names}
            Kf, pf = take(RL)[0:RW], take(RL)[0:RW]
            pi = pf.bitcast(I32)
            carry = take(2)
            recv = {k: (H if k == "nrm" else H.bitcast(I32))[0:RW, 0:4 * RL].rearrange("p (j k) -> p j k", k=4) for k in names}
            rec = recv["dst"]
            for k in names:
                ld = bPL.dma(pool.dma_start, s_in, raw[k], inputs[k].rearrange("(p j) -> p j", j=RL))
            io = bPL.put(pool.iota, Vi, [[1, VB]], base=0, channel_multiplier=0)
            kf = bDV.put(vec.tensor_copy, Kf, raw["dst"], after=[ld])
            vf = bDV.put(vec.tensor_copy, V, Vi, after=[io])
            h = bDV.put(vec.memset, H, 0.0)
            for j in range(RL):
                h = bDV.put(vec.scalar_tensor_tensor, H[0:RW], V[0:RW], Kf[:, j:j + 1], H[0:RW], ALU.is_equal, ALU.add,
                            after=[h, vf, kf])
            cy = bDV.put(vec.memset, carry, 0.0)
            used = None
            for c in range(0, VB, 448):
                w = [h, used] if used else [h]
                bPE.put(ten.matmul, B[6][:, 0:448], ones, H[:, c:c + 448], start=True, stop=True, after=w)
                mm = bPE.put(ten.matmul, B[7][:, 0:448], upper, H[:, c:c + 448], start=True, stop=True)
                x = cur[:, c:c + 448]
                v = bDV.put(vec.tensor_copy, got[:, 0:448], B[6][:, 0:448], after=[mm])
                v = bDV.put(vec.tensor_tensor_scan, x, onesw, got[:, 0:448], 0.0, ALU.mult, ALU.add, after=[v])
                v = bDV.put(vec.tensor_scalar, x, x, carry[:, 0:1], None, ALU.add, after=[v, cy])
                cy = bDV.put(vec.tensor_copy, carry[:, 0:1], x[:, 447:448], after=[v])
                v = bDV.put(vec.tensor_tensor, x, x, got[:, 0:448], ALU.subtract, after=[cy])
                used = bDV.put(vec.tensor_tensor, x, x, B[7][:, 0:448], ALU.add, after=[v])
            v = used
            for j in range(RL):
                u = bDV.put(vec.scalar_tensor_tensor, got[0:RW], V[0:RW], Kf[:, j:j + 1], cur[0:RW], ALU.is_equal, ALU.mult,
                            after=[v])
                v = bDV.put(vec.tensor_reduce, pf[:, j:j + 1], got[0:RW], AX, ALU.add, after=[u])
                v = bDV.put(vec.scalar_tensor_tensor, cur[0:RW], V[0:RW], Kf[:, j:j + 1], cur[0:RW], ALU.is_equal, ALU.add,
                            after=[v])
            pos = bDV.put(vec.tensor_copy, pi, pf, after=[v])
            for n, k in enumerate(names):
                v = bDV.put(vec.tensor_copy, recv[k][:, :, n], raw[k], after=[pos])
            for j in range(RL):
                r = bPL.dma(pool.indirect_dma_start, s_rec, REC, bass.IndirectOffsetOnAxis(ap=pi[:, j:j + 1], axis=0),
                            rec[:, j, :], None, after=[v, edges])
            r = bPL.dma(pool.dma_start, s_back, rec.rearrange("p j k -> p (j k)"),
                        REC.rearrange("(p j) k -> p (j k)", j=RL), after=[r])
            for n, k in enumerate(names):
                v = bDV.put(vec.tensor_copy, raw[k], recv[k][:, :, n], after=[r])
            for k in names:
                r = bPL.dma(pool.dma_start, s_se, SE[k].rearrange("t c -> (t c)")[0:E].rearrange("(p j) -> p j", j=RL), raw[k],
                            after=[v])
            bPL.put(pool.memset, flagf[:, 1:2], 0.0, after=[r])
            top[0] = base1
            return bPE, bDV, bPL

        tab = {}

        def edge_tables():
            mm = PE.put(ten.matmul, B[7][0:1, 0:1], flagf[0:RW, 0:1], ones[0:RW, 0:1], start=True, stop=True,
                        after=[worse_ok, o1] + fr(7))
            flag = free[7] = DVE.put(vec.tensor_copy, flagi[0:1, :], B[7][0:1, 0:1], after=[mm])
            yield
            bPE, bDV, bPL = sort_edges()
            rest = [flag] + [st for st in st_free if st]
            PE.branch(bPE, flagi[0:1, 0:1], after=rest + [u0, o1] + fr(6) + fr(7))
            DVE.branch(bDV, flagi[0:1, 0:1], after=rest)
            PL.branch(bPL, flagi[0:1, 0:1], after=rest)
            fi = take(2, dt=I32)
            ff = take(2)
            sio = take(2)
            thr = take(2)
            cnt = take(2)
            tf = take(2)
            ti = take(2, dt=I32)
            df = take(2)
            d128 = take(2)
            drow = take(EW)
            diag = take(2 * P).rearrange("p (g c) -> p g c", g=2)
            junk = take(EW)
            s_f = stream("d_f")
            z = DVE.put(vec.memset, fi, 1000000)
            PL.dma(pool.dma_start, s_f, fi[:, 0:1], SE["dst"][0:P, 0:1], after=[edges, z], allow_slow_non_contiguous=True)
            f_in = PL.dma(pool.dma_start, s_f, fi[0:ET - P, 1:2], SE["dst"][P:ET, 0:1], allow_slow_non_contiguous=True)
            v = DVE.put(vec.tensor_copy, sio, ioi[:, 0:2], after=[c4])
            t1 = DVE.put(vec.tensor_scalar, thr, sio, float(P), float(P), ALU.mult, ALU.add, after=[v])
            f1 = DVE.put(vec.tensor_copy, ff, fi, after=[f_in])
            f2 = DVE.put(vec.scalar_tensor_tensor, ff, sio, float(P), ff, ALU.mult, ALU.add, after=[f1])
            q = None
            for g in range(2):
                q = DVE.put(vec.tensor_scalar, diag[:, g, :], ident[:, :], ff[:, g:g + 1], None, ALU.mult, after=[f2] + const)
            yield
            for g in range(2):
                mm = PE.put(ten.matmul, B[6][:, g * P:(g + 1) * P], ones, diag[:, g, :], start=True, stop=True,
                            after=[q, o1] + fr(6))
            ct = None
            for g in range(2):
                w = [ct] if ct else []
                ct = DVE.put(vec.tensor_scalar, junk[:, 0:ET], B[6][:, 0:ET], thr[:, g:g + 1], None, ALU.is_lt, ALU.add,
                             accum_out=cnt[:, g:g + 1], after=[mm, t1] + w)
            free[6] = ct
            u = DVE.put(vec.tensor_scalar, tf, cnt, -1.0, 0.0, ALU.add, ALU.max, after=[ct])
            ti_ok = DVE.put(vec.tensor_copy, ti, tf, after=[u])
            u = DVE.put(vec.tensor_tensor, df, sio, tf, ALU.subtract, after=[u])
            u = DVE.put(vec.tensor_scalar, df, df, float(NT), None, ALU.min, after=[u])
            d_ok = DVE.put(vec.tensor_scalar, d128, df, float(P), None, ALU.mult, after=[u])
            yield
            for g in range(2):
                mm = PE.put(ten.matmul, B[7][0:1, g * P:(g + 1) * P], df[:, g:g + 1], ident[:, :], start=True, stop=True,
                            after=[d_ok] + fr(7))
            u = DVE.put(vec.tensor_copy, drow[0:1, :], B[7][0:1, 0:EW], after=[mm])
            free[7] = u
            for m in doff:
                tab["offs"] = DVE.put(vec.tensor_scalar, doff[m][:, :], drow[0:1, 0:S], float(m), None, ALU.mult, after=[u])

            rows = {k: take(512, dt=(F32 if k == "nrm" else I32)).rearrange("p (g c) -> p g c", g=2) for k in names}
            s_rw = stream("d_rw")
            zr = None
            for k in names:
                zr = DVE.put(vec.memset, rows[k][:, 1, :], 0.0 if k == "nrm" else 0)
            for k in names:
                for g in range(2):
                    m = P if g == 0 else S - P
                    PL.dma(pool.indirect_dma_start, s_rw, rows[k][0:m, g, :], None, SE[k],
                           bass.IndirectOffsetOnAxis(ap=ti[0:m, g:g + 1], axis=0), after=[ti_ok, edges, zr])
            got = s_rw.done()
            i1 = take(512).rearrange("p (g c) -> p g c", g=2)
            sf = take(512).rearrange("p (g c) -> p g c", g=2)
            dl = take(512).rearrange("p (g c) -> p g c", g=2)
            dlb = take(256, dt=BF16).rearrange("p (g c) -> p g c", g=2)
            ne = take(2 * (EW + 1)).rearrange("p (g c) -> p g c", g=2)
            rr = take(512).rearrange("p (g c) -> p g c", g=2)
            q1 = DVE.put(vec.scalar_tensor_tensor, i1, rows["src"], float(R), rows["rel"], ALU.mult, ALU.add, after=[got])
            q2 = DVE.put(vec.tensor_copy, sf, rows["src"])
            for g in range(2):
                q3 = DVE.put(vec.tensor_scalar, dl[:, g, :], rows["dst"][:, g, :], d128[:, g:g + 1], None, ALU.subtract,
                             after=[d_ok])
            q4 = DVE.put(vec.tensor_copy, dlb, dl, after=[q3])
            DVE.put(vec.memset, ne[:, :, 0:1], 1.0)
            DVE.put(vec.memset, ne[:, :, EW:EW + 1], 1.0)
            q5 = DVE.put(vec.tensor_tensor, ne[:, :, 1:EW], dl[:, :, 1:EW], dl[:, :, 0:EW - 1], ALU.not_equal)
            q6 = DVE.put(vec.tensor_scalar, rr, ne[:, :, 0:EW], -BIG, None, ALU.mult, after=[q5])
            tabs = [(i1, idx1T, q1), (sf, srcT, q2), (rows["nrm"], nrmT, got), (dl, dlT, q3), (ne[:, :, 1:EW + 1], laT, q5)]
            yield
            yield
            for n, (src, dst, ok) in enumerate(tabs):
                b = 6 + n % 2
                for g in range(4):
                    mm = PE.put(ten.transpose, B[b][:, g * P:(g + 1) * P], src[:, g // 2, g % 2 * P:(g % 2 + 1) * P], ident[:, :],
                                after=[ok] + fr(b) + const)
                tab[n] = free[b] = DVE.put(vec.tensor_copy, dst[:, :].rearrange("p (g s a) -> p g a s", g=2, a=2),
                                           B[b].rearrange("p (g a s) -> p g a s", g=2, a=2), after=[mm])
            s_dl = stream("d_dl")
            for src, dst, ok in ((rr, RD, q6), (dlb, DLD, q4)):
                SP.dma(sync.dma_start, s_dl, dst[0:P, :], src[:, 0, :], after=[ok])
                SP.dma(sync.dma_start, s_dl, dst[P:S, :], src[0:S - P, 1, :])
            tab["steps"] = s_dl.done()

        work = edge_tables()
        st_free = [None] * 2
        x_free = [None] * 2
        tr_rows = TR.rearrange("(n r) d -> n (r d)", r=R)
        for i in range(NT):
            c = i % 2
            xs = XT[:, :, i * P:(i + 1) * P]
            h = DVE.put(vec.tensor_copy, xhi[c], xs, after=[xt[i]] + opt(x_free[c]))
            lo = DVE.put(vec.tensor_tensor, xlo[c], xs, xhi[c].bitcast(F32), ALU.subtract, after=[h])
            for j in range(8):
                b = j % 6
                terms = [(x, k, w) for x, w in ((xhi, whi), (xhi, wlo), (xlo, whi)) for k in range(2)]
                for n, (x, k, w) in enumerate(terms):
                    mm = PE.put(ten.matmul, B[b][:, :], x[c][:, k, :], w[:, k, 2 * j:2 * j + 2, :].rearrange("p r d -> p (r d)"),
                                start=(n == 0), stop=(n == 5), after=[lo, w_in[j // 2]] + fr(b), sig=(n == 5))
                x_free[c] = mm
                w = [w_in[2], w_in[3]] + opt(st_free[i % 2])
                free[b] = AC.put(act.copy, stage[:, i % 2, j * 512:(j + 1) * 512], B[b][:, :], after=[mm] + w)
                if j % 4 == 3:
                    h = j // 4 * 8 * D
                    st = SP.dma(sync.dma_start, s_tr[i % 2], tr_rows[i * P:(i + 1) * P, h:h + 8 * D],
                                stage[:, i % 2, h:h + 8 * D], after=[free[b]])
            st_free[i % 2] = st
            if i > 1:
                next(work, None)
        for _ in work:
            pass
        tr_done = list(st_free)

        def reg_bank(eng, name):
            return [[eng.alloc_register(f"{name}{k}_{i}") for i in range(CH)] for k in range(2)]

        class Offsets:

            def __init__(self, queue, eng, mult, most):
                self.q, self.eng, self.mult, self.most = queue, eng, mult, most

            def load(self, s0, after=()):
                bank = regs[self.q, self.mult if self.mult in (8, 48) else 0][(s0 // CH) % 2]
                self.q.put(self.eng.load, bank, doff[self.mult][0:1, s0:s0 + CH], sig=False, after=after)

            def at(self, s):
                r = regs[self.q, self.mult if self.mult in (8, 48) else 0][(s // CH) % 2][s % CH]
                return self.eng.snap(r, min_val=0, max_val=self.most)

        regs = {k: reg_bank(e, n) for k, e, n in (((DVE, 0), vec, "rv"), ((DVE, 8), vec, "rm"), ((DVE, 48), vec, "rt"),
                                                  ((PE, 48), ten, "rp"))}

        tr_mm = x_free[(NT - 1) % 2]
        top[0] = base0
        NG = 6
        Gr = take(NG * 2 * D).rearrange("p (n a d) -> p n a d", n=NG, a=2)
        zer = take(D)
        s_zg = stream("d_zg")
        z = DVE.put(vec.memset, zer, 0.0, after=[tr_mm])
        OHr = take(NG * 2 * P).rearrange("p (n a d) -> p n a d", n=NG, a=2)
        s_g = [stream(f"d_g{i}") for i in range(NG)]
        xf = X[:, :, :].rearrange("p t d -> p (t d)")
        xo = Offsets(DVE, vec, D, (NS - 1) * D)
        mmt = [None] * NG
        gts = {}
        last_add = [DVE.last()]
        ready = [tab[0], tab[2], tab[3], tr_mm] + tr_done

        def add_x(s, bank):
            def go():
                o = xf[:, bass.ds(xo.at(s), D)]
                return vec.tensor_tensor(o, o, bank[:, 0:D], ALU.add)
            return go

        LAG = 3
        for s in range(SU + LAG):
            if s < SU:
                n = s % NG
                w = [mmt[n]] if mmt[n] else []
                got = []
                for h in range(2):
                    q = 2 * s + h
                    g = PL.dma(pool.indirect_dma_start, s_g[n], Gr[:, n, h, :], None, TR,
                               bass.IndirectOffsetOnAxis(ap=idx1T[:, q:q + 1], axis=0), after=ready + w)
                    oh = DVE.put(vec.tensor_scalar, OHr[:, n, h, :], iorow[:, :], dlT[:, q:q + 1], nrmT[:, q:q + 1],
                                 ALU.is_equal, ALU.mult, after=w + [tab[2], tab[3]])
                    got += [g, oh]
                for h in range(2):
                    mm = PE.put(ten.matmul, B[n][:, 0:D], OHr[:, n, h, :], Gr[:, n, h, :], start=(h == 0), stop=(h == 1),
                                after=got + fr(n), sig=(h == 1))
                mmt[n] = gts[s] = mm
                if s % 13 == 12 and s // 13 < MT // 5:
                    j = s // 13 * 5
                    zg = SP.dma(sync.dma_start, s_zg, XG[j * P:(j + 5) * P, :].rearrange("(t p) d -> p t d", p=P),
                                zer.rearrange("p (o d) -> p o d", o=1).to_broadcast([P, 5, D]), after=[z, mm])
            if s >= LAG:
                q = s - LAG
                if q % CH == 0:
                    xo.load(q, after=[tab["offs"]])
                n = q % NG
                last_add[0] = free[n] = DVE.put(add_x(q, B[n]), after=[gts[q], last_add[0]], late=True)
        x1 = last_add[0]

        quiet = everyone() + [x1, zg]
        top[0] = LATER = ARENA - 5600
        wx2 = [take(2 * 272).rearrange("p (k c) -> p k c", k=2) for _ in range(2)]
        bb2 = [take(D) for _ in range(2)]
        tad = take((NS + CH) * 8)
        sW1 = take(2 * D).rearrange("p (k c) -> p k c", k=2)
        sW2 = take(2 * P).rearrange("p (k c) -> p k c", k=2)
        sW3 = take(D)
        eW1 = take(2 * 4 * P).rearrange("p (k e c) -> p k e c", k=2, e=4)
        eW2 = take(4 * 64).rearrange("p (e c) -> p e c", e=4)
        eW3 = take(4 * D).rearrange("p (e c) -> p e c", e=4)
        gW = take(2 * 4).rearrange("p (k c) -> p k c", k=2)
        gB = take(4)
        sb1 = take(2)
        sb2 = take(1)
        eb1 = take(4)
        eb2 = take(4)
        B5 = take(D)

        top[0] = base0
        YB = [take(2 * D).rearrange("p (k d) -> p k d", k=2) for _ in range(4)]
        m8 = take(NT * 8).rearrange("p (t r) -> p t r", t=NT)
        posi = take(2 * NT, dt=I32).rearrange("p (k t) -> p k t", k=2)
        avb2 = [take(2 * D).rearrange("p (s c) -> p s c", s=2) for _ in range(2)]
        wtmp = take(D)
        n, m = top[0], 2 * HID
        w3h, w3l = ([parts[:, n + (2 * i + c) * m:n + (2 * i + c + 1) * m].rearrange("p (k d) -> p k d", k=4)
                     for c in range(2)] for i in range(2))
        n += 4 * m
        hidh, hidl = ([parts[:, n + (2 * i + c) * HID:n + (2 * i + c + 1) * HID] for c in range(2)] for i in range(2))
        XN = take(NT * D).rearrange("p (t d) -> p t d", t=NT)
        assert n + 4 * HID <= top[0] <= PARTS
        gw = take(2 * R).rearrange("p (k r) -> p k r", k=2)
        gbb = take(R)
        s_gw = stream("d_gw")
        SP.dma(sync.dma_start, s_gw, gw, a["L0_ffn_gate_w"].rearrange("(k p) r -> p k r", p=P), after=quiet)
        gw_in = SP.dma(sync.dma_start, s_gw, gbb, a["L0_ffn_gate_b"].rearrange("(o r) -> o r", o=1).to_broadcast([P, R]))
        lg = take(NT * R).rearrange("p (t r) -> p t r", t=NT)
        i8 = take(NT * 8, dt=U32).rearrange("p (t r) -> p t r", t=NT)
        i8f = take(NT * 8).rearrange("p (t r) -> p t r", t=NT)
        tmp = take(NT * 2).rearrange("p (t r) -> p t r", t=NT)
        oh2 = [take(NT * R).rearrange("p (t r) -> p t r", t=NT) for _ in range(2)]
        both = take(NT * R).rearrange("p (t r) -> p t r", t=NT)
        seen = take((NT + 1) * R).rearrange("p (t r) -> p t r", t=NT + 1)
        place = take(NT * R).rearrange("p (t r) -> p t r", t=NT)
        cnt = take(R)
        nt_ = take(R)
        ts_ = take(R)
        cmp_ = arena[:, base0:base0 + MT * R]
        ej = take(MT)
        eji = take(MT + 15, dt=I32)
        posf = take(2 * NT).rearrange("p (k t) -> p k t", k=2)
        upper = take(P)
        ones = take(P)
        NW = 3
        W1 = [take(2 * HID).rearrange("p (k h) -> p k h", k=2) for _ in range(NW)]
        W2 = [take(2 * HID).rearrange("p (k h) -> p k h", k=2) for _ in range(NW)]
        W3 = [take(4 * D).rearrange("p (k d) -> p k d", k=4) for _ in range(NW)]
        XGt = [take(D) for _ in range(NW)]
        xTt = [take(2 * P).rearrange("p (k c) -> p k c", k=2) for _ in range(2)]
        sil = [take(512) for _ in range(2)]
        hid = [take(512) for _ in range(2)]
        yst = [take(D) for _ in range(2)]
        assert top[0] <= LATER, (top[0], LATER)

        o1 = DVE.put(vec.memset, ones, 1.0, after=quiet)
        u0 = PL.put(pool.memset, upper, 1.0, after=quiet)
        u0 = PL.put(pool.affine_select, out=upper, in_=upper, compare_op=ALU.is_gt, fill=0.0, base=0,
                    pattern=[[1, P]], channel_multiplier=-1, after=[u0])
        se = [DVE.put(vec.memset, seen[:, 0, :], 0.0, after=quiet)]
        s_sc = stream("d_sc")
        logit_ok = {}
        HALF = 15
        ranked = [None]

        def gate_logits(i, ready):
            b = int(i >= HALF)
            n = i - b * HALF
            for k in range(2):
                logit_ok[b] = PE.put(ten.matmul, B[b][:, n * R:(n + 1) * R], XT[:, k, i * P:(i + 1) * P],
                                           gw[:, k, :], start=(k == 0), stop=(k == 1), after=[gw_in, ready] + fr(b),
                                           sig=(k == 1))

        def softmax(x, w, tmp, after):
            n = x.shape[1]
            v = DVE.put(vec.tensor_reduce, tmp[:, :, 0], x, AX, ALU.max, after=after)
            v = DVE.put(vec.tensor_tensor, x, x, tmp[:, :, 0:1].to_broadcast([P, n, w]), ALU.subtract, after=[v])
            v = AC.put(act.activation, x, x, ACT.Exp, after=[v])
            v = DVE.put(vec.tensor_reduce, tmp[:, :, 0], x, AX, ALU.add, after=[v])
            v = DVE.put(vec.reciprocal, tmp[:, :, 1], tmp[:, :, 0], after=[v])
            return DVE.put(vec.tensor_tensor, x, x, tmp[:, :, 1:2].to_broadcast([P, n, w]), ALU.mult, after=[v])

        def top2(x, m8, i8, i8f, after):
            v = None
            for i in range(x.shape[1]):
                v = DVE.put(vec.max, m8[:, i, :], x[:, i, :], after=after)
            for i in range(x.shape[1]):
                v = DVE.put(vec.max_index, i8[:, i, :], m8[:, i, :], x[:, i, :], after=[v])
            return DVE.put(vec.tensor_copy, i8f, i8, after=[v])

        def spread(w, wide, dst, tmp, after):
            io = iorow[:, 0:wide].rearrange("p (o r) -> p o r", o=1).to_broadcast([P, NT, wide])
            u = []
            for j, o in enumerate((dst, tmp)):
                v = DVE.put(vec.tensor_tensor, o, io, i8f[:, :, j:j + 1].to_broadcast([P, NT, wide]), ALU.is_equal, after=after)
                u.append(DVE.put(vec.tensor_tensor, o, o, w[:, :, j:j + 1].to_broadcast([P, NT, wide]), ALU.mult, after=[v]))
            return DVE.put(vec.tensor_tensor, dst, dst, tmp, ALU.add, after=u)

        def rows_of(v, n):
            return v.rearrange("p (o r) -> p o r", o=1).to_broadcast([P, n, R])

        def route(b, t0, t1):
            n = t1 - t0
            x = lg[:, t0:t1, :]
            v = free[b] = DVE.put(vec.tensor_tensor, x, B[b][:, 0:n * R].rearrange("p (t r) -> p t r", t=n),
                                  rows_of(gbb, n), ALU.add, after=[logit_ok[b], gw_in])
            v = softmax(x, R, tmp[:, t0:t1, :], [v])
            v = top2(x, m8[:, t0:t1, :], i8[:, t0:t1, :], i8f[:, t0:t1, :], [v])
            io = rows_of(iorow[:, 0:R], n)
            u = [DVE.put(vec.tensor_tensor, oh2[k][:, t0:t1, :], io, i8f[:, t0:t1, k:k + 1].to_broadcast([P, n, R]),
                         ALU.is_equal, after=[v]) for k in range(2)]
            v = DVE.put(vec.tensor_tensor, both[:, t0:t1, :], oh2[0][:, t0:t1, :], oh2[1][:, t0:t1, :], ALU.add, after=u)
            for i in range(t0, t1):
                se[0] = DVE.put(vec.tensor_tensor, seen[:, i + 1, :], seen[:, i, :], both[:, i, :], ALU.add, after=[v, se[0]])
            c = 2 + b
            PE.put(ten.matmul, B[c][:, 0:n * R], upper, both[:, t0:t1, :].rearrange("p t r -> p (t r)"), start=True, stop=False,
                   after=[v, u0] + fr(c), sig=False)
            mp = PE.put(ten.matmul, B[c][:, 0:n * R], ones, seen[:, t0:t1, :].rearrange("p t r -> p (t r)"), start=False,
                        stop=True, after=[se[0], o1])
            ranked[0] = free[c] = DVE.put(vec.tensor_copy, place[:, t0:t1, :],
                                          B[c][:, 0:n * R].rearrange("p (t r) -> p t r", t=n), after=[mp])

        xt = layernorm(lambda t0: [x1], keep=XN, then=gate_logits)[NT - 1]
        route(0, 0, HALF)
        route(1, HALF, NT)
        mt = PE.put(ten.matmul, B[4][:, 0:R], ones, seen[:, NT, :], start=True, stop=True, after=[se[0], o1] + fr(4))
        vc = free[4] = DVE.put(vec.tensor_copy, cnt, B[4][:, 0:R], after=[mt])
        cm3 = cmp_[:, 0:NT * R].rearrange("p (r t) -> p r t", r=R)
        v = DVE.put(vec.tensor_scalar, cm3, iorow[:, 0:NT].rearrange("p (o t) -> p o t", o=1).to_broadcast([P, R, NT]),
                    float(P), None, ALU.mult, after=quiet)
        v = DVE.put(vec.tensor_tensor, cm3, cnt.rearrange("p (r o) -> p r o", o=1).to_broadcast([P, R, NT]), cm3, ALU.is_gt,
                    after=[vc, v])
        v = DVE.put(vec.tensor_reduce, nt_, cm3, AX, ALU.add, after=[v])
        v = DVE.put(vec.tensor_tensor_scan, ts_, ones[:, 0:R], nt_, 0.0, ALU.mult, ALU.add, after=[v, o1])
        v = DVE.put(vec.tensor_tensor, ts_, ts_, nt_, ALU.subtract, after=[v])
        vts = v
        v = DVE.put(vec.scalar_tensor_tensor, place, rows_of(ts_, NT), float(P), place, ALU.mult, ALU.add, after=[v, ranked[0]])
        u = []
        for k in range(2):
            w = DVE.put(vec.tensor_tensor, oh2[k], oh2[k], place, ALU.mult, after=[v])
            u.append(DVE.put(vec.tensor_reduce, posf[:, k, :], oh2[k], AX, ALU.add, after=[w]))
        pos_ok = DVE.put(vec.tensor_copy, posi, posf, after=u)
        for i in range(NT):
            for k in range(2):
                sc = PL.dma(pool.indirect_dma_start, s_sc, XG, bass.IndirectOffsetOnAxis(ap=posi[:, k, i:i + 1], axis=0),
                            XN[:, i, :], None, after=[pos_ok, zg, xt])
        cj = cmp_.rearrange("p (j r) -> p j r", r=R)
        v = DVE.put(vec.tensor_tensor, cj[0:1], ts_[0:1].rearrange("p (o r) -> p o r", o=1).to_broadcast([1, MT, R]),
                    iorow[0:1, 0:MT].rearrange("p (j o) -> p j o", o=1).to_broadcast([1, MT, R]), ALU.is_le, after=[vts])
        v = DVE.put(vec.tensor_reduce, ej[0:1, 0:MT], cj[0:1], AX, ALU.add, after=[v])
        v = DVE.put(vec.tensor_scalar, ej[0:1, 0:MT], ej[0:1, 0:MT], -1.0, None, ALU.add, after=[v])
        z = DVE.put(vec.memset, eji[0:1, :], 0, after=quiet)
        ej_ok = DVE.put(vec.tensor_copy, eji[0:1, 0:MT], ej[0:1, 0:MT], after=[v, z])
        v = DVE.put(vec.tensor_tensor, tmp[:, :, 0], m8[:, :, 0], m8[:, :, 1], ALU.add)
        v = DVE.put(vec.reciprocal, tmp[:, :, 1], tmp[:, :, 0], after=[v])
        gate = DVE.put(vec.tensor_tensor, m8[:, :, 0:2], m8[:, :, 0:2], tmp[:, :, 1:2].to_broadcast([P, NT, 2]), ALU.mult,
                       after=[v])

        s_fw = stream("d_fw")
        s_gp = [stream(f"d_gp{i}") for i in range(4)]
        gp_in = {}
        for layer in range(2):
            W, asrc, adst, bias = (a[f"L1_gnn_{n}{layer + 1}"] for n in ("W", "a_src", "a_dst", "b"))
            SP.dma(sync.dma_start, s_gp[layer], wx2[layer][:, :, 0:D], W.rearrange("(k p) c -> p k c", p=P), after=quiet)
            gp_in[layer] = SP.dma(sync.dma_start, s_gp[layer], bb2[layer],
                                  bias.rearrange("(o c) -> o c", o=1).to_broadcast([P, D]))

        def score_weights(layer):
            wx, avb = wx2[layer], avb2[layer]
            for n, v in enumerate((a[f"L1_gnn_a_src{layer + 1}"], a[f"L1_gnn_a_dst{layer + 1}"])):
                v_in = SP.dma(sync.dma_start, s_gp[2 + layer], avb[:, n, :],
                              v.rearrange("h c -> (h c)").rearrange("(o c) -> o c", o=1).to_broadcast([P, D]),
                              after=quiet)
            v = None
            for k in range(2):
                for n in range(2):
                    v = DVE.put(vec.tensor_tensor, wtmp, wx[:, k, 0:D], avb[:, n, :], ALU.mult,
                                after=[gp_in[layer], v_in, DVE.last()] + ([v] if v else quiet))
                    v = DVE.put(vec.tensor_reduce, wx[:, k, D + 8 * n:D + 8 * n + 8],
                                wtmp.rearrange("p (h c) -> p h c", h=8), AX, ALU.add, after=[v])
            return v

        wx_ok = [score_weights(0), score_weights(1)]
        z1 = DVE.put(vec.memset, tad[:, NT * 8:], 0.0, after=quiet)

        def load(view, src, **kw):
            return SP.dma(sync.dma_start, s_fw, view, src, after=quiet, **kw)

        z = DVE.put(vec.memset, B5[0:8, :], 0.0, after=quiet)
        load(sW1, a["L1_ffn_sW1"].rearrange("(k p) c -> p k c", p=P))
        load(sW2, a["L1_ffn_sW2"].rearrange("(k p) c -> p k c", p=P))
        load(sW3, a["L1_ffn_sW3"])
        for k in range(2):
            load(eW1[:, k], a["L1_ffn_eW1"][:, k * P:(k + 1) * P, :].rearrange("e p c -> p e c"))
        load(eW2, a["L1_ffn_eW2"].rearrange("e p c -> p e c"))
        load(eW3[0:64], a["L1_ffn_eW3"].rearrange("e p c -> p e c"))
        load(gW, a["L1_ffn_gW"].rearrange("(k p) c -> p k c", p=P))
        load(gB, a["L1_ffn_gb"].rearrange("(o c) -> o c", o=1).to_broadcast([P, 4]))
        load(sb1, a["L1_ffn_sb1"].rearrange("(k p) -> p k", p=P), allow_slow_non_contiguous=True)
        load(sb2, a["L1_ffn_sb2"].rearrange("(p o) -> p o", o=1), allow_slow_non_contiguous=True)
        load(eb1, a["L1_ffn_eb1"].rearrange("e p -> p e"), allow_slow_non_contiguous=True)
        load(eb2[0:64], a["L1_ffn_eb2"].rearrange("e p -> p e"), allow_slow_non_contiguous=True)
        SP.dma(sync.dma_start, s_fw, B5[0:4, :], a["L1_ffn_eb3"], after=[z])
        w_in = SP.dma(sync.dma_start, s_fw, B5[4:5, :], a["L1_ffn_sb3"].rearrange("(o c) -> o c", o=1))

        s_ew = [stream(f"d_ew{i}") for i in range(NW)]
        s_xg = [stream(f"d_xg{i}") for i in range(NW)]
        s_yg = [stream(f"d_yg{i}") for i in range(2)]
        rsp = [[sync.alloc_register(f"rs{k}_{i}") for i in range(16)] for k in range(2)]
        wv = [a[n].rearrange("e (k p) h -> p e k h", p=P) for n in ("L0_ffn_w1", "L0_ffn_w2", "L0_ffn_w3")]

        def weights(j, n, dst):
            def go():
                e = sync.snap(rsp[(j // 16) % 2][j % 16], min_val=0, max_val=R - 1)
                return sync.dma_start(dst.rearrange("p (o k) h -> p o k h", o=1), wv[n][:, bass.ds(e, 1), :, :])
            return go

        w_free = [None] * NW
        g_free = [None] * NW
        ew, xg = {}, {}

        def load_tile(j):
            b = j % NW
            if j % 16 == 0:
                SP.put(sync.load, rsp[(j // 16) % 2], eji[0:1, j:j + 16], sig=False, after=[ej_ok])
            for n, W in enumerate((W1, W2, W3)):
                ew[j] = SP.dma(weights(j, n, W[b]), s_ew[b], after=opt(w_free[b]) + [ej_ok] + quiet)

        def load_rows(j):
            b = j % NW
            xg[j] = SP.dma(sync.dma_start, s_xg[b], XGt[b], XG[j * P:(j + 1) * P, :], after=[sc] + opt(g_free[b]))

        for j in range(NW):
            load_tile(j)
        for j in range(NW):
            load_rows(j)
        xt_free, sil_free, hid_free, y_free = [None] * 2, [None] * 2, [None] * 2, [None] * 2
        xt_ok, hid_ok, w3_ok = {}, {}, {}

        def turn(j):
            b, c = j % NW, j % 2
            for k in range(2):
                t = PE.put(ten.transpose, B[6 + c][:, k * P:(k + 1) * P], XGt[b][:, k * P:(k + 1) * P], ident[:, :],
                           after=[xg[j]] + fr(6 + c))
            g_free[b] = t
            xt_ok[j] = free[6 + c] = AC.put(act.copy, xTt[c], B[6 + c][:, 0:2 * P].rearrange("p (k c) -> p k c", k=2),
                                            after=[t] + opt(xt_free[c]) + quiet)
            if j + NW < MT:
                load_rows(j + NW)

        def up(j):
            b, c = j % NW, j % 2
            w = AC.put(act.copy, w3h[c], W3[b], after=[ew[j], sc] + opt(hid_free[c]))
            w3_ok[j] = DVE.put(vec.tensor_tensor, w3l[c], W3[b], w3h[c].bitcast(F32), ALU.subtract, after=[w])
            for bank, W in ((c, W1), (2 + c, W2)):
                for h in range(4):
                    for k in range(2):
                        mm = PE.put(ten.matmul, B[bank][:, h * P:(h + 1) * P], W[b][:, k, h * P:(h + 1) * P], xTt[c][:, k, :],
                                    start=(k == 0), stop=(k == 1), after=[ew[j], xt_ok[j]] + fr(bank), sig=(h == 3 and k == 1))
                if bank == c:
                    sl = free[bank] = AC.put(act.activation, sil[c], B[bank][:, :], ACT.Silu, after=[mm] + opt(sil_free[c]) + quiet)
            xt_free[c] = mm
            v = free[2 + c] = sil_free[c] = DVE.put(vec.tensor_tensor, hid[c], sil[c], B[2 + c][:, :], ALU.mult,
                                                    after=[mm, sl] + opt(hid_free[c]))
            v = AC.put(act.copy, hidh[c], hid[c], after=[v])
            hid_ok[j] = DVE.put(vec.tensor_tensor, hidl[c], hid[c], hidh[c].bitcast(F32), ALU.subtract, after=[v])

        def down(j):
            b, c = j % NW, j % 2
            terms = [(x, w, h) for x, w in ((hidh, w3h), (hidh, w3l), (hidl, w3h)) for h in range(4)]
            for n, (x, w, h) in enumerate(terms):
                mm = PE.put(ten.matmul, B[4 + c][:, 0:D], x[c][:, h * P:(h + 1) * P], w[c][:, h, :],
                            start=(n == 0), stop=(n == 11), after=[hid_ok[j], w3_ok[j]] + fr(4 + c), sig=(n == 11))
            hid_free[c] = w_free[b] = mm
            y = free[4 + c] = DVE.put(vec.tensor_copy, yst[c], B[4 + c][:, 0:D], after=[mm] + opt(y_free[c]))
            y_free[c] = AC.dma(act.dma_start, s_yg[c], YG[j * P:(j + 1) * P, :], yst[c], after=[y])
            if j + NW < MT:
                load_tile(j + NW)

        turn(0)
        for j in range(MT):
            if j + 1 < MT:
                turn(j + 1)
            up(j)
            if j:
                down(j - 1)
        down(MT - 1)

        s_yb = [stream(f"d_yb{i}") for i in range(4)]
        yb_free = [None] * 4
        moe_done = everyone() + y_free

        def combine(t0):
            v = None
            for i in range(t0, t0 + GT):
                b = i % 4
                for k in range(2):
                    g = PL.dma(pool.indirect_dma_start, s_yb[b], YB[b][:, k, :], None, YG,
                               bass.IndirectOffsetOnAxis(ap=posi[:, k, i:i + 1], axis=0),
                               after=y_free + opt(yb_free[b]) + [pos_ok] + quiet)
                v = DVE.put(vec.scalar_tensor_tensor, X[:, i, :], YB[b][:, 0, :], m8[:, i, 0:1], X[:, i, :], ALU.mult,
                            ALU.add, after=[g, gate])
                v = yb_free[b] = DVE.put(vec.scalar_tensor_tensor, X[:, i, :], YB[b][:, 1, :], m8[:, i, 1:2], X[:, i, :],
                                         ALU.mult, ALU.add, after=[v])
            return [v]

        top[0] = base0
        rep = [idx1T[0:8 * CH, i * EW:(i + 1) * EW].bitcast(F32) for i in range(2)]
        AS, SC = xn[:, 0, 0:P], xn[0:8 * CH, 1, :]
        SM, EE, VV = (xn[:, 2, 0:P], xn[:, 3, 0:P], nrmT[:, 0:8 * CH])
        SM, EE, VV = (v.rearrange("p (s c) -> p s c", c=8) for v in (SM, EE, VV))
        EX = [nrmT[:, (1 + i) * P:(2 + i) * P].rearrange("p (s c) -> p s c", c=8) for i in range(2)]
        ACC = take(NS * MSG)
        acc3 = ACC.rearrange("p (n c) -> p n c", c=HW)
        NW_ = NS + CH
        M = take(NW_ * 8)
        ln_ = take(CH * 8)
        Mo = take(8)
        lo_ = take(8)
        fc = take(8)
        ft = take(NW_ * 8)
        TB = take(NW_ * 24, dt=BF16)
        TB3 = TB.rearrange("p (n c) -> p n c", c=48)
        tmid = take(CH * 8)
        Gall = take(NG4 * CC * ROW)
        G = [Gall[:, i * CC * ROW:(i + 1) * CC * ROW].rearrange("p (s c) -> p s c", c=ROW) for i in range(NG4)]
        xtf = XT[:, :, :].rearrange("p k n -> p (k n)")
        OH = [xtf[:, i * CC * P:(i + 1) * CC * P].rearrange("p (s c) -> p s c", c=P) for i in range(2)]
        OT = [xtf[:, (4 + i) * CC * P // 2:(5 + i) * CC * P // 2].bitcast(BF16) for i in range(2)]
        hst = G[3].rearrange("p s c -> p (s c)")[:, 0:4 * ROW].rearrange("p (b c) -> p b c", b=4)
        SB = take(CC * 13, dt=BF16).rearrange("p (s c) -> p s c", c=26)
        OHb = [take(CC * P // 2, dt=BF16).rearrange("p (s c) -> p s c", c=P) for _ in range(2)]
        vp = take(CH)
        assert top[0] <= LATER, (top[0], LATER)
        O = [Gall[:, i * 5 * D:(i + 1) * 5 * D].rearrange("p (t c) -> p t c", c=D) for i in range(3)]
        O2 = [Gall[:, (3 + i) * 5 * D:(4 + i) * 5 * D].rearrange("p (t c) -> p t c", c=D) for i in range(3)]
        s_rep = [stream(f"d_rep{i}") for i in range(2)]
        s_gat = [stream(f"d_gat{i}") for i in range(NG4)]
        s_ot = [stream(f"d_ot{i}") for i in range(2)]
        s_ht = [stream(f"d_ht{i}") for i in range(4)]
        mo_ = Offsets(DVE, vec, 8, (NS - 1) * 8)
        ao_ = Offsets(DVE, vec, MSG, (NS - 1) * MSG)
        to_ = Offsets(PE, ten, 48, (NS - 1) * 48)
        tb_ = Offsets(DVE, vec, 48, (NS - 1) * 48)

        def keep_m(s):
            return lambda: vec.tensor_copy(Mo, M[:, bass.ds(mo_.at(s), 8)])

        def old_m(s):
            return lambda: vec.tensor_tensor(lo_, Mo, tad[:, bass.ds(mo_.at(s), 8)], ALU.add)

        def window(s):
            return lambda: vec.tensor_tensor(ln_, M[:, bass.ds(mo_.at(s), 8 * CH)], tad[:, bass.ds(mo_.at(s), 8 * CH)], ALU.add)

        def table(s, c):
            return TB[:, bass.ds(tb_.at(s), 48 * CH)].rearrange("p (n c) -> p n c", c=48)[:, :, c:c + 8]

        def rescale(s):
            def go():
                o = ACC[:, bass.ds(ao_.at(s), MSG)].rearrange("p (h c) -> p h c", c=HW)
                return vec.tensor_tensor(o, o, fc.rearrange("p (h o) -> p h o", o=1).to_broadcast([P, 8, HW]), ALU.mult)
            return go

        def max_m(s, j):
            def go():
                o = M[:, bass.ds(mo_.at(s), 8)]
                return vec.tensor_tensor(o, o, VV[:, j, :], ALU.max)
            return go

        def add_acc(s, bank):
            def go():
                o = ACC[:, bass.ds(ao_.at(s), MSG)]
                return vec.tensor_tensor(o, o, bank[:, 0:MSG], ALU.add)
            return go

        def expand(c, j, b):
            def go():
                t = TB[:, bass.ds(to_.at(c * CH + j // 2), 48)]
                return ten.matmul(B[4 + j // 8][:, 48 * (j % 8):48 * (j % 8) + 48], OT[b][:, j * P:(j + 1) * P], t,
                                  start=True, stop=True)
            return go

        def leaky(dst, src, after):
            return DVE.put(vec.scalar_tensor_tensor, dst, src, 0.2, src, ALU.mult, ALU.max, after=after)

        hfree = [None] * 4

        def ones_column(after):
            return DVE.put(vec.memset, hst, 1.0, after=after)

        def project(layer, ready, quiet, ones_ok):

            def go(i, xt):
                b = i % 4
                for k in range(2):
                    mm = PE.put(ten.matmul, B[b][:, 0:272], XT[:, k, i * P:(i + 1) * P], wx2[layer][:, k, :],
                                start=(k == 0), stop=(k == 1), after=[xt, wx_ok[layer]] + fr(b), sig=(k == 1))
                w = opt(hfree[b]) + quiet
                AC.put(act.copy, hst[:, b, 0:MSG].rearrange("p (h c) -> p h c", c=HW)[:, :, 0:32],
                       B[b][:, 0:D].rearrange("p (h c) -> p h c", c=32), after=[mm, ones_ok] + w)
                cp = AC.put(act.copy, hst[:, b, MSG:ROW], B[b][:, D:D + 8])
                ready["ad"] = free[b] = AC.put(act.copy, tad[:, i * 8:(i + 1) * 8], B[b][:, D + 8:D + 16], after=[z1])
                hfree[b] = SP.dma(sync.dma_start, s_ht[b], HT[layer][i * P:(i + 1) * P, :], hst[:, b, :], after=[cp])

            return go

        def gat(layer, ad_ok, quiet, acc_ok):
            minit = DVE.put(vec.memset, M, -BIG, after=quiet)
            ht_ok = [s.done() for s in s_ht]
            ad3 = tad.rearrange("p (n h) -> p n h", h=8)

            tok = {}

            def thirds(name, place, src, rest, after, width=8):

                def put(fn, *args, after):
                    return DVE.put(lambda: fn(*(x() if callable(x) else x for x in args)), after=after, late=True)

                v = put(vec.tensor_copy, place(0), src, after=after)
                yield
                v = put(vec.tensor_tensor, rest, src, place(0), ALU.subtract, after=[v])
                yield
                v = put(vec.tensor_copy, place(1), rest, after=[v])
                yield
                v = put(vec.tensor_tensor, rest, rest, place(1), ALU.subtract, after=[v])
                yield
                tok[name] = put(vec.tensor_copy, place(2), rest, after=[v])
                yield

            def whole(k):
                return TB3[:, :, 16 * k:16 * k + 8]

            def heads_of(v):
                return v.rearrange("p (n h) -> p n h", h=8)

            for _ in thirds("sp", whole, heads_of(tad), heads_of(ft), [ad_ok]):
                pass
            sp_ad = tok["sp"]
            slots = [[None] * CC for _ in range(NG4)]
            ot_free, rep_free, oh_free = [None] * 2, [None] * 2, [None] * 2
            mx_ok = {}
            g_in, ot_in, rep_in, oh_ok, ob_ok, ot_ok, w_ok = {}, {}, {}, {}, {}, {}, {}
            last_max = [minit]
            last_add = [acc_ok]

            def gathers(c):
                b = c % NG4
                for j in range(min(CC, 2 * (SU - c * CH))):
                    s = c * CC + j
                    w = opt(slots[b][j // 4 * 4 + 3]) + ht_ok + quiet
                    g_in[c] = PL.dma(pool.indirect_dma_start, s_gat[b], G[b][:, j, :], None, HT[layer],
                                     bass.IndirectOffsetOnAxis(ap=srcT[:, s:s + 1], axis=0), after=w)

            def fetch(c):
                b = c % 2
                rep_in[c] = SP.dma(sync.dma_start, s_rep[b], rep[b],
                                   RD[c * CH:(c + 1) * CH, :].rearrange("s (o c) -> s o c", o=1).to_broadcast([CH, 8, EW]),
                                   after=opt(rep_free[b]) + quiet + [tab["steps"]])
                ot_in[c] = SP.dma(sync.dma_start, s_ot[b], OT[b],
                                  DLD[c * CH:(c + 1) * CH, :].rearrange("s c -> (s c)").rearrange("(o n) -> o n", o=1)
                                  .to_broadcast([P, CC * P]), after=opt(ot_free[b]) + ht_ok)

            def turn_scores(c):
                cp = AC.put(act.copy, AS.rearrange("p (a s h) -> p s a h", a=2, h=8),
                             G[c % NG4][:, :, MSG:ROW].rearrange("p (s a) h -> p s a h", a=2),
                            after=[g_in[c]] + opt(tok.get("t")) + quiet)
                for n in range(2):
                    tok["t"] = PE.put(ten.transpose, B[7][0:8 * CH, n * P:(n + 1) * P], AS[:, n * 8 * CH:(n + 1) * 8 * CH],
                                      ident[:, :], after=[cp] + fr(7))
                yield

            def masks(c):
                b = c % 2
                v = None
                for j in range(CC):
                    q = c * CC + j
                    v = AC.put(act.activation, OHb[b][:, j, :], iorow[:, :], ACT.Abs, scale=-1.0, bias=dlT[:, q:q + 1],
                               after=quiet + opt(oh_ok.get(c - 2)) + opt(mx_ok.get(c - 2)))
                ob_ok[c] = AC.put(act.activation, OHb[b], OHb[b], ACT.Relu, scale=-1.0, bias=onec[:, 0:1], after=[v])

            def across(c):
                b = c % 2
                ot_ok[c] = DVE.put(vec.tensor_scalar, OT[b], OT[b], iocol[:, 0:1], None, ALU.is_equal, after=[ot_in[c]])
                yield

            def widen(c):
                b = c % 2
                oh_ok[c] = AC.put(act.copy, OH[b], OHb[b], after=[ob_ok[c]] + opt(oh_free[b]) + ht_ok)

            def ends(c):
                b = c % 2
                sc = rep_free[b] = DVE.put(vec.tensor_tensor_scan, SC, rep[b], B[7][0:8 * CH, 0:EW], -BIG, ALU.add, ALU.max,
                                           after=[tok["t"], rep_in[c]])
                for n in range(2):
                    tb = PE.put(ten.transpose, B[7][:, EW + n * 8 * CH:EW + (n + 1) * 8 * CH], SC[:, n * P:(n + 1) * P],
                                ident[0:8 * CH, 0:8 * CH], after=[sc])
                yield
                la = laT[:, c * CC:(c + 1) * CC].rearrange("p (s o) -> p s o", o=1)
                DVE.put(vec.tensor_copy, SB[:, :, 8:9], la)
                yield
                v = free[7] = DVE.put(vec.tensor_tensor, SM.rearrange("p (s a) h -> p s a h", a=2),
                                      B[7][:, EW:EW + P].rearrange("p (a s h) -> p s a h", a=2, h=8),
                                      la.rearrange("p (s a) o -> p s a o", a=2).to_broadcast([P, CH, 2, 8]), ALU.mult, after=[tb])
                yield
                yield from thirds("sb", lambda k: SB[:, :, (0, 9, 17)[k]:(8, 17, 25)[k]], SM, SM, [v])
                v = tok["sb"]
                for j in range(CC):
                    n = 9 * (j // 2)
                    terms = [(9, 0), (8, 9), (8, 17)]
                    for i, (m, k) in enumerate(terms[::-1] if j % 2 else terms):
                        tok["m"] = PE.put(ten.matmul, B[6][:, n:n + m], OHb[b][:, j, :], SB[:, j, k:k + m],
                                          start=(j % 2 == 0 and i == 0), stop=(j % 2 == 1 and i == 2),
                                          after=[ob_ok[c], v] + fr(6), sig=(j == CC - 1 and i == 2))
                mx_ok[c] = tok["m"]

            def values(c):
                pm = B[6][:, 0:9 * CH].rearrange("p (s c) -> p s c", c=9)
                v = DVE.put(vec.tensor_scalar, vp, pm[:, :, 8], -1.0, BIG, ALU.add, ALU.mult, after=[tok["m"]])
                yield
                v = DVE.put(vec.tensor_tensor, VV, pm[:, :, 0:8],
                            vp.rearrange("p (s o) -> p s o", o=1).to_broadcast([P, CH, 8]), ALU.add, after=[v])
                yield
                free[6] = v
                mo_.load(c * CH)
                last_max[0] = DVE.put(keep_m(c * CH), after=[last_max[0]], late=True)
                yield
                for j in range(CH):
                    last_max[0] = DVE.put(max_m(c * CH + j, j), after=[last_max[0], v], late=True)
                    yield

            def tables(c):
                b = c % 2
                to_.load(c * CH)
                tb_.load(c * CH)
                v = DVE.put(window(c * CH), after=[last_max[0], sp_ad], late=True)
                yield
                v = leaky(ln_, ln_, [v])
                yield
                f = None
                if c:
                    f = DVE.put(old_m(c * CH), after=[sp_ad], late=True)
                    yield
                    f = leaky(lo_, lo_, [f])
                    yield
                    f = DVE.put(vec.tensor_tensor, fc, lo_, ln_[:, 0:8], ALU.subtract, after=[f, v])
                    tok["f"] = AC.put(act.activation, fc, fc, ACT.Exp, after=[f])
                yield from thirds("sp", lambda k: lambda: table(c * CH, 8 + 16 * k), heads_of(ln_), heads_of(tmid),
                                  [v] + opt(ot_free[1 - b]))
                sp = tok["sp"]
                for j in range(CC):
                    n = 4 + j // 8
                    tok["e"] = PE.put(expand(c, j, b), after=[sp, ot_ok[c]] + fr(n), sig=(j == CC - 1))
                ot_free[b] = tok["e"]

            def weights_of(c):
                pe = PS[:, 4:6, 0:384].rearrange("p b (s c) -> p b s c", c=48)
                e4 = EE.rearrange("p (b s) c -> p b s c", b=2)
                g4 = G[c % NG4][:, :, MSG:ROW].rearrange("p (b s) c -> p b s c", b=2)
                v = DVE.put(vec.tensor_tensor, e4, pe[:, :, :, 0:8], g4, ALU.add, after=[tok["e"]])
                yield
                for k in (16, 32):
                    v = DVE.put(vec.tensor_tensor, e4, e4, pe[:, :, :, k:k + 8], ALU.add, after=[v])
                    yield
                v = leaky(EE, EE, [v])
                yield
                for k in (8, 24, 40):
                    v = DVE.put(vec.tensor_tensor, e4, e4, pe[:, :, :, k:k + 8], ALU.subtract, after=[v])
                    yield
                free[4] = free[5] = v
                v = DVE.put(vec.tensor_scalar, EE, EE, 0.0, None, ALU.min, after=[v])
                tok["x"] = AC.put(act.activation, EX[c % 2], EE, ACT.Exp, after=[v])
                yield

            def weigh(c):
                g = G[c % NG4]
                w_ok[c] = []
                for q in range(0, CC, 2):
                    gm = g[:, q:q + 2, 0:MSG].rearrange("p s (h c) -> p s h c", c=HW)
                    ex = EX[c % 2][:, q:q + 2, :].rearrange("p s (h o) -> p s h o", o=1).to_broadcast([P, 2, 8, HW])
                    w_ok[c].append(DVE.put(vec.tensor_tensor, gm, gm, ex, ALU.mult, after=[tok["x"]]))
                    yield

            def open_sums(c):
                ao_.load(c * CH)
                if c:
                    last_add[0] = DVE.put(rescale(c * CH), after=[tok["f"], last_add[0]], late=True)

            mms = {}

            def products(c, j0, j1):
                b = c % 2
                for j in range(j0, min(j1, SU - c * CH)):
                    n = j % 4
                    for h in range(2):
                        q = 2 * j + h
                        mms[j] = PE.put(ten.matmul, B[n][:, 0:MSG], OH[b][:, q, :], G[c % NG4][:, q, 0:MSG], start=(h == 0),
                                        stop=(h == 1), after=[w_ok[c][j], oh_ok[c]] + fr(n), sig=(h == 1))
                    slots[c % NG4][2 * j + 1] = oh_free[b] = mms[j]

            def adds(c, j0, j1):
                for j in range(j0, min(j1, SU - c * CH)):
                    n = j % 4
                    last_add[0] = free[n] = DVE.put(add_acc(c * CH + j, B[n]), after=[mms[j], last_add[0]], late=True)
                    yield

            def first_sums(c):
                yield from adds(c, 0, 4)
                products(c, 4, 8)

            def weave(*chains):
                chains = list(chains)
                while chains:
                    for g in list(chains):
                        if next(g, chains) is chains:
                            chains.remove(g)

            def none():
                return iter(())

            for c in range(NG4):
                gathers(c)
            fetch(0)
            fetch(1)
            masks(0)
            for i in range(-2, NCH):
                c, n, q = i, i + 1, i + 2
                c_on, n_on, q_on = (0 <= k < NCH for k in (c, n, q))
                if q_on:
                    weave(turn_scores(q))
                weave(tables(n) if n_on else none(), first_sums(c) if c_on else none())
                if n_on:
                    widen(n)
                scan = ends(q) if q_on else none()
                weave(islice(scan, 2), adds(c, 4, 8) if c_on else none(), across(q) if q_on else none())
                weave(weights_of(n) if n_on else none(), scan)
                if q + 1 < NCH:
                    masks(q + 1)
                weave(weigh(n) if n_on else none(), values(q) if q_on else none())
                if n_on:
                    open_sums(n)
                    products(n, 0, 4)
                if n_on and n + 2 < NCH:
                    fetch(n + 2)
                if c_on and c + NG4 < NCH:
                    gathers(c + NG4)
            return last_add[0]

        def heads(t0, dst, after):
            num = acc3[:, t0 * 8:(t0 + GT) * 8, 0:32]
            return DVE.put(vec.tensor_tensor, dst.rearrange("p t (h c) -> p (t h) c", c=32), num,
                           ft[:, t0 * 8:(t0 + GT) * 8].rearrange("p (n o) -> p n o", o=1).to_broadcast([P, 8 * GT, 32]), ALU.mult,
                           after=after)

        def denominators(after):
            v = DVE.put(vec.tensor_scalar, ft[:, 0:NS * 8], acc3[:, :, 32], 1e-16, None, ALU.add, after=after)
            return DVE.put(vec.reciprocal, ft[:, 0:NS * 8], ft[:, 0:NS * 8], after=[v])

        ready = {}
        one = ones_column(moe_done)
        low = 4 * 2 * D + NT * 10
        DVE.put(vec.memset, ACC[:, low:], 0.0, after=moe_done)
        xt = layernorm(combine, then=project(0, ready, moe_done, one))
        quiet = everyone() + list(xt.values())
        ad = gat(0, ready["ad"], quiet, DVE.put(vec.memset, ACC[:, 0:low], 0.0, after=quiet))
        den = denominators([ad])
        quiet = everyone()
        one = ones_column(quiet)
        go = project(1, ready, quiet, one)
        t_free, v_of, e_of = [None] * 3, {}, {}
        acc_ok = PL.put(pool.memset, ACC[:, NT * MSG:], 0.0, after=[den])
        for t0 in range(0, NT + GT, GT):
            b = t0 // GT % 3
            if t0 < NT:
                num = heads(t0, O[b], quiet + [den] + opt(t_free[b]))
                v_of[t0] = DVE.put(vec.tensor_tensor, O[b], O[b],
                                   bb2[0].rearrange("p (o c) -> p o c", o=1).to_broadcast([P, GT, D]), ALU.add,
                                   after=[num, gp_in[0]])
                acc_ok = PL.put(pool.memset, ACC[:, t0 * MSG:(t0 + GT) * MSG], 0.0, after=[num])
                xb = PL.put(pool.tensor_tensor, X[:, t0:t0 + GT, :], X[:, t0:t0 + GT, :],
                            bb2[1].rearrange("p (o c) -> p o c", o=1).to_broadcast([P, GT, D]), ALU.add,
                            after=[gp_in[1], den])
                e = AC.put(act.activation, O2[b], O[b], ACT.Exp, after=[v_of[t0]])
                e_of[t0] = e
            if t0:
                t1, b = t0 - GT, (t0 // GT - 1) % 3
                v = DVE.put(vec.tensor_scalar, O2[b], O2[b], 1.0, -1.0, ALU.min, ALU.add, after=[e_of[t1]])
                v = DVE.put(vec.scalar_tensor_tensor, O[b], O[b], 0.0, O2[b], ALU.max, ALU.add, after=[v, v_of[t1]])
                for i in range(t1, t0):
                    t_free[b], xt[i] = transpose_into_xt(i, O[b][:, i - t1, :], v, quiet)
                    if i > 1:
                        go(i - 2, xt[i - 2])
        for i in (NT - 2, NT - 1):
            go(i, xt[i])
        quiet = everyone() + list(xt.values())
        ad = gat(1, ready["ad"], quiet, acc_ok)
        den = denominators([ad])
        quiet = everyone()

        o_free, sums = [None] * 3, {}

        def attend(t0):
            for t in ((0, GT) if t0 == 0 else (t0 + GT,)):
                if t < NT:
                    b = t // GT % 3
                    v = heads(t, O[b], quiet + [den] + opt(o_free[b]))
                    sums[t] = o_free[b] = PL.put(pool.tensor_tensor, X[:, t:t + GT, :], X[:, t:t + GT, :], O[b], ALU.add,
                                                 after=[v])
            return [sums[t0]]

        def gates(i, ready):
            for k in range(2):
                PE.put(ten.matmul, B[0][:, i * 4:(i + 1) * 4], XT[:, k, i * P:(i + 1) * P], gW[:, k, :],
                       start=(k == 0), stop=(k == 1), after=[w_in, ready] + fr(0), sig=(k == 1))

        xt = layernorm(attend, then=gates)[NT - 1]
        mm = PE.last()
        quiet = everyone() + [xt]
        top[0] = base0

        lg4 = take(NT * 8).rearrange("p (t r) -> p t r", t=NT)
        m8 = take(NT * 8).rearrange("p (t r) -> p t r", t=NT)
        i8 = take(NT * 8, dt=U32).rearrange("p (t r) -> p t r", t=NT)
        i8f = take(NT * 8).rearrange("p (t r) -> p t r", t=NT)
        t2_ = take(NT * 2).rearrange("p (t r) -> p t r", t=NT)
        wts = take(NT * 8).rearrange("p (t r) -> p t r", t=NT)
        wt2 = take(NT * 8).rearrange("p (t r) -> p t r", t=NT)
        wT = take(NP)
        H1 = take(2 * 2 * 512).rearrange("p (b k n) -> p b k n", b=2, k=2)
        H2 = take(2 * 512).rearrange("p (b n) -> p b n", b=2)
        E1 = take(4 * 512).rearrange("p (b n) -> p b n", b=4)
        E2 = take(8 * 512).rearrange("p (b n) -> p b n", b=8)
        z = DVE.put(vec.memset, lg4, -1.0, after=quiet)
        v = free[0] = DVE.put(vec.tensor_tensor, lg4[:, :, 0:4], B[0][:, 0:NT * 4].rearrange("p (t r) -> p t r", t=NT),
                              gB.rearrange("p (o r) -> p o r", o=1).to_broadcast([P, NT, 4]), ALU.add, after=[mm, z, w_in])
        v = softmax(lg4[:, :, 0:4], 4, t2_, [v])
        v = top2(lg4, m8, i8, i8f, [v])
        v = DVE.put(vec.tensor_tensor, t2_[:, :, 0], m8[:, :, 1], m8[:, :, 0], ALU.subtract, after=[v])
        v = AC.put(act.activation, m8[:, :, 1], t2_[:, :, 0], ACT.Exp, after=[v])
        v = DVE.put(vec.tensor_scalar, t2_[:, :, 0], m8[:, :, 1], 1.0, None, ALU.add, after=[v])
        v = DVE.put(vec.reciprocal, m8[:, :, 0], t2_[:, :, 0], after=[v])
        v = DVE.put(vec.tensor_tensor, m8[:, :, 1], m8[:, :, 1], m8[:, :, 0], ALU.mult, after=[v])
        v = spread(m8, 8, wts, wt2, [v])
        gate = DVE.put(vec.memset, wts[:, :, 4:5], 1.0, after=[v])
        wt_ok = None

        def gate_rows():
            nonlocal wt_ok
            for t0 in range(0, NT, 4):
                b = 4 + t0 // 4 % 4
                n = min(4, NT - t0)
                for i in range(n):
                    tp = PE.put(ten.transpose, B[b][0:8, i * P:(i + 1) * P], wts[:, t0 + i, :], ident[:, :],
                                after=[gate] + fr(b))
                wt_ok = free[b] = AC.put(act.copy, wT[0:8, t0 * P:(t0 + n) * P], B[b][0:8, 0:n * P], after=[tp] + quiet)

        h1_free, h2_free, e1_free, e2_free = [None] * 2, [None] * 2, [None] * 4, [None] * 8
        ne_ = 0
        nb = 0
        final = {}

        def hidden(tc):
            n0 = tc * 512
            nn = min(512, NP - n0)
            hb = tc % 2

            def layer(dst, parts, lhs, rhs, bias, after, width=P):
                nonlocal nb
                b = nb % 4
                nb += 1
                for k in range(parts):
                    mm = PE.put(ten.matmul, B[b][0:width, 0:nn], lhs(k), rhs(k), start=(k == 0), stop=(k == parts - 1),
                                after=[w_in] + after + quiet + fr(b), sig=(k == parts - 1))
                free[b] = AC.put(act.activation, dst, B[b][0:width, 0:nn], ACT.Relu, bias=bias, after=[mm])
                return mm, free[b]

            def xr(k):
                return XT[:, k, n0:n0 + nn]

            def first(m):
                return layer(H1[:, hb, m, 0:nn], 2, lambda k: sW1[:, k, m * P:(m + 1) * P], xr, sb1[:, m:m + 1],
                             opt(h1_free[hb]))[1]

            def expert(e):
                return layer(E1[:, e, 0:nn], 2, lambda k: eW1[:, k, e, :], xr, eb1[:, e:e + 1], opt(e1_free[e]))[1]

            def second(e, t):
                e1_free[e], t = layer(E2[0:64, hb * 4 + e, 0:nn], 1, lambda k: eW2[:, e, :], lambda k: E1[:, e, 0:nn],
                                      eb2[0:64, e:e + 1], [t] + opt(e2_free[hb * 4 + e]), width=64)
                return t

            r = [first(0), first(1)]
            t = [expert(0)]
            h1_free[hb], h2 = layer(H2[:, hb, 0:nn], 2, lambda k: sW2[:, k, :], lambda k: H1[:, hb, k, 0:nn], sb2[:, 0:1],
                                    r + opt(h2_free[hb]))
            e2 = []
            for e in range(4):
                if e < 3:
                    t.append(expert(e + 1))
                e2.append(second(e, t[e]))
            return h2, e2

        def outputs(tc, h2, e2):
            nonlocal ne_
            n0 = tc * 512
            nn = min(512, NP - n0)
            hb = tc % 2
            for q in range(nn // P):
                i = tc * 4 + q
                b = 4 + ne_ % 4
                ne_ += 1
                PE.put(ten.matmul, B[b][:, 0:D], H2[:, hb, q * P:(q + 1) * P], sW3, start=True, stop=False,
                       after=[h2, wt_ok] + fr(b), sig=False)
                mm = PE.put(ten.matmul, B[b][:, 0:D], wT[0:8, i * P:(i + 1) * P], B5[0:8, :], start=False, stop=True)
                v = free[b] = DVE.put(vec.tensor_tensor, X[:, i, :], X[:, i, :], B[b][:, 0:D], ALU.add, after=[mm])
                h2_free[hb] = mm
                for e in range(4):
                    b = 4 + ne_ % 4
                    ne_ += 1
                    mm = PE.put(ten.matmul, B[b][:, 0:D], E2[0:64, hb * 4 + e, q * P:(q + 1) * P], eW3[0:64, e, :],
                                start=True, stop=True, after=[e2[e]] + fr(b))
                    e2_free[hb * 4 + e] = mm
                    v = free[b] = DVE.put(vec.scalar_tensor_tensor, X[:, i, :], B[b][:, 0:D], wts[:, i, e:e + 1],
                                          X[:, i, :], ALU.mult, ALU.add, after=[mm, v])
            k = nn // P
            if tc < 6:
                SP.dma(sync.dma_start, s_out, out[n0:n0 + nn, :].rearrange("(t p) d -> p t d", p=P),
                       X[:, tc * 4:tc * 4 + 4, :], after=[v])
            else:
                SP.dma(sync.dma_start, s_out, out[n0:N, :], X[0:N - n0, NT - 1, :], after=[v])

        got = hidden(0)
        for tc in range(7):
            nxt = hidden(tc + 1) if tc < 6 else None
            if tc == 0:
                gate_rows()
            outputs(tc, *got)
            got = nxt

        block = ctx.enter_context(nc.Block())

        @block.sync
        def _(eng):
            SP.play(eng)
            eng.wait_ge(s_out.sem, s_out.n)

        @block.gpsimd
        def _(eng):
            PL.play(eng)

        @block.scalar
        def _(eng):
            AC.play(eng)

        @block.tensor
        def _(eng):
            PE.play(eng)

        @block.vector
        def _(eng):
            DVE.play(eng)


_INS = ['x', 'src', 'dst', 'edge_type_16', 'edge_weight1', 'L0_gnn_weight', 'L0_ffn_gate_w', 'L0_ffn_gate_b',
        'L0_ffn_w1', 'L0_ffn_w2', 'L0_ffn_w3', 'L1_gnn_W1', 'L1_gnn_a_src1', 'L1_gnn_a_dst1', 'L1_gnn_b1',
        'L1_gnn_W2', 'L1_gnn_a_src2', 'L1_gnn_a_dst2', 'L1_gnn_b2', 'L1_ffn_sW1', 'L1_ffn_sb1', 'L1_ffn_sW2',
        'L1_ffn_sb2', 'L1_ffn_sW3', 'L1_ffn_sb3', 'L1_ffn_eW1', 'L1_ffn_eb1', 'L1_ffn_eW2', 'L1_ffn_eb2',
        'L1_ffn_eW3', 'L1_ffn_eb3', 'L1_ffn_gW', 'L1_ffn_gb']


def kernel(**inputs):
    import numpy as _np
    import concourse.bacc as _bacc
    from concourse.bass_utils import run_bass_kernel_spmd as _run

    nc = _bacc.Bacc("TRN2", target_bir_lowering=False, num_devices=1)
    arrays, aps = {}, {}
    for name in _INS:
        v = _np.ascontiguousarray(inputs[name])
        arrays[f"in_{name}_dram"] = v
        aps[name] = nc.dram_tensor(f"in_{name}_dram", v.shape, mybir.dt.from_np(v.dtype), kind="ExternalInput").ap()
    out = nc.dram_tensor("out_0_dram", (N, D), F32, kind="ExternalOutput").ap()
    build(nc, aps, out)
    r = _run(nc, [arrays], core_ids=[0])
    return r.results[0]["out_0_dram"]
```
